# Optimizing a Trainium2 kernel written in Bass

```python
import numpy as np
import jax
import jax.numpy as jnp

def _softmax(x, axis=-1):
    return jax.nn.softmax(x, axis=axis)

def _gelu(x):
    return jax.nn.gelu(x, approximate=True)

def _silu(x):
    return jax.nn.silu(x)

def _sigmoid(x):
    return jax.nn.sigmoid(x)

def _layernorm(x, axis=-1, eps=1e-05):
    m = jnp.mean(x, axis=axis, keepdims=True)
    v = jnp.var(x, axis=axis, keepdims=True)
    return (x - m) / jnp.sqrt(v + eps)

def _scatter_add(tgt, idx, src, axis=0):
    return tgt.at[idx].add(src)

def _segment_sum(src, seg, n):
    return jax.ops.segment_sum(src, seg, n)
kernel_name = 'mk_xattn_ffn_d2_seqx_r8_45582d'

def setup_inputs(seed: int=0):
    np.random.seed(seed)
    _w = jnp.asarray

    def _rec_inputs():
        import jax
        import jax.numpy as jnp
        _rk = jax.random.key(seed)
        x = -0.0005207 + 1.001 * jax.random.normal(jax.random.fold_in(_rk, 1), (8, 256, 128), jnp.float32)
        _lenS = 256 - jax.random.randint(jax.random.fold_in(_rk, 7), (8,), 0, max(1, 256 // 4) + 1, jnp.int32)
        _lenS2 = 512 - jax.random.randint(jax.random.fold_in(_rk, 8), (8,), 0, max(1, 512 // 4) + 1, jnp.int32)
        _ctx_1024P = jax.random.normal(jax.random.fold_in(_rk, 11), (8, 16, 128), jnp.float32)
        _ctx_1024c = jax.random.dirichlet(jax.random.fold_in(_rk, 511), 0.3 * jnp.ones((16,), jnp.float32), (8, 512))
        _ctx_1024t = jnp.einsum('bsk,bkd->bsd', _ctx_1024c, _ctx_1024P)
        _ctx_1024t = _ctx_1024t * jax.lax.rsqrt(jnp.mean(jnp.square(_ctx_1024t)) + 1e-12) * 0.953939
        ctx_1024 = -0.000514642 + 1.00011 * (_ctx_1024t + 0.3 * jax.random.normal(jax.random.fold_in(_rk, 611), (8, 512, 128), jnp.float32))
        _validS = jnp.arange(256)[None, :] < _lenS[:, None]
        _validS2 = jnp.arange(512)[None, :] < _lenS2[:, None]
        _causal = jnp.tril(jnp.ones((256, 256), dtype=bool))
        mask_BxS2_bk1 = jnp.broadcast_to(_validS2[:, :], (8, 512))
        return (x, ctx_1024, mask_BxS2_bk1)
    x, ctx_1024, mask_BxS2_bk1 = _rec_inputs()

    def _L0_xattn_setup():
        import jax, jax.numpy as jnp
        import numpy as np
        import math
        B, S, D, H = (1, 256, 128, 16)
        DK = D // H
        DH = 64
        LOG_T_MIN = math.log(0.1)
        LOG_T_MAX = math.log(10.0)

        def _linear(x, W, b):
            return x @ W.T + b
        key = jax.random.key(seed)
        ks = jax.random.split(key, 20)
        p = 0.02
        return {'query': jax.random.normal(ks[0], (B, S, D), jnp.float32), 'key': jax.random.normal(ks[1], (B, S, D), jnp.float32), 'value': jax.random.normal(ks[2], (B, S, D), jnp.float32), 'Wq': jax.random.normal(ks[3], (D, D), jnp.float32) * p, 'bq': jax.random.normal(ks[4], (D,), jnp.float32) * p, 'Wk': jax.random.normal(ks[5], (D, D), jnp.float32) * p, 'bk': jax.random.normal(ks[6], (D,), jnp.float32) * p, 'Wv': jax.random.normal(ks[7], (D, D), jnp.float32) * p, 'bv': jax.random.normal(ks[8], (D,), jnp.float32) * p, 'Wo': jax.random.normal(ks[9], (D, D), jnp.float32) * p, 'bo': jax.random.normal(ks[10], (D,), jnp.float32) * p, 'w1': jax.random.normal(ks[11], (DH, 3), jnp.float32) * 0.3, 'b1': jax.random.normal(ks[12], (DH,), jnp.float32) * 0.1, 'w2': jax.random.normal(ks[13], (DH, DH), jnp.float32) * 0.1, 'b2': jax.random.normal(ks[14], (DH,), jnp.float32) * 0.1, 'w3': jax.random.normal(ks[15], (1, DH), jnp.float32) * 0.1, 'b3': jnp.full((1,), (LOG_T_MIN + LOG_T_MAX) / 2, jnp.float32)}
    _L0_xattn_all = _L0_xattn_setup()
    _L0_xattn_in = {k: v for k, v in _L0_xattn_all.items() if k in ('Wq', 'bq', 'Wk', 'bk', 'Wv', 'bv', 'Wo', 'bo', 'w1', 'b1', 'w2', 'b2', 'w3', 'b3')}
    del _L0_xattn_all

    def _L0_ffn_setup():
        import jax, jax.numpy as jnp
        import numpy as np
        B, T, D, F, E = (2, 128, 128, 512, 8)
        EPS = 1e-06
        key = jax.random.key(seed)
        k = jax.random.split(key, 5)
        scale = 0.02
        return {'x': jax.random.normal(k[0], (B, T, D), dtype=jnp.float32), 'rms_w': jnp.ones((D,), dtype=jnp.float32), 'gate_w': jax.random.normal(k[1], (E, D), dtype=jnp.float32) * scale, 'W1': jax.random.normal(k[2], (E, D, F), dtype=jnp.float32) * scale, 'b1': jnp.zeros((E, F), dtype=jnp.float32), 'W2': jax.random.normal(k[3], (E, F, D), dtype=jnp.float32) * scale, 'b2': jnp.zeros((E, D), dtype=jnp.float32)}
    _L0_ffn_all = _L0_ffn_setup()
    _L0_ffn_in = {k: v for k, v in _L0_ffn_all.items() if k in ('rms_w', 'gate_w', 'W1', 'b1', 'W2', 'b2')}
    del _L0_ffn_all

    def _L1_xattn_setup():
        import jax, jax.numpy as jnp
        import numpy as np
        DIM = 128
        DIM_HEAD = 64
        HEADS = 8
        INNER = DIM_HEAD * HEADS
        EPS = 1e-05

        def layernorm(x, g, b):
            mu = jnp.mean(x, axis=-1, keepdims=True)
            var = jnp.var(x, axis=-1, keepdims=True)
            return (x - mu) * jax.lax.rsqrt(var + EPS) * g + b
        key = jax.random.key(seed)
        ks = jax.random.split(key, 8)
        b, n, m = (8, 512, 64)
        x = jax.random.normal(ks[0], (b, n, DIM), dtype=jnp.float32)
        latents = jax.random.normal(ks[1], (b, m, DIM), dtype=jnp.float32)
        mask = jax.random.bernoulli(ks[2], 0.9, (b, n))
        s = DIM ** (-0.5)
        Wq = jax.random.normal(ks[3], (DIM, INNER), dtype=jnp.float32) * s
        Wkv = jax.random.normal(ks[4], (DIM, 2 * INNER), dtype=jnp.float32) * s
        Wo = jax.random.normal(ks[5], (INNER, DIM), dtype=jnp.float32) * INNER ** (-0.5)
        ln_x_g = jnp.ones((DIM,), jnp.float32)
        ln_x_b = jnp.zeros((DIM,), jnp.float32)
        ln_l_g = jnp.ones((DIM,), jnp.float32)
        ln_l_b = jnp.zeros((DIM,), jnp.float32)
        ln_o_g = jnp.ones((DIM,), jnp.float32)
        ln_o_b = jnp.zeros((DIM,), jnp.float32)
        return {'x': x, 'latents': latents, 'mask': mask, 'Wq': Wq, 'Wkv': Wkv, 'Wo': Wo, 'ln_x_g': ln_x_g, 'ln_x_b': ln_x_b, 'ln_l_g': ln_l_g, 'ln_l_b': ln_l_b, 'ln_o_g': ln_o_g, 'ln_o_b': ln_o_b}
    _L1_xattn_all = _L1_xattn_setup()
    _L1_xattn_in = {k: v for k, v in _L1_xattn_all.items() if k in ('Wq', 'Wkv', 'Wo', 'ln_x_g', 'ln_x_b', 'ln_l_g', 'ln_l_b', 'ln_o_g', 'ln_o_b')}
    del _L1_xattn_all

    def _L1_ffn_setup():
        import jax, jax.numpy as jnp
        import numpy as np
        NUM_EXPERTS = 8
        TOP_K = 2

        def _swiglu(x, w1, w2, w3):
            return jax.nn.silu(x @ w1) * (x @ w3) @ w2
        key = jax.random.key(seed)
        ks = jax.random.split(key, 9)
        B, S, D, H, E = (1, 128, 128, 128, NUM_EXPERTS)
        std = 0.02
        return {'x': jax.random.normal(ks[0], (B, S, D), jnp.float32), 'router_w': jax.random.normal(ks[1], (D, E), jnp.float32) * std, 'expert_bias': jnp.zeros((E,), jnp.float32), 'w1': jax.random.normal(ks[2], (E, D, H), jnp.float32) * std, 'w2': jax.random.normal(ks[3], (E, H, D), jnp.float32) * std, 'w3': jax.random.normal(ks[4], (E, D, H), jnp.float32) * std, 'sw1': jax.random.normal(ks[5], (D, H), jnp.float32) * std, 'sw2': jax.random.normal(ks[6], (H, D), jnp.float32) * std, 'sw3': jax.random.normal(ks[7], (D, H), jnp.float32) * std}
    _L1_ffn_all = _L1_ffn_setup()
    _L1_ffn_in = {k: v for k, v in _L1_ffn_all.items() if k in ('router_w', 'expert_bias', 'w1', 'w2', 'w3', 'sw1', 'sw2', 'sw3')}
    del _L1_ffn_all
    return {'x': x, 'ctx_1024': ctx_1024, 'mask_BxS2_bk1': mask_BxS2_bk1, 'L0_xattn_Wq': _L0_xattn_in['Wq'], 'L0_xattn_bq': _L0_xattn_in['bq'], 'L0_xattn_Wk': _L0_xattn_in['Wk'], 'L0_xattn_bk': _L0_xattn_in['bk'], 'L0_xattn_Wv': _L0_xattn_in['Wv'], 'L0_xattn_bv': _L0_xattn_in['bv'], 'L0_xattn_Wo': _L0_xattn_in['Wo'], 'L0_xattn_bo': _L0_xattn_in['bo'], 'L0_xattn_w1': _L0_xattn_in['w1'], 'L0_xattn_b1': _L0_xattn_in['b1'], 'L0_xattn_w2': _L0_xattn_in['w2'], 'L0_xattn_b2': _L0_xattn_in['b2'], 'L0_xattn_w3': _L0_xattn_in['w3'], 'L0_xattn_b3': _L0_xattn_in['b3'], 'L0_ffn_rms_w': _L0_ffn_in['rms_w'], 'L0_ffn_gate_w': _L0_ffn_in['gate_w'], 'L0_ffn_W1': _L0_ffn_in['W1'], 'L0_ffn_b1': _L0_ffn_in['b1'], 'L0_ffn_W2': _L0_ffn_in['W2'], 'L0_ffn_b2': _L0_ffn_in['b2'], 'L1_xattn_Wq': _L1_xattn_in['Wq'], 'L1_xattn_Wkv': _L1_xattn_in['Wkv'], 'L1_xattn_Wo': _L1_xattn_in['Wo'], 'L1_xattn_ln_x_g': _L1_xattn_in['ln_x_g'], 'L1_xattn_ln_x_b': _L1_xattn_in['ln_x_b'], 'L1_xattn_ln_l_g': _L1_xattn_in['ln_l_g'], 'L1_xattn_ln_l_b': _L1_xattn_in['ln_l_b'], 'L1_xattn_ln_o_g': _L1_xattn_in['ln_o_g'], 'L1_xattn_ln_o_b': _L1_xattn_in['ln_o_b'], 'L1_ffn_router_w': _L1_ffn_in['router_w'], 'L1_ffn_expert_bias': _L1_ffn_in['expert_bias'], 'L1_ffn_w1': _L1_ffn_in['w1'], 'L1_ffn_w2': _L1_ffn_in['w2'], 'L1_ffn_w3': _L1_ffn_in['w3'], 'L1_ffn_sw1': _L1_ffn_in['sw1'], 'L1_ffn_sw2': _L1_ffn_in['sw2'], 'L1_ffn_sw3': _L1_ffn_in['sw3']}

def reference(x, ctx_1024, mask_BxS2_bk1, L0_xattn_Wq, L0_xattn_bq, L0_xattn_Wk, L0_xattn_bk, L0_xattn_Wv, L0_xattn_bv, L0_xattn_Wo, L0_xattn_bo, L0_xattn_w1, L0_xattn_b1, L0_xattn_w2, L0_xattn_b2, L0_xattn_w3, L0_xattn_b3, L0_ffn_rms_w, L0_ffn_gate_w, L0_ffn_W1, L0_ffn_b1, L0_ffn_W2, L0_ffn_b2, L1_xattn_Wq, L1_xattn_Wkv, L1_xattn_Wo, L1_xattn_ln_x_g, L1_xattn_ln_x_b, L1_xattn_ln_l_g, L1_xattn_ln_l_b, L1_xattn_ln_o_g, L1_xattn_ln_o_b, L1_ffn_router_w, L1_ffn_expert_bias, L1_ffn_w1, L1_ffn_w2, L1_ffn_w3, L1_ffn_sw1, L1_ffn_sw2, L1_ffn_sw3):
    import jax
    import jax.numpy as jnp

    def _L0_xattn_ref(query, key, value, Wq, bq, Wk, bk, Wv, bv, Wo, bo, w1, b1, w2, b2, w3, b3):
        import jax, jax.numpy as jnp
        import numpy as np
        import math
        B, S, D, H = (1, 256, 128, 16)
        DK = D // H
        DH = 64
        LOG_T_MIN = math.log(0.1)
        LOG_T_MAX = math.log(10.0)

        def _linear(x, W, b):
            return x @ W.T + b
        b, sq, d = query.shape
        sk = key.shape[1]
        h, dk = (H, DK)
        Q = _linear(query, Wq, bq).reshape(b, sq, h, dk).transpose(0, 2, 1, 3)
        K = _linear(key, Wk, bk).reshape(b, sk, h, dk).transpose(0, 2, 1, 3)
        V = _linear(value, Wv, bv).reshape(b, sk, h, dk).transpose(0, 2, 1, 3)
        qk = jnp.einsum('bhqd,bhkd->bhqk', Q, K)
        scores = qk / math.sqrt(dk)
        mean_sim = scores.mean(axis=(-2, -1))
        max_sim = scores.max(axis=-1).mean(axis=-1)
        probs = jax.nn.softmax(scores, axis=-1)
        entropy_proxy = jnp.var(probs, axis=-1, ddof=1).mean(axis=-1)
        feats = jnp.stack([mean_sim, max_sim, entropy_proxy], axis=-1)
        hidden = jax.nn.gelu(_linear(feats, w1, b1), approximate=False)
        hidden = jax.nn.gelu(_linear(hidden, w2, b2), approximate=False)
        log_t = jnp.clip(_linear(hidden, w3, b3), LOG_T_MIN, LOG_T_MAX)
        t = jnp.exp(log_t)[..., None]
        attn_scores = qk / (2.0 * t)
        attn = jax.nn.softmax(attn_scores, axis=-1)
        attn = jnp.nan_to_num(attn, nan=0.0)
        out = jnp.einsum('bhqk,bhkd->bhqd', attn, V)
        out = out.transpose(0, 2, 1, 3).reshape(b, sq, d)
        return _linear(out, Wo, bo)

    def _L0_ffn_ref(x, rms_w, gate_w, W1, b1, W2, b2):
        import jax, jax.numpy as jnp
        import numpy as np
        B, T, D, F, E = (2, 128, 128, 512, 8)
        EPS = 1e-06
        ms = jnp.mean(x * x, axis=-1, keepdims=True)
        xn = x * jax.lax.rsqrt(ms + EPS) * rms_w
        logits = jnp.einsum('btd,ed->bte', xn, gate_w)
        scores = jax.nn.softmax(logits, axis=-1)
        top1_idx = jnp.argmax(scores, axis=-1)
        top1_score = jnp.max(scores, axis=-1)
        out = jnp.zeros_like(xn)
        for e in range(E):
            h = jax.nn.silu(jnp.einsum('btd,df->btf', xn, W1[e]) + b1[e])
            ye = jnp.einsum('btf,fd->btd', h, W2[e]) + b2[e]
            out = jnp.where((top1_idx == e)[..., None], ye, out)
        return out * top1_score[..., None]

    def _L1_xattn_ref(x, latents, mask, Wq, Wkv, Wo, ln_x_g, ln_x_b, ln_l_g, ln_l_b, ln_o_g, ln_o_b):
        import jax, jax.numpy as jnp
        import numpy as np
        DIM = 128
        DIM_HEAD = 64
        HEADS = 8
        INNER = DIM_HEAD * HEADS
        EPS = 1e-05

        def layernorm(x, g, b):
            mu = jnp.mean(x, axis=-1, keepdims=True)
            var = jnp.var(x, axis=-1, keepdims=True)
            return (x - mu) * jax.lax.rsqrt(var + EPS) * g + b
        scale = DIM_HEAD ** (-0.5)
        b, m = (latents.shape[0], latents.shape[1])
        xn = layernorm(x, ln_x_g, ln_x_b)
        ln = layernorm(latents, ln_l_g, ln_l_b)
        q = ln @ Wq
        kv_in = jnp.concatenate([xn, ln], axis=1)
        kv = kv_in @ Wkv
        k, v = jnp.split(kv, 2, axis=-1)
        q = q.reshape(b, m, HEADS, DIM_HEAD).transpose(0, 2, 1, 3)
        k = k.reshape(b, k.shape[1], HEADS, DIM_HEAD).transpose(0, 2, 1, 3)
        v = v.reshape(b, v.shape[1], HEADS, DIM_HEAD).transpose(0, 2, 1, 3)
        sim = jnp.einsum('bhid,bhjd->bhij', q * scale, k) * scale
        full_mask = jnp.concatenate([mask, jnp.ones((b, m), dtype=bool)], axis=1)
        max_neg = -jnp.finfo(sim.dtype).max
        sim = jnp.where(full_mask[:, None, None, :], sim, max_neg)
        attn = jax.nn.softmax(sim.astype(jnp.float32), axis=-1).astype(sim.dtype)
        out = jnp.einsum('bhij,bhjd->bhid', attn, v)
        out = out.transpose(0, 2, 1, 3).reshape(b, m, INNER)
        out = out @ Wo
        return layernorm(out, ln_o_g, ln_o_b)

    def _L1_ffn_ref(x, router_w, expert_bias, w1, w2, w3, sw1, sw2, sw3):
        import jax, jax.numpy as jnp
        import numpy as np
        NUM_EXPERTS = 8
        TOP_K = 2

        def _swiglu(x, w1, w2, w3):
            return jax.nn.silu(x @ w1) * (x @ w3) @ w2
        B, S, D = x.shape
        E, K = (NUM_EXPERTS, TOP_K)
        N = B * S
        x_flat = x.reshape(N, D)
        logits = x_flat @ router_w
        scores = jax.nn.softmax(logits.astype(jnp.float32), axis=-1)
        _, sel = jax.lax.top_k(scores + expert_bias[None, :], K)
        top_scores = jnp.take_along_axis(scores, sel, axis=-1)
        flat_exp = sel.reshape(-1)
        order = jnp.argsort(flat_exp)
        exp_sorted = flat_exp[order]
        routed_input = x_flat[order // K]
        routed_output = jnp.zeros_like(routed_input)
        for e in range(E):
            mask = (exp_sorted == e)[:, None]
            y_e = _swiglu(routed_input, w1[e], w2[e], w3[e])
            routed_output = routed_output + jnp.where(mask, y_e, 0.0)
        unsorted = jnp.zeros((N * K, D), routed_output.dtype).at[order].set(routed_output)
        unsorted = unsorted.reshape(N, K, D)
        out_experts = jnp.einsum('nk,nkd->nd', top_scores, unsorted)
        shared_out = _swiglu(x_flat, sw1, sw2, sw3)
        return (shared_out + out_experts).reshape(B, S, D)
    x = x + _L0_xattn_ref(_layernorm(x, axis=-1), ctx_1024, ctx_1024, L0_xattn_Wq, L0_xattn_bq, L0_xattn_Wk, L0_xattn_bk, L0_xattn_Wv, L0_xattn_bv, L0_xattn_Wo, L0_xattn_bo, L0_xattn_w1, L0_xattn_b1, L0_xattn_w2, L0_xattn_b2, L0_xattn_w3, L0_xattn_b3)
    x = x + _L0_ffn_ref(_layernorm(x, axis=-1), L0_ffn_rms_w, L0_ffn_gate_w, L0_ffn_W1, L0_ffn_b1, L0_ffn_W2, L0_ffn_b2)
    x = x + _L1_xattn_ref(ctx_1024, _layernorm(x, axis=-1), mask_BxS2_bk1, L1_xattn_Wq, L1_xattn_Wkv, L1_xattn_Wo, L1_xattn_ln_x_g, L1_xattn_ln_x_b, L1_xattn_ln_l_g, L1_xattn_ln_l_b, L1_xattn_ln_o_g, L1_xattn_ln_o_b)
    x = x + _L1_ffn_ref(_layernorm(x, axis=-1), L1_ffn_router_w, L1_ffn_expert_bias, L1_ffn_w1, L1_ffn_w2, L1_ffn_w3, L1_ffn_sw1, L1_ffn_sw2, L1_ffn_sw3)
    return x

_drawn_inputs = setup_inputs


def setup_inputs(seed=0):
    import zlib

    import numpy as np

    out = dict(_drawn_inputs(seed))
    spreads = {'L0_ffn_rms_w': (1.0, 0.6),
     'L0_ffn_b1': (0.0, 0.8),
     'L0_ffn_b2': (0.0, 0.597),
     'L1_xattn_ln_x_g': (1.0, 0.2),
     'L1_xattn_ln_x_b': (0.0, 0.1),
     'L1_xattn_ln_l_g': (1.0, 0.6),
     'L1_xattn_ln_l_b': (0.0, 0.1),
     'L1_xattn_ln_o_g': (1.0, 0.2),
     'L1_xattn_ln_o_b': (0.0, 0.1),
     'L1_ffn_expert_bias': (0.0, 0.8)}
    factors = {'L0_xattn_Wq': 8.0,
     'L0_xattn_bq': 8.0,
     'L0_xattn_Wk': 8.0,
     'L0_xattn_bk': 8.0,
     'L0_xattn_bv': 8.0,
     'L0_xattn_w1': 8.0,
     'L0_xattn_b1': 8.0,
     'L0_xattn_w2': 8.0,
     'L0_xattn_b2': 8.0,
     'L0_xattn_w3': 8.0,
     'L0_ffn_gate_w': 4.175,
     'L0_ffn_W1': 8.0,
     'L0_ffn_W2': 7.478,
     'L1_ffn_router_w': 8.0,
     'L1_ffn_w1': 8.0,
     'L1_ffn_w2': 8.0,
     'L1_ffn_w3': 8.0,
     'L1_ffn_sw1': 8.0,
     'L1_ffn_sw2': 8.0,
     'L1_ffn_sw3': 8.0}
    for name, (base, spread) in spreads.items():
        noise = np.random.default_rng([zlib.crc32(name.encode()), seed]).standard_normal(out[name].shape)
        drawn = base * np.exp(spread * noise) if base else spread * noise
        out[name] = jnp.asarray(drawn.astype(out[name].dtype))
    for name, factor in factors.items():
        out[name] = (out[name] * factor).astype(out[name].dtype)
    return out
```

```python
from contextlib import ExitStack, contextmanager

import concourse.bass as bass
from concourse import mybir

F32 = mybir.dt.float32
BF16 = mybir.dt.bfloat16
U8 = mybir.dt.uint8
I32 = mybir.dt.int32
ACT = mybir.ActivationFunctionType
ALU = mybir.AluOpType
AX = mybir.AxisListType

P = 128
B, SQ, SK, D = 8, 256, 512, 128
NT = B * SQ // P
QT, KT = SQ // P, SK // P
H0, DK = 16, 8
PAIRS = H0 // 2
ROWS = 6 * DK
MAXROWS = 3
LAG = 3
H1, DH = 8, 64
INNER = H1 * DH
NK1 = SK + SQ
KJ = NK1 // P
E0, F0 = 8, 512
FC = F0 // P
E1 = 8
LN_EPS, RMS_EPS = 1e-5, 1e-6
LOG_T_MIN, LOG_T_MAX = -2.302585092994046, 2.302585092994046
PARTS = [(0, 0), (1, 0), (2, 0), (0, 1), (0, 2), (1, 1)]


class Steps:

    def __init__(self, eng, sem):
        self.eng, self.sem, self.n, self.base = eng, sem, 0, 0

    @contextmanager
    def loop(self, start, end, step, per_turn):
        before, turns = self.n, (end - start) // step
        with self.eng.Fori(start, end, step) as i:
            self.base = (i - start) * (per_turn // step) if start else i * (per_turn // step)
            yield i
        assert self.n - before == per_turn and per_turn % step == 0, (self.n - before, per_turn)
        self.base = 0
        self.n = before + turns * per_turn

    def mark(self, ins):
        self.n += 1
        ins.then_inc(self.sem, 1)

    def wait(self):
        self.eng.wait_ge(self.sem, self.base + self.n)

    def done(self, ins):
        self.mark(ins)
        self.wait()


def layer_norm_stats(dve, steps, nc, src, tile_ids, stats, mv):
    for t in tile_ids:
        steps.mark(nc.vector.bn_stats(stats[:, t, :], src[:, t, :]))
    steps.wait()
    for t in tile_ids:
        steps.mark(nc.vector.bn_aggr(mv[:, t, :], stats[:, t, :]))
    steps.wait()


def build(nc, dram, out, upto=99):
    es = ExitStack()
    with es:
        def sb(stack, name, shape, dt=F32):
            return stack.enter_context(nc.sbuf_tensor(name, shape, dt))

        def sem(name):
            return es.enter_context(nc.semaphore(name))

        X = sb(es, "X", [P, NT, D])
        identf = sb(es, "identf", [P, P])
        identb = sb(es, "identb", [P, P], BF16)
        stats = sb(es, "stats", [P, 48, 6])
        mv = sb(es, "mv", [P, 48, 2])
        rstd = sb(es, "rstd", [P, 48])
        rtmp = sb(es, "rtmp", [P, 48])
        mhalf = sb(es, "mhalf", [P, 48])
        ps = es.enter_context(nc.psum_tensor("ps", [P, 8, 512], F32))
        env = dict(nc=nc, dram=dram, es=es, sb=sb, sem=sem, X=X, identf=identf, identb=identb, stats=stats,
                   mv=mv, rstd=rstd, rtmp=rtmp, mhalf=mhalf, ps=ps)
        with ExitStack() as la:
            attention0(env, la)
        if upto >= 2:
            with ExitStack() as lb:
                experts0(env, lb)
        if upto >= 3:
            with ExitStack() as lc:
                attention1(env, lc)
        if upto >= 4:
            with ExitStack() as ld:
                experts1(env, ld)
        stored = sem("stored")
        with nc.Block() as block:
            @block.sync
            def _(sp):
                sp.dma_start(out.rearrange("(t p) d -> p t d", p=P), X[:, :, :]).then_inc(stored, 16)
                sp.wait_ge(stored, 16)


def attention0(env, stack):
    nc, dram, sem, X, ps = env["nc"], env["dram"], env["sem"], env["X"], env["ps"]
    identf, identb, stats, mv = env["identf"], env["identb"], env["stats"], env["mv"]
    rstd, rtmp, mhalf = env["rstd"], env["rtmp"], env["mhalf"]

    def sb(name, shape, dt=F32):
        return env["sb"](stack, name, shape, dt)

    C = 1.0 / DK ** 0.5
    Qf = sb("Qf", [P, B, SQ])
    Kf = sb("Kf", [P, B, SK])
    V = sb("V", [P, B * KT, H0, DK + 1])
    qsum, ksum = sb("qsum", [P, B]), sb("ksum", [P, B])
    sel, prodsel = sb("sel", [P, H0]), sb("prodsel", [P, B, H0])
    Qp, Kp = sb("Qp", [P, 3, SQ], BF16), sb("Kp", [P, 3, SK], BF16)
    qres, kres = sb("qres", [P, SQ]), sb("kres", [P, SK])
    Q1 = [sb(f"Q1_{i}", [P, PAIRS, SQ], BF16) for i in range(2)]
    K1 = [sb(f"K1_{i}", [P, PAIRS, SK], BF16) for i in range(2)]
    Q2 = [sb(f"Q2_{i}", [P, PAIRS, SQ], BF16) for i in range(2)]
    K2 = [sb(f"K2_{i}", [P, PAIRS, SK], BF16) for i in range(2)]
    boB = sb("boB", [P, D])
    woT = sb("woT", [P, D])
    w1c = sb("w1c", [P, 3, 64])
    w2T = sb("w2T", [64, 64])
    b1c, b2c = sb("b1c", [64, 1]), sb("b2c", [64, 1])
    w3c, b3c = sb("w3c", [64, P]), sb("b3c", [P, 1])

    Vw = [sb(f"Vw{i}", [P, KT, H0, 32]) for i in range(2)]
    parts_ready = sem("parts_ready")
    loaded = {n: sem(f"ld0_{n}") for n in ("x", "ctx0", "ctx2", "ctx4", "ctx6", "proj", "consts")}
    with ExitStack() as pro:
        def pb(name, shape, dt=F32):
            return env["sb"](pro, name, shape, dt)
        ctxT = pb("ctxT", [P, B, SK])
        Xn = pb("Xn", [P, NT, D])
        XnT = pb("XnT", [P, NT * P])
        wqT, wkT, wvT = pb("wqT", [P, D]), pb("wkT", [P, D]), pb("wvT", [P, D])
        bqc, bkc, bqn = pb("bqc", [P, 1]), pb("bkc", [P, 1]), pb("bqn", [P, 1])
        bvB = pb("bvB", [P, D])
        steps0, rs_ready, k_mm, v_mm = sem("steps0"), sem("rs_ready"), sem("k_mm"), sem("v_mm")
        xn_ready, t_mm, xt_ready, q_mm, q_out, k_out, v_out = (
            sem(n) for n in ("xn_ready", "t_mm", "xt_ready", "q_mm", "q_out", "k_out", "v_out"))
        bq_neg, pool0, mv_ready = sem("bq_neg"), sem("pool0"), sem("mv_ready")
        ones_set, steps1 = sem("ones_set"), sem("steps1")

        with nc.Block() as block:
            @block.sync
            def _(sp):
                xt = dram["x"].rearrange("(t p) d -> p t d", p=P)
                sp.dma_start(X[:, 0:NT // 2, :], xt[:, 0:NT // 2, :]).then_inc(loaded["x"], 16)
                sp.dma_start(X[:, NT // 2:NT, :], xt[:, NT // 2:NT, :]).then_inc(loaded["x"], 16)
                for n, t in (("wk0T", wkT), ("wv0T", wvT), ("wq0T", wqT)):
                    sp.dma_start(t[:, :], dram[n]).then_inc(loaded["proj"], 16)
                sp.dma_start(bkc[:, :], dram["bk0"]).then_inc(loaded["proj"], 16)
                sp.dma_start(bqc[:, :], dram["bq0"]).then_inc(loaded["proj"], 16)
                sp.dma_start(bvB[:, :], dram["bv0"].to_broadcast([P, D])).then_inc(loaded["proj"], 16)
                for b in range(0, B, 2):
                    sp.dma_start(ctxT[:, b:b + 2, :], dram["ctxT"][:, b:b + 2, :]).then_inc(loaded[f"ctx{b}"], 16)
                sp.dma_start(identf[:, :], dram["ident"]).then_inc(loaded["consts"], 16)
                sp.dma_start(boB[:, :], dram["bo0"].to_broadcast([P, D])).then_inc(loaded["consts"], 16)
                sp.dma_start(woT[:, :], dram["wo0T"]).then_inc(loaded["consts"], 16)
                sp.dma_start(sel[:, :], dram["sel"]).then_inc(loaded["consts"], 16)
                for f in range(3):
                    sp.dma_start(w1c[:, f, :], dram["tw1T"][f:f + 1, :].to_broadcast([P, 64])).then_inc(loaded["consts"], 16)
                sp.dma_start(w2T[:, :], dram["tw2T"]).then_inc(loaded["consts"], 16)
                sp.dma_start(b1c[:, :], dram["tb1"]).then_inc(loaded["consts"], 16)
                sp.dma_start(b2c[:, :], dram["tb2"]).then_inc(loaded["consts"], 16)
                sp.dma_start(w3c[:, :], dram["tw3"]).then_inc(loaded["consts"], 16)
                sp.dma_start(b3c[:, :], dram["tb3"].to_broadcast([P, 1])).then_inc(loaded["consts"], 16)

            @block.gpsimd
            def _(pool):
                nc.gpsimd.memset(mhalf[:, :], -0.5).then_inc(pool0, 1)
                pool.wait_ge(mv_ready, 1)
                nc.gpsimd.tensor_scalar(rtmp[:, 0:NT], mv[:, 0:NT, 1], LN_EPS, None, ALU.add).then_inc(pool0, 1)
                pool.wait_ge(pool0, 2)
                nc.gpsimd.tensor_tensor(rstd[:, 0:NT], rtmp[:, 0:NT], mhalf[:, 0:NT], ALU.pow).then_inc(rs_ready, 1)
                for i in range(2):
                    nc.gpsimd.memset(Vw[i][:, :, :, :], 0.0).then_inc(ones_set, 1)
                for i in range(2):
                    nc.gpsimd.memset(K1[i][:, :, :], 1.0).then_inc(ones_set, 1)

            @block.tensor
            def _(pe):
                pe.wait_ge(loaded["proj"], 16 * 6)
                for b in range(B):
                    if b % 2 == 0:
                        pe.wait_ge(loaded[f"ctx{b}"], 16)
                    if b >= 2:
                        pe.wait_ge(k_out, b - 1)
                    nc.tensor.matmul(ps[:, b % 2, :], wkT[:, :], ctxT[:, b, :], start=True, stop=True).then_inc(k_mm, 1)
                    if b >= 2:
                        pe.wait_ge(v_out, b - 1)
                    for j in range(KT):
                        mm = nc.tensor.matmul(ps[:, 4 + b % 2, j * P:(j + 1) * P], ctxT[:, b, j * P:(j + 1) * P],
                                              wvT[:, :], start=True, stop=True)
                    mm.then_inc(v_mm, 1)
                pe.wait_ge(loaded["consts"], 16 * 12)
                for g in range(4):
                    pe.wait_ge(xn_ready, 4 * (g + 1))
                    for i in range(4):
                        mm = nc.tensor.transpose(ps[:, (2, 3, 6, 7)[g], i * P:(i + 1) * P], Xn[:, 4 * g + i, :], identf[:, :])
                    mm.then_inc(t_mm, 1)
                for g in range(4):
                    pe.wait_ge(xt_ready, g + 1)
                    if g < 2:
                        pe.wait_ge(k_out, B)
                    if g >= 2:
                        pe.wait_ge(v_out, B)
                    nc.tensor.matmul(ps[:, (0, 1, 4, 5)[g], :], wqT[:, :], XnT[:, g * 512:(g + 1) * 512],
                                     start=True, stop=True).then_inc(q_mm, 1)

            @block.scalar
            def _(act):
                act.wait_ge(loaded["proj"], 16 * 6)
                nc.scalar.mul(bqn[:, :], bqc[:, :], -C).then_inc(bq_neg, 1)
                for b in range(B):
                    act.wait_ge(k_mm, b + 1)
                    nc.scalar.activation(Kf[:, b, :], ps[:, b % 2, :], ACT.Identity, bias=bkc[:, :],
                                         accum_out=ksum[:, b:b + 1]).then_inc(k_out, 1)
                for g in range(4):
                    act.wait_ge(t_mm, g + 1)
                    nc.scalar.copy(XnT[:, g * 512:(g + 1) * 512], ps[:, (2, 3, 6, 7)[g], :]).then_inc(xt_ready, 1)
                act.wait_ge(bq_neg, 1)
                for b in range(B):
                    g = b // 2
                    act.wait_ge(q_mm, g + 1)
                    nc.scalar.activation(Qf[:, b, :], ps[:, (0, 1, 4, 5)[g], (b % 2) * SQ:(b % 2 + 1) * SQ], ACT.Identity,
                                         bias=bqn[:, :], scale=-C, accum_out=qsum[:, b:b + 1]).then_inc(q_out, 1)

            @block.vector
            def _(dve):
                st, st2 = Steps(dve, steps0), Steps(dve, steps1)
                dve.wait_ge(loaded["x"], 32)
                layer_norm_stats(dve, st, nc, X, range(NT), stats, mv)
                nc.vector.memset(V[:, :, :, DK:DK + 1], 1.0).then_inc(mv_ready, 1)
                dve.wait_ge(loaded["proj"], 16 * 6)

                def v_evac(b):
                    dve.wait_ge(v_mm, b + 1)
                    nc.vector.tensor_tensor(
                        V[:, b * KT:(b + 1) * KT, :, 0:DK],
                        ps[:, 4 + b % 2, :].rearrange("p (j h d) -> p j h d", j=KT, h=H0),
                        bvB[:, :].rearrange("p (a h d) -> p a h d", a=1, h=H0).to_broadcast([P, KT, H0, DK]),
                        ALU.add).then_inc(v_out, 1)
                for b in range(2):
                    v_evac(b)
                dve.wait_ge(rs_ready, 1)
                for t in range(NT):
                    nc.vector.tensor_scalar(Xn[:, t, :], X[:, t, :], mv[:, t, 0:1], rstd[:, t:t + 1],
                                            ALU.subtract, ALU.mult).then_inc(xn_ready, 1)
                    if t % 3 == 2 and t // 3 + 2 < B:
                        v_evac(t // 3 + 2)
                for b in range(NT // 3 + 2, B):
                    v_evac(b)
                dve.wait_ge(loaded["consts"], 16 * 12)
                nc.vector.tensor_copy(identb[:, :], identf[:, :]).then_inc(steps0, 1)
                dve.wait_ge(xn_ready, NT)
                nc.vector.tensor_tensor(X[:, :, :], X[:, :, :],
                                        boB[:, :].rearrange("p (a d) -> p a d", a=1).to_broadcast([P, NT, D]),
                                        ALU.add).then_inc(steps0, 1)
                for f, c in enumerate((-1.0 / (SQ * SK), -1.0 / SQ, 1.0 / (SQ * (SK - 1.0) * (SK / 2) ** 2))):
                    nc.vector.tensor_scalar(w1c[:, f, :], w1c[:, f, :], c, None, ALU.mult).then_inc(steps0, 1)
                for f32_, parts, res, n in ((Kf[:, 0, :], Kp, kres, B), (Qf[:, 0, :], Qp, qres, 1)):
                    dve.wait_ge(k_out if parts is Kp else q_out, n)
                    st2.done(nc.vector.tensor_copy(parts[:, 0, :], f32_))
                    st2.done(nc.vector.tensor_tensor(res[:, :], f32_, parts[:, 0, :], ALU.subtract))
                    st2.done(nc.vector.tensor_copy(parts[:, 1, :], res[:, :]))
                    nc.vector.tensor_tensor(parts[:, 2, :], res[:, :], parts[:, 1, :], ALU.subtract).then_inc(parts_ready, 1)
                dve.wait_ge(q_out, B)
                for b in range(B):
                    nc.vector.tensor_scalar(prodsel[:, b, :], sel[:, :], qsum[:, b:b + 1], ksum[:, b:b + 1],
                                            ALU.mult, ALU.mult).then_inc(steps0, 1)

    RB = ROWS + MAXROWS
    minv = [sb(f"minv{i}", [P, 2, PAIRS, QT]) for i in range(2)]
    bst = sb("bst", [P, H0 * QT, 6])
    e1 = [sb(f"e1_{i}", [P, QT, SK]) for i in range(4)]
    e2 = [sb(f"e2_{i}", [P, KT, SQ]) for i in range(2)]
    maxp = sb("maxp", [P, 2, MAXROWS, PAIRS, QT], BF16)
    maxres = sb("maxres", [P, 2, PAIRS * QT])
    NROW = 2 * MAXROWS * PAIRS * QT
    maxpT = sb("maxpT", [NROW, P], BF16)
    vs = [sb(f"vs{i}", [P, H0 * QT]) for i in range(8)]
    h1, h2 = sb("h1", [64, H0]), sb("h2", [64, H0])
    logt, invt, tscale = sb("logt", [P, H0]), sb("invt", [P, H0]), sb("tscale", [P, H0])
    OT = [sb(f"OT{i}", [P, 2 * SQ]) for i in range(2)]
    rz = sb("rz", [P, 2, QT, 4])
    On = sb("On", [P, QT, D])
    OnT = sb("OnT", [P, QT * P])

    S1_BANKS, S2_BANK, O_BANK, M_BANK = (0, 2), 4, 6, 7
    s = {n: sem("a0_" + n) for n in (
        "stack1", "stack2", "max_rows", "s1_ready", "s1_min", "e1_ready", "e1_used", "s2_ready", "e2_ready",
        "pv_done", "v_ready", "maxp_ready", "maxp_mm", "maxp_out", "f_ready", "m1_mm", "g1", "m2_mm", "g2",
        "m3_mm", "logt_ready", "invt_ready", "t_ready", "ot_out", "ot_mm", "on_ready", "on_mm", "on_out", "wo_mm", "x_added",
        "dstep", "pstep")}
    N1, N2, NM = 24 * 16, 3 * 16, 2 * 16

    def at(k, n):
        return k >= n if isinstance(k, int) else True

    def is_last(k):
        return isinstance(k, int) and k == B - 1

    def sync_step(sp, k, par):
        if at(k, 2):
            sp.wait_ge(s["s2_ready"], (k - 1) * H0)
        if at(k, 1):
            sp.wait_ge(s["stack2"], k * N2)
        sp.wait_ge(s["stack1"], (k + 1) * N1)
        sp.dma_start(K2[par][:, :, :], K1[par][:, :, :]).then_inc(s["stack2"], 16)
        for half in range(2):
            r = slice(64 * half, 64 * half + ROWS)
            sp.dma_start(Q2[par][r, :, :], Q1[par][r, :, :]).then_inc(s["stack2"], 16)
        if not is_last(k):
            sp.wait_ge(parts_ready, 2 * (k + 2))
            if at(k, 1):
                sp.wait_ge(s["s1_ready"], k * H0)
            load_stack1(sp, 1 - par)
        sp.wait_ge(s["maxp_out"], k + 1)
        for half in range(2):
            sp.dma_start(Q2[par][64 * half + ROWS:64 * half + RB, :, :],
                         maxpT[half * NROW // 2:(half + 1) * NROW // 2, :]).then_inc(s["max_rows"], 16)

    def load_stack1(sp, par):
        for parts, stack_, x in ((Qp, Q1[par], 0), (Kp, K1[par], 1)):
            for c, pair in enumerate(PARTS):
                for half in range(2):
                    r = 64 * half + DK * c
                    sp.dma_start(stack_[r:r + DK, :, :], parts[64 * half:64 * half + 64, pair[x], :]).then_inc(s["stack1"], 16)

    def gpsimd_step(pool, st, k, par):
        if not is_last(k):
            pool.wait_ge(s["stack1"], (k + 1) * N1)
            for full, parts, res in ((Kf, Kp, kres), (Qf, Qp, qres)):
                src = full[:, k + 1, :]
                st.done(nc.gpsimd.tensor_copy(parts[:, 0, :], src))
                st.done(nc.gpsimd.tensor_tensor(res[:, :], src, parts[:, 0, :], ALU.subtract))
                st.done(nc.gpsimd.tensor_copy(parts[:, 1, :], res[:, :]))
                nc.gpsimd.tensor_tensor(parts[:, 2, :], res[:, :], parts[:, 1, :], ALU.subtract).then_inc(parts_ready, 1)
        if at(k, 2):
            pool.wait_ge(s["pv_done"], (k - 1) * H0)
        nc.gpsimd.tensor_copy(Vw[par][:, :, :, 0:DK + 1].rearrange("p j h c -> p (j h) c"),
                              V[:, k * KT:(k + 1) * KT, :, :].rearrange("p j h c -> p (j h) c")).then_inc(s["v_ready"], 1)

    def tensor_step(pe, k, par):
        first, second = not (isinstance(k, int) and k == B), at(k, 1)
        if isinstance(k, int) and k == 0:
            score1(pe, 0, par, 0)
        for h in range(H0 + LAG):
            g = h - LAG
            if first and h + 1 < H0:
                score1(pe, k, par, h + 1)
            if first and h + 1 == H0 and not is_last(k):
                score1(pe, k + 1, 1 - par, 0)
            if second and h == 0:
                temperature_mm(pe, k, par)
            if second and g >= 0:
                score2(pe, k, par, g)
            if second and g >= 1:
                values(pe, k, par, g - 1)
            if at(k, 2) and h == 2:
                output_transpose(pe, k, 1)
            if at(k, 2) and h == 4:
                normed_transpose(pe, k)
            if at(k, 2) and h == 6:
                project_mm(pe, k)
            if second and h == 13:
                output_transpose(pe, k, 0)
            if first and h == H0 + 1:
                pe.wait_ge(s["maxp_ready"], k + 1)
                if at(k, 1):
                    pe.wait_ge(s["on_ready"], 2 * k - 1)
                nc.tensor.transpose(ps[0:NROW, M_BANK, 0:64].bitcast(BF16),
                                    maxp[:, :, :, :, :].rearrange("p a b c d -> p (a b c d)"),
                                    identb[:, :]).then_inc(s["maxp_mm"], 1)
        if second:
            values(pe, k, par, H0 - 1)

    def score1(pe, k, par, h):
        base, pair = 64 * (h % 2), h // 2
        if h == 0:
            pe.wait_ge(s["stack1"], (k + 1) * N1)
        if h >= 2 or at(k, 1):
            pe.wait_ge(s["e1_ready"], k * H0 + h - 1)
        for q in range(QT):
            mm = nc.tensor.matmul(ps[:, S1_BANKS[h % 2] + q, :], Q1[par][base:base + ROWS, pair, q * P:(q + 1) * P],
                                  K1[par][base:base + ROWS, pair, :], start=True, stop=True)
        mm.then_inc(s["s1_ready"], 1)

    def score2(pe, k, par, g):
        base, pair = 64 * (g % 2), g // 2
        if g == 0:
            pe.wait_ge(s["stack2"], k * N2)
            pe.wait_ge(s["max_rows"], k * NM)
        if g >= 1 or at(k, 2):
            pe.wait_ge(s["e2_ready"], (k - 1) * H0 + g)
        for j in range(KT):
            mm = nc.tensor.matmul(ps[:, S2_BANK + j // 2, (j % 2) * SQ:(j % 2 + 1) * SQ],
                                  K2[1 - par][base:base + RB, pair, j * P:(j + 1) * P],
                                  Q2[1 - par][base:base + RB, pair, :], start=True, stop=True)
        mm.then_inc(s["s2_ready"], 1)

    def values(pe, k, par, g):
        pe.wait_ge(s["e2_ready"], (k - 1) * H0 + g + 1)
        if g == 0:
            pe.wait_ge(s["v_ready"], k)
        if g % 8 == 0 and (g or at(k, 2)):
            pe.wait_ge(s["ot_out"], 2 * (k - 1) + g // 8)
        r, c = 32 * (g % 4), (g // 4) % 2 * SQ
        for j in range(KT):
            mm = nc.tensor.matmul(ps[r:r + 32, O_BANK, c:c + SQ], Vw[1 - par][:, j, g, :], e2[g % 2][:, j, :],
                                  start=(j == 0), stop=(j == KT - 1))
        mm.then_inc(s["pv_done"], 1)

    def temperature_mm(pe, k, par):
        pe.wait_ge(s["f_ready"], k)
        pe.wait_ge(s["maxp_out"], k)
        o = ps[0:64, M_BANK, 64:64 + H0]
        fmin = minv[1 - par][:, :, :, :].rearrange("p a b q -> p (a b) q")
        fvar = vs[7][:, :].rearrange("p (u q) -> p u q", q=QT)
        nc.tensor.matmul(o, w1c[:, 0, :], prodsel[:, k - 1, :] if isinstance(k, int) else
                         prodsel[:, bass.ds(k - 1, 1), :].rearrange("p a h -> p (a h)"), start=True, stop=False)
        for q in range(QT):
            nc.tensor.matmul(o, w1c[:, 1, :], fmin[:, :, q], start=False, stop=False)
            mm = nc.tensor.matmul(o, w1c[:, 2, :], fvar[:, :, q], start=False, stop=(q == QT - 1))
        mm.then_inc(s["m1_mm"], 1)
        pe.wait_ge(loaded["consts"], 16 * 12)
        pe.wait_ge(s["g1"], k)
        nc.tensor.matmul(ps[0:64, M_BANK, 96:96 + H0], w2T[:, :], h1[:, :], start=True, stop=True).then_inc(s["m2_mm"], 1)
        pe.wait_ge(loaded["consts"], 16 * 12)
        pe.wait_ge(s["g2"], k)
        nc.tensor.matmul(ps[:, M_BANK, 128:128 + H0], w3c[:, :], h2[:, :], start=True, stop=True).then_inc(s["m3_mm"], 1)

    def output_transpose(pe, k, half):
        pe.wait_ge(s["ot_out"], 2 * k - 1 - half)
        if half and isinstance(k, int) and k > B:
            pe.wait_ge(s["on_ready"], 2 * k - 3)
        elif half or not at(k, 2):
            pe.wait_ge(s["logt_ready"], k)
        else:
            pe.wait_ge(s["x_added"], k - 1)
        for i in range(4):
            mm = nc.tensor.transpose(ps[:, M_BANK, i * P:(i + 1) * P], OT[half][:, i * P:(i + 1) * P], identf[:, :])
        mm.then_inc(s["ot_mm"], 1)

    def normed_transpose(pe, k):
        pe.wait_ge(s["on_ready"], 2 * (k - 1))
        for q in range(QT):
            mm = nc.tensor.transpose(ps[:, M_BANK, q * P:(q + 1) * P], On[:, q, :], identf[:, :])
        mm.then_inc(s["on_mm"], 1)

    def project_mm(pe, k):
        pe.wait_ge(s["on_out"], k - 1)
        for q in range(QT):
            mm = nc.tensor.matmul(ps[:, M_BANK, q * P:(q + 1) * P], OnT[:, q * P:(q + 1) * P], woT[:, :],
                                  start=True, stop=True)
        mm.then_inc(s["wo_mm"], 1)

    def output_evac(act, k, half):
        act.wait_ge(s["pv_done"], (k - 1) * H0 + (0 if half else 8))
        if at(k, 2 + half):
            act.wait_ge(s["ot_mm"], 2 * k - 3 - half)
        nc.scalar.copy(OT[half][:, :], ps[:, O_BANK, :]).then_inc(s["ot_out"], 1)

    def scalar_step(act, k, par):
        first, second = not (isinstance(k, int) and k == B), at(k, 1)
        for h in range(H0 + LAG):
            g = h - LAG
            if first and h < H0:
                act.wait_ge(s["s1_min"], k * H0 + h + 1)
                if h >= 4 or at(k, 1):
                    act.wait_ge(s["e1_used"], k * H0 + h - 3)
                for q in range(QT):
                    a = nc.scalar.activation(e1[h % 4][:, q, :], ps[:, S1_BANKS[h % 2] + q, :], ACT.Exp, scale=-1.0,
                                             bias=minv[par][:, h % 2, h // 2, q:q + 1])
                a.then_inc(s["e1_ready"], 1)
            if at(k, 2) and h == 0:
                output_evac(act, k, 1)
            if second and h == 12:
                output_evac(act, k, 0)
            if second and h == 0:
                act.wait_ge(s["m1_mm"], k)
                nc.scalar.activation(h1[:, :], ps[0:64, M_BANK, 64:64 + H0], ACT.Gelu, bias=b1c[:, :]).then_inc(s["g1"], 1)
                act.wait_ge(s["m2_mm"], k)
                nc.scalar.activation(h2[:, :], ps[0:64, M_BANK, 96:96 + H0], ACT.Gelu, bias=b2c[:, :]).then_inc(s["g2"], 1)
            if second and h == 1:
                act.wait_ge(s["logt_ready"], k)
                nc.scalar.activation(invt[:, :], logt[:, :], ACT.Exp, scale=-1.0).then_inc(s["invt_ready"], 1)
            if second and g >= 0:
                act.wait_ge(s["s2_ready"], (k - 1) * H0 + g + 1)
                if g >= 2 or at(k, 2):
                    act.wait_ge(s["pv_done"], (k - 1) * H0 + g - 1)
                if g == 0:
                    act.wait_ge(s["t_ready"], k)
                c = (g % 2) * PAIRS + g // 2
                nc.scalar.activation(e2[g % 2][:, :, :].rearrange("p j q -> p (j q)"),
                                     ps[:, S2_BANK:S2_BANK + 2, :].rearrange("p a b -> p (a b)"), ACT.Exp,
                                     scale=tscale[:, c:c + 1]).then_inc(s["e2_ready"], 1)
            if first and h == H0 + 1:
                act.wait_ge(s["maxp_mm"], k + 1)
                if at(k, 1):
                    act.wait_ge(s["max_rows"], k * NM)
                nc.scalar.copy(maxpT[:, :], ps[0:NROW, M_BANK, 0:64].bitcast(BF16)).then_inc(s["maxp_out"], 1)

    def vector_step(dve, st, k, par):
        first, second = not (isinstance(k, int) and k == B), at(k, 1)
        if isinstance(k, int) and k == 0:
            row_min(dve, k, par, 0)
        for h in range(H0):
            if first and h + 1 < H0:
                row_min(dve, k, par, h + 1)
            if first and h + 1 == H0:
                if not is_last(k):
                    row_min(dve, k + 1, 1 - par, 0)
                max_parts(dve, st, k, par)
            if first:
                dve.wait_ge(s["e1_ready"], k * H0 + h + 1)
                for q in range(QT):
                    i = nc.vector.bn_stats(bst[:, ((h % 2) * PAIRS + h // 2) * QT + q, :], e1[h % 4][:, q, :])
                i.then_inc(s["e1_used"], 1)
            if second and h == 0:
                dve.wait_ge(s["m3_mm"], k)
                st.done(nc.vector.tensor_scalar(logt[:, :], ps[:, M_BANK, 128:128 + H0], b3c[:, :], LOG_T_MIN, ALU.add, ALU.max))
                nc.vector.tensor_scalar(logt[:, :], logt[:, :], LOG_T_MAX, None, ALU.min).then_inc(s["logt_ready"], 1)
            if second and h == 1:
                dve.wait_ge(s["invt_ready"], k)
                if at(k, 2):
                    dve.wait_ge(s["e2_ready"], (k - 1) * H0)
                nc.vector.tensor_scalar(tscale[:, :], invt[:, :], -(DK ** 0.5) / 2.0, None, ALU.mult).then_inc(s["t_ready"], 1)
            if at(k, 2) and h == 3:
                output_norm(dve, st, k, 1)
            if at(k, 2) and h == 5:
                normed_copy(dve, k)
            if at(k, 2) and h == 7:
                output_add(dve, k)
            if second and h == 13:
                output_norm(dve, st, k, 0)
        if first:
            variances(dve, st, k)

    def row_min(dve, k, par, h):
        dve.wait_ge(s["s1_ready"], k * H0 + h + 1)
        nc.vector.tensor_reduce(minv[par][:, h % 2, h // 2, :], ps[:, S1_BANKS[h % 2]:S1_BANKS[h % 2] + QT, :], AX.X,
                                ALU.min).then_inc(s["s1_min"], 1)

    def max_parts(dve, st, k, par):
        dve.wait_ge(s["s1_min"], (k + 1) * H0)
        m = [minv[par][:, a, :, :].rearrange("p c q -> p (c q)") for a in range(2)]
        part = [[maxp[:, a, i, :, :].rearrange("p c q -> p (c q)") for i in range(3)] for a in range(2)]
        for a in range(2):
            st.mark(nc.vector.tensor_scalar(part[a][0], m[a], -1.0, None, ALU.mult))
        st.wait()
        for a in range(2):
            st.mark(nc.vector.scalar_tensor_tensor(maxres[:, a, :], m[a], -1.0, part[a][0], ALU.mult, ALU.subtract))
        st.wait()
        for a in range(2):
            st.mark(nc.vector.tensor_copy(part[a][1], maxres[:, a, :]))
        st.wait()
        for a in range(2):
            i = nc.vector.tensor_tensor(part[a][2], maxres[:, a, :], part[a][1], ALU.subtract)
        i.then_inc(s["maxp_ready"], 1)

    def variances(dve, st, k):
        dve.wait_ge(s["e1_used"], (k + 1) * H0)
        m, d, m2, dd, r, r2, v, f = (x[:, :] for x in vs)
        st.mark(nc.vector.tensor_tensor(m, bst[:, :, 1], bst[:, :, 4], ALU.add))
        st.mark(nc.vector.tensor_tensor(d, bst[:, :, 1], bst[:, :, 4], ALU.subtract))
        st.mark(nc.vector.tensor_tensor(m2, bst[:, :, 2], bst[:, :, 5], ALU.add))
        st.wait()
        st.mark(nc.vector.tensor_tensor(dd, d, d, ALU.mult))
        st.mark(nc.vector.reciprocal(r, m))
        st.wait()
        st.mark(nc.vector.scalar_tensor_tensor(v, dd, SK / 4.0, m2, ALU.mult, ALU.add))
        st.mark(nc.vector.tensor_tensor(r2, r, r, ALU.mult))
        st.wait()
        nc.vector.tensor_tensor(f, v, r2, ALU.mult).then_inc(s["f_ready"], 1)

    def output_norm(dve, st, k, half):
        dve.wait_ge(s["ot_mm"], 2 * k - 1 - half)
        o = ps[:, M_BANK, :].rearrange("p (c q h r) -> p c q h r", c=2, q=QT, h=4)
        for q in range(QT):
            st.mark(nc.vector.reciprocal(rz[:, :, q, :], o[:, :, q, :, DK]))
        st.wait()
        if half == 0 and at(k, 2):
            dve.wait_ge(s["on_mm"], k - 1)
        for q in range(QT):
            i = nc.vector.tensor_tensor(
                On[:, q, half * 64:half * 64 + 64].rearrange("p (c h d) -> p c h d", c=2, h=4), o[:, :, q, :, 0:DK],
                rz[:, :, q, :].rearrange("p c (h a) -> p c h a", a=1).to_broadcast([P, 2, 4, DK]), ALU.mult)
        i.then_inc(s["on_ready"], 1)

    def normed_copy(dve, k):
        dve.wait_ge(s["on_mm"], k - 1)
        nc.vector.tensor_copy(OnT[:, :], ps[:, M_BANK, 0:QT * P]).then_inc(s["on_out"], 1)

    def output_add(dve, k):
        dve.wait_ge(s["wo_mm"], k - 1)
        xs = X[:, bass.ds((k - 2) * QT, QT), :]
        nc.vector.tensor_tensor(xs, xs, ps[:, M_BANK, 0:QT * P].rearrange("p (q d) -> p q d", q=QT),
                                ALU.add).then_inc(s["x_added"], 1)

    with nc.Block() as block:
        @block.sync
        def _(sp):
            sp.wait_ge(parts_ready, 2)
            load_stack1(sp, 0)
            for k in range(B):
                sync_step(sp, k, k % 2)

        @block.gpsimd
        def _(pool):
            st = Steps(pool, s["pstep"])
            for k in range(B):
                gpsimd_step(pool, st, k, k % 2)

        @block.tensor
        def _(pe):
            for k in (0, 1):
                tensor_step(pe, k, k % 2)
            with pe.Fori(2, B - 2, 2) as i:
                tensor_step(pe, i, 0)
                tensor_step(pe, i + 1, 1)
            for k in (B - 2, B - 1, B):
                tensor_step(pe, k, k % 2)
            output_transpose(pe, B + 1, 1)
            normed_transpose(pe, B + 1)
            project_mm(pe, B + 1)

        @block.scalar
        def _(act):
            for k in (0, 1):
                scalar_step(act, k, k % 2)
            with act.Fori(2, B - 2, 2) as i:
                scalar_step(act, i, 0)
                scalar_step(act, i + 1, 1)
            for k in (B - 2, B - 1, B):
                scalar_step(act, k, k % 2)
            output_evac(act, B + 1, 1)

        @block.vector
        def _(dve):
            st = Steps(dve, s["dstep"])
            for k in (0, 1):
                vector_step(dve, st, k, k % 2)
            with st.loop(2, B - 2, 2, 2 * 18) as i:
                vector_step(dve, st, i, 0)
                vector_step(dve, st, i + 1, 1)
            for k in (B - 2, B - 1, B):
                vector_step(dve, st, k, k % 2)
            output_norm(dve, st, B + 1, 1)
            normed_copy(dve, B + 1)
            output_add(dve, B + 1)


def experts0(env, stack):
    nc, dram, sem, X, ps = env["nc"], env["dram"], env["sem"], env["X"], env["ps"]
    identf, stats, mv, rstd, rtmp, mhalf = (env[n] for n in ("identf", "stats", "mv", "rstd", "rtmp", "mhalf"))

    def sb(name, shape, dt=F32):
        return env["sb"](stack, name, shape, dt)

    W1 = sb("W1", [P, E0, F0])
    W2 = sb("W2", [P, E0, FC, D])
    b1t = sb("b1t", [P, E0 * FC])
    b2t = sb("b2t", [E0, D])
    rmsw = sb("rmsw", [P, 1])
    gwT = sb("gwT", [P, E0])
    rank = sb("rank", [P, E0])
    Xn = sb("XnB", [P, NT, D])
    XnT = sb("XnTB", [P, NT * P])
    L, ex, key, G = (sb(n, [P, NT, E0]) for n in ("LB", "exB", "keyB", "GB"))
    mx, den, kmx = (sb(n, [P, NT]) for n in ("mxB", "denB", "kmxB"))
    r1, r2 = sb("r1B", [P, NT]), sb("r2B", [P, NT])
    GT = sb("GTB", [E0, NT * P])
    hT = [sb(f"hTB{i}", [P, 512]) for i in range(8)]
    s = {n: sem("b_" + n) for n in (
        "small", "w1", "w2", "steps", "psteps", "stats", "rstd", "xn", "t_mm", "xt", "l_mm", "l_out", "shifted", "exps",
        "gates", "gt_mm", "gt_out", "bias_mm", "h_mm", "h_out", "y_mm", "y_added")}

    with nc.Block() as block:
        @block.sync
        def _(sp):
            for t, n in ((rmsw, "rms_w"), (gwT, "gate_wT"), (rank, "rank"), (b1t, "eb1"), (b2t, "eb2")):
                sp.dma_start(t[:, :], dram[n]).then_inc(s["small"], 16)
            sp.dma_start(W1[:, :, :], dram["eW1"].rearrange("e d f -> d e f")).then_inc(s["w1"], 16)
            sp.dma_start(W2[:, :, :, :].rearrange("p e c d -> p (e c) d"),
                         dram["eW2"].rearrange("e (c p) d -> p (e c) d", p=P)).then_inc(s["w2"], 16)

        @block.gpsimd
        def _(pool):
            st = Steps(pool, s["psteps"])
            pool.wait_ge(s["stats"], 1)
            v = mv[:, 0:NT, 1]
            st.done(nc.gpsimd.tensor_scalar(rtmp[:, 0:NT], v, LN_EPS, None, ALU.add))
            st.done(nc.gpsimd.tensor_tensor(r1[:, :], rtmp[:, 0:NT], mhalf[:, 0:NT], ALU.pow))
            st.done(nc.gpsimd.tensor_tensor(r2[:, :], r1[:, :], r1[:, :], ALU.mult))
            st.done(nc.gpsimd.tensor_tensor(r2[:, :], r2[:, :], v, ALU.mult))
            st.done(nc.gpsimd.tensor_scalar(r2[:, :], r2[:, :], RMS_EPS, None, ALU.add))
            st.done(nc.gpsimd.tensor_tensor(r2[:, :], r2[:, :], mhalf[:, 0:NT], ALU.pow))
            nc.gpsimd.tensor_tensor(rstd[:, 0:NT], r1[:, :], r2[:, :], ALU.mult).then_inc(s["rstd"], 1)

        @block.tensor
        def _(pe):
            for g in range(4):
                pe.wait_ge(s["xn"], 4 * (g + 1))
                for i in range(4):
                    mm = nc.tensor.transpose(ps[:, g, i * P:(i + 1) * P], Xn[:, 4 * g + i, :], identf[:, :])
                mm.then_inc(s["t_mm"], 1)
            pe.wait_ge(s["small"], 16 * 5)
            for t in range(NT):
                if t % 4 == 0:
                    pe.wait_ge(s["xt"], t // 4 + 1)
                mm = nc.tensor.matmul(ps[:, 4, t * E0:(t + 1) * E0], XnT[:, t * P:(t + 1) * P], gwT[:, :], start=True, stop=True)
            mm.then_inc(s["l_mm"], 1)
            pe.wait_ge(s["gates"], 1)
            for t in range(NT):
                mm = nc.tensor.transpose(ps[0:E0, t // 4, (t % 4) * P:(t % 4 + 1) * P], G[:, t, :], identf[:, :])
            mm.then_inc(s["gt_mm"], 1)
            pe.wait_ge(s["gt_out"], 1)
            for t in range(NT):
                mm = nc.tensor.matmul(ps[:, 4 + t // 4, (t % 4) * P:(t % 4 + 1) * P], GT[:, t * P:(t + 1) * P], b2t[:, :],
                                      start=True, stop=True)
            mm.then_inc(s["bias_mm"], 1)

        @block.scalar
        def _(act):
            act.wait_ge(s["small"], 16 * 5)
            for g in range(4):
                act.wait_ge(s["t_mm"], g + 1)
                nc.scalar.activation(XnT[:, g * 512:(g + 1) * 512], ps[:, g, :], ACT.Identity, scale=rmsw[:, :]).then_inc(s["xt"], 1)
            act.wait_ge(s["shifted"], 1)
            nc.scalar.activation(ex[:, :, :], ex[:, :, :], ACT.Exp).then_inc(s["exps"], 1)
            act.wait_ge(s["gt_mm"], 1)
            nc.scalar.copy(GT[:, :].rearrange("p (b c) -> p b c", b=4), ps[0:E0, 0:4, :]).then_inc(s["gt_out"], 1)

        @block.vector
        def _(dve):
            st = Steps(dve, s["steps"])
            layer_norm_stats(dve, st, nc, X, range(NT), stats, mv)
            nc.vector.memset(kmx[:, :], 0.0).then_inc(s["stats"], 1)
            dve.wait_ge(s["rstd"], 1)
            for t in range(NT):
                nc.vector.tensor_scalar(Xn[:, t, :], X[:, t, :], mv[:, t, 0:1], rstd[:, t:t + 1],
                                        ALU.subtract, ALU.mult).then_inc(s["xn"], 1)

            def over_experts(a):
                return a[:, :].rearrange("p (t a) -> p t a", a=1).to_broadcast([P, NT, E0])
            rk = rank[:, :].rearrange("p (a e) -> p a e", a=1).to_broadcast([P, NT, E0])
            dve.wait_ge(s["l_mm"], 1)
            st.done(nc.vector.tensor_copy(L[:, :, :].rearrange("p t e -> p (t e)"), ps[:, 4, 0:NT * E0]))
            st.done(nc.vector.tensor_reduce(mx[:, :], L[:, :, :], AX.X, ALU.max))
            nc.vector.tensor_tensor(ex[:, :, :], L[:, :, :], over_experts(mx), ALU.subtract).then_inc(s["shifted"], 1)
            dve.wait_ge(s["small"], 16 * 5)
            st.done(nc.vector.tensor_tensor(key[:, :, :], L[:, :, :], over_experts(mx), ALU.is_equal))
            st.done(nc.vector.tensor_tensor(key[:, :, :], key[:, :, :], rk, ALU.mult))
            st.done(nc.vector.tensor_reduce(kmx[:, :], key[:, :, :], AX.X, ALU.max))
            st.done(nc.vector.tensor_tensor(key[:, :, :], key[:, :, :], over_experts(kmx), ALU.is_equal))
            dve.wait_ge(s["exps"], 1)
            st.done(nc.vector.tensor_reduce(den[:, :], ex[:, :, :], AX.X, ALU.add))
            st.done(nc.vector.reciprocal(den[:, :], den[:, :]))
            nc.vector.tensor_tensor(G[:, :, :], key[:, :, :], over_experts(den), ALU.mult).then_inc(s["gates"], 1)
            dve.wait_ge(s["bias_mm"], 1)
            for g in range(4):
                st.mark(nc.vector.tensor_tensor(X[:, 4 * g:4 * g + 4, :], X[:, 4 * g:4 * g + 4, :],
                                                ps[:, 4 + g, :].rearrange("p (t d) -> p t d", t=4), ALU.add))
            st.wait()

    HB, YB = 0, 4
    with nc.Block() as block:
        @block.tensor
        def _(pe):
            pe.wait_ge(s["w1"], 16)
            pe.wait_ge(s["w2"], 16)

            def up(g, e):
                for f in range(FC):
                    n = g * (E0 * FC) + e * FC + f
                    if not (isinstance(g, int) and g == 0 and e == 0):
                        pe.wait_ge(s["h_out"], n - FC + 1)
                    nc.tensor.matmul(ps[:, HB + f, :], W1[:, e, f * P:(f + 1) * P], XnT[:, bass.ds(g * 512, 512)],
                                     start=True, stop=True).then_inc(s["h_mm"], 1)

            def down(g, e):
                pe.wait_ge(s["h_out"], g * (E0 * FC) + e * FC + FC)
                if not (isinstance(g, int) and g == 0 and e < 2):
                    pe.wait_ge(s["y_added"], g * E0 + e - 1)
                for t in range(4):
                    for f in range(FC):
                        mm = nc.tensor.matmul(ps[:, YB + e % 2, t * P:(t + 1) * P], hT[(e % 2) * FC + f][:, t * P:(t + 1) * P],
                                              W2[:, e, f, :], start=(f == 0), stop=(f == FC - 1))
                mm.then_inc(s["y_mm"], 1)

            def group(g):
                up(g, 0)
                for e in range(E0):
                    if e + 1 < E0:
                        up(g, e + 1)
                    down(g, e)
            group(0)
            with pe.Fori(1, 4) as g:
                group(g)

        @block.scalar
        def _(act):
            def group(g):
                for e in range(E0):
                    for f in range(FC):
                        act.wait_ge(s["h_mm"], g * (E0 * FC) + e * FC + f + 1)
                        if f == 0 and not (isinstance(g, int) and g == 0 and e < 2):
                            act.wait_ge(s["y_mm"], g * E0 + e - 1)
                        nc.scalar.activation(hT[(e % 2) * FC + f][:, :], ps[:, HB + f, :], ACT.Silu,
                                             bias=b1t[:, e * FC + f:e * FC + f + 1]).then_inc(s["h_out"], 1)
            group(0)
            with act.Fori(1, 4) as g:
                group(g)

        @block.vector
        def _(dve):
            def group(g):
                for e in range(E0):
                    dve.wait_ge(s["y_mm"], g * E0 + e + 1)
                    if not (isinstance(g, int) and g == 0 and e == 0):
                        dve.wait_ge(s["y_added"], g * E0 + e)
                    for t in range(4):
                        x = X[:, bass.ds(g * 4 + t, 1), :].rearrange("p a d -> p (a d)")
                        gate = G[:, bass.ds(g * 4 + t, 1), e:e + 1].rearrange("p a d -> p (a d)")
                        i = nc.vector.scalar_tensor_tensor(x, ps[:, YB + e % 2, t * P:(t + 1) * P], gate, x, ALU.mult, ALU.add)
                    i.then_inc(s["y_added"], 1)
            group(0)
            with dve.Fori(1, 4) as g:
                group(g)


def attention1(env, stack):
    nc, dram, sem, X, ps = env["nc"], env["dram"], env["sem"], env["X"], env["ps"]
    identf, stats, mv, rstd, rtmp, mhalf = (env[n] for n in ("identf", "stats", "mv", "rstd", "rtmp", "mhalf"))

    def sb(name, shape, dt=F32):
        return env["sb"](stack, name, shape, dt)

    NC = B * KT
    NA = NC + NT
    LT = sb("LT", [P, B, NK1])
    wq, wkv = sb("wq1", [P, INNER]), sb("wkv1", [P, 2 * INNER])
    wo = sb("wo1", [DH + 1, H1, D + 1])
    gout, bout = sb("gout", [P, D]), sb("bout", [P, D])
    mask01 = sb("mask01", [P, NC])
    s = {n: sem("c_" + n) for n in (
        "ctx", "small", "mask", "weights", "steps", "psteps", "stats", "eps_added", "rstd", "xn", "t_mm", "lt", "inv",
        "wo_cleared", "mask_cols", "filled", "biased")}

    with ExitStack() as pro:
        def pb(name, shape, dt=F32):
            return env["sb"](pro, name, shape, dt)
        CN = pb("CN", [P, NC, D])
        N = pb("Nc", [P, NA, D])
        gx, bx, gl, bl = (pb(n, [P, 1]) for n in ("gx", "bx", "gl", "bl"))
        maskB, maskc = pb("maskB", [P, B * SK // 4], I32), pb("maskc", [P, NC // 4], I32)
        invB = pb("invB", [P, B * SK], U8)
        r2 = pb("r2c", [P, NT])

        with nc.Block() as block:
            @block.sync
            def _(sp):
                sp.dma_start(CN[:, :, :], dram["ctx"].rearrange("(t p) d -> p t d", p=P)).then_inc(s["ctx"], 16)
                for t, n in ((gx, "lnx_g"), (bx, "lnx_b"), (gl, "lnl_g"), (bl, "lnl_b")):
                    sp.dma_start(t[:, :], dram[n]).then_inc(s["small"], 16)
                sp.dma_start(maskB[:, :], dram["mask"].to_broadcast([P, B * SK // 4])).then_inc(s["mask"], 16)
                sp.dma_start(maskc[:, :], dram["maskc"]).then_inc(s["mask"], 16)
                for t, n in ((wq, "wq1"), (wkv, "wkv1")):
                    sp.dma_start(t[:, :], dram[n]).then_inc(s["weights"], 16)
                sp.wait_ge(s["wo_cleared"], 2)
                sp.dma_start(wo[0:DH, :, 0:D], dram["wo1"].rearrange("(h p) d -> p h d", p=DH)).then_inc(s["weights"], 16)
                for t, n in ((gout, "lno_g"), (bout, "lno_b")):
                    sp.dma_start(t[:, :], dram[n].to_broadcast([P, D])).then_inc(s["weights"], 16)

            @block.gpsimd
            def _(pool):
                st = Steps(pool, s["psteps"])
                nc.gpsimd.memset(wo[:, :, :], 0.0).then_inc(s["wo_cleared"], 1)
                pool.wait_ge(s["wo_cleared"], 1)
                nc.gpsimd.memset(wo[DH:DH + 1, :, D:D + 1], 1.0).then_inc(s["wo_cleared"], 1)
                pool.wait_ge(s["wo_cleared"], 2)
                pool.wait_ge(s["stats"], 1)
                st.done(nc.gpsimd.tensor_scalar(rtmp[:, 0:NC], mv[:, 0:NC, 1], LN_EPS, None, ALU.add))
                nc.gpsimd.tensor_tensor(rstd[:, 0:NC], rtmp[:, 0:NC], mhalf[:, 0:NC], ALU.pow).then_inc(s["rstd"], 1)
                pool.wait_ge(s["stats"], 2)
                v, r1, r = mv[:, NC:NA, 1], rtmp[:, NC:NA], rstd[:, NC:NA]
                st.done(nc.gpsimd.tensor_scalar(r1, v, LN_EPS, None, ALU.add))
                st.done(nc.gpsimd.tensor_tensor(r1, r1, mhalf[:, NC:NA], ALU.pow))
                st.done(nc.gpsimd.tensor_tensor(r2[:, :], r1, r1, ALU.mult))
                st.done(nc.gpsimd.tensor_tensor(r2[:, :], r2[:, :], v, ALU.mult))
                st.done(nc.gpsimd.tensor_scalar(r2[:, :], r2[:, :], LN_EPS, None, ALU.add))
                st.done(nc.gpsimd.tensor_tensor(r2[:, :], r2[:, :], mhalf[:, 0:NT], ALU.pow))
                nc.gpsimd.tensor_tensor(r, r1, r2[:, :], ALU.mult).then_inc(s["rstd"], 1)
                pool.wait_ge(s["mask"], 32)
                nc.gpsimd.tensor_scalar(mask01[:, :], maskc[:, :].bitcast(U8), 0.0, None, ALU.add).then_inc(s["mask_cols"], 1)

            @block.tensor
            def _(pe):
                for g in range(NA // 4):
                    pe.wait_ge(s["xn"], 4 * (g + 1))
                    if g >= 8:
                        pe.wait_ge(s["lt"], g - 7)
                    for i in range(4):
                        mm = nc.tensor.transpose(ps[:, g % 8, i * P:(i + 1) * P], N[:, 4 * g + i, :], identf[:, :])
                    mm.then_inc(s["t_mm"], 1)

            @block.scalar
            def _(act):
                act.wait_ge(s["small"], 16 * 4)
                for g in range(NA // 4):
                    act.wait_ge(s["t_mm"], g + 1)
                    if g < B:
                        nc.scalar.activation(LT[:, g, 0:SK], ps[:, g % 8, :], ACT.Identity, scale=gx[:, :],
                                             bias=bx[:, :]).then_inc(s["lt"], 1)
                    else:
                        b = 2 * (g - B)
                        nc.scalar.activation(LT[:, b:b + 2, SK:NK1], ps[:, g % 8, :].rearrange("p (a q) -> p a q", a=2),
                                             ACT.Identity, scale=gl[:, :], bias=bl[:, :]).then_inc(s["lt"], 1)

            @block.vector
            def _(dve):
                st = Steps(dve, s["steps"])
                dve.wait_ge(s["ctx"], 16)
                for t in range(NC):
                    st.mark(nc.vector.bn_stats(stats[:, t, :], CN[:, t, :]))
                st.wait()
                for t in range(NC):
                    st.mark(nc.vector.bn_aggr(mv[:, t, :], stats[:, t, :]))
                st.wait()
                dve.wait_ge(s["mask"], 32)
                nc.vector.tensor_scalar(invB[:, :], maskB[:, :].bitcast(U8), 0.0, None, ALU.is_equal).then_inc(s["stats"], 1)
                for t in range(NT):
                    st.mark(nc.vector.bn_stats(stats[:, NC + t, :], X[:, t, :]))
                st.wait()
                for t in range(NT):
                    st.mark(nc.vector.bn_aggr(mv[:, NC + t, :], stats[:, NC + t, :]))
                st.wait()
                dve.wait_ge(s["rstd"], 1)
                for t in range(NA):
                    if t == 0:
                        nc.vector.tensor_scalar(N[:, 0, :], CN[:, 0, :], mv[:, 0, 0:1], rstd[:, 0:1], ALU.subtract, ALU.mult).then_inc(s["xn"], 1)
                        continue
                    if t == 1:
                        nc.vector.memset(stats[:, 0, 0:1], 0.0).then_inc(s["stats"], 1)
                    if t == NC:
                        dve.wait_ge(s["rstd"], 2)
                    src = CN[:, t, :] if t < NC else X[:, t - NC, :]
                    nc.vector.tensor_scalar(N[:, t, :], src, mv[:, t, 0:1], rstd[:, t:t + 1],
                                            ALU.subtract, ALU.mult).then_inc(s["xn"], 1)
                dve.wait_ge(s["stats"], 1)
                for b in range(B):
                    dve.wait_ge(s["lt"], B + b // 2 + 1)
                    nc.vector.copy_predicated(LT[:, b, 0:SK], invB[:, b * SK:(b + 1) * SK],
                                              LT[:, b, SK:SK + 1].to_broadcast([P, SK])).then_inc(s["filled"], 1)
                dve.wait_ge(s["weights"], 16 * 5)
                dve.wait_ge(s["xn"], NA)
                nc.vector.tensor_tensor(X[:, :, :], X[:, :, :],
                                        bout[:, :].rearrange("p (a d) -> p a d", a=1).to_broadcast([P, NT, D]),
                                        ALU.add).then_inc(s["biased"], 1)

    LTb = sb("LTb", [P, NK1])
    mkb = sb("mkb", [P, KT])
    Q = sb("Qc", [P, INNER // P, SQ])
    K = sb("Kc", [P, INNER // P, NK1])
    V = sb("Vc", [P, KJ, H1, DH + 1])
    mn, rz = sb("mnc", [P, 2]), sb("rzc", [P, QT])
    e = [sb(f"ec{i}", [P, 2, NK1 // 2]) for i in range(2)]
    eT = [sb(f"eTc{i}", [P, KJ, SQ]) for i in range(2)]
    OT = [sb(f"OTc{i}", [DH + 1, SQ]) for i in range(2)]
    y, yn = sb("yc", [P, QT, D]), sb("ync", [P, QT, D])
    T_BANK, O_BANK, Y_BANK = 4, 6, 7
    SCALE = 1.0 / DH
    UNITS, NJOB = H1 * QT, 8
    s = {n: sem("c1_" + n) for n in (
        "batch", "ones", "job_mm", "job_act", "job_dve", "s_mm", "row_min", "exp", "t_mm", "t_dve", "t_act",
        "pv_mm", "ot", "wo_mm", "y_added", "ystat", "yr", "yn", "dstep", "pstep")}

    def at(k, n):
        return k >= n if isinstance(k, int) else True

    def job_mm(pe, k, i):
        if i >= 3:
            pe.wait_ge(s["job_act" if (i - 3) % 2 == 0 else "job_dve"], k * 4 + (i - 3) // 2 + 1)
        bank = 2 * (i % 3)
        for a in range(2):
            if i < 3:
                j = 2 * i + a
                mm = nc.tensor.matmul(ps[:, bank + a, :], LTb[:, j * P:(j + 1) * P], wkv[:, INNER:2 * INNER], start=True, stop=True)
            elif i == 3:
                for c in (2 * a, 2 * a + 1):
                    mm = nc.tensor.matmul(ps[:, bank + a, (c % 2) * SQ:(c % 2 + 1) * SQ], wq[:, c * P:(c + 1) * P],
                                          LTb[:, SK:NK1], start=True, stop=True)
            else:
                c = i - 4
                mm = nc.tensor.matmul(ps[:, bank + a, 0:NK1 // 2], wkv[:, c * P:(c + 1) * P],
                                      LTb[:, a * NK1 // 2:(a + 1) * NK1 // 2], start=True, stop=True)
        mm.then_inc(s["job_mm"], 1)

    def job_out(eng, k, i):
        eng.wait_ge(s["job_mm"], k * NJOB + i + 1)
        bank, on_act = 2 * (i % 3), i % 2 == 0
        if i < 3:
            for a in range(2):
                j = 2 * i + a
                src, dst = ps[:, bank + a, :].rearrange("p (h d) -> p h d", h=H1), V[:, j, :, 0:DH]
                if on_act:
                    ins = nc.scalar.activation(dst, src, ACT.Copy, scale=mkb[:, j:j + 1] if j < KT else 1.0)
                else:
                    ins = nc.vector.tensor_scalar(dst, src, mkb[:, j:j + 1], None, ALU.mult)
        elif i == 3:
            ins = nc.vector.tensor_scalar(Q[:, :, :].rearrange("p (a c) q -> p a (c q)", a=2), ps[:, bank:bank + 2, :],
                                          -SCALE, None, ALU.mult)
        else:
            src, dst = ps[:, bank:bank + 2, 0:NK1 // 2], K[:, i - 4, :].rearrange("p (a k) -> p a k", a=2)
            ins = nc.scalar.copy(dst, src) if on_act else nc.vector.tensor_copy(dst, src)
        ins.then_inc(s["job_act" if on_act else "job_dve"], 1)

    def score(pe, k, u):
        h, q = u // 2, u % 2
        r = slice(64 * (h % 2), 64 * (h % 2) + DH)
        if u == 0:
            pe.wait_ge(s["job_act"], k * 4 + 4)
        elif u == 1:
            pe.wait_ge(s["job_dve"], k * 4 + 4)
        else:
            pe.wait_ge(s["exp"], k * UNITS + u - 1)
        for a in range(2):
            mm = nc.tensor.matmul(ps[:, 2 * (u % 2) + a, 0:NK1 // 2], Q[r, h // 2, q * P:(q + 1) * P],
                                  K[r, h // 2, a * NK1 // 2:(a + 1) * NK1 // 2], start=True, stop=True)
        mm.then_inc(s["s_mm"], 1)

    def transpose(pe, k, u):
        pe.wait_ge(s["exp"], k * UNITS + u + 1)
        if u:
            pe.wait_ge(s["t_dve"], k * UNITS + u)
            pe.wait_ge(s["t_act"], k * UNITS + u)
        for j in range(KJ):
            mm = nc.tensor.transpose(ps[:, T_BANK + j // 4, (j % 4) * P:(j % 4 + 1) * P],
                                     e[u % 2][:, j // 3, (j % 3) * P:(j % 3 + 1) * P], identf[:, :])
            if j == 3:
                mm.then_inc(s["t_mm"], 1)
        mm.then_inc(s["t_mm"], 1)

    def values(pe, k, h, half):
        if half == 0:
            if h == 0:
                pe.wait_ge(s["ones"], k + 1)
            pe.wait_ge(s["t_dve"], k * UNITS + 2 * h + 2)
            pe.wait_ge(s["t_act"], k * UNITS + 2 * h + 2)
            if h or at(k, 1):
                pe.wait_ge(s["ot"], k * H1 + h)
        for j in range(3 * half, 3 * half + 3):
            mm = nc.tensor.matmul(ps[0:DH + 1, O_BANK, 0:SQ], V[:, j, h, :], eT[h % 2][:, j, :],
                                  start=(j == 0), stop=(j == KJ - 1))
        if half:
            mm.then_inc(s["pv_mm"], 1)

    def project_mm(pe, k, h):
        pe.wait_ge(s["ot"], k * H1 + h + 1)
        if h or at(k, 1):
            pe.wait_ge(s["y_added"], k * H1 + h)
        for q in range(QT):
            mm = nc.tensor.matmul(ps[:, Y_BANK, q * (D + 1):(q + 1) * (D + 1)], OT[h % 2][:, q * P:(q + 1) * P], wo[:, h, :],
                                  start=True, stop=True)
        mm.then_inc(s["wo_mm"], 1)

    def tensor_step(pe, k):
        pe.wait_ge(s["batch"], 2 * (k + 1))
        for i in range(NJOB):
            job_mm(pe, k, i)
            if i == 0 and at(k, 1):
                project_mm(pe, k - 1, H1 - 1)
        score(pe, k, 0)
        for u in range(UNITS):
            if u + 1 < UNITS:
                score(pe, k, u + 1)
            transpose(pe, k, u)
            if u >= 2:
                values(pe, k, (u - 2) // 2, u % 2)
            if u >= 4 and u % 2 == 0:
                project_mm(pe, k, (u - 4) // 2)
        project_mm(pe, k, H1 - 2)
        for half in range(2):
            values(pe, k, H1 - 1, half)

    def scalar_step(act, k):
        act.wait_ge(s["batch"], 2 * (k + 1))
        for i in range(0, NJOB, 2):
            job_out(act, k, i)

        def exps(u):
            act.wait_ge(s["row_min"], k * UNITS + u + 1)
            if u >= 2:
                act.wait_ge(s["t_mm"], 2 * (k * UNITS + u - 1))
            nc.scalar.activation(e[u % 2][:, :, :], ps[:, 2 * (u % 2):2 * (u % 2) + 2, 0:NK1 // 2], ACT.Exp, scale=-1.0,
                                 bias=mn[:, u % 2:u % 2 + 1]).then_inc(s["exp"], 1)
        exps(0)
        for u in range(UNITS):
            if u + 1 < UNITS:
                exps(u + 1)
            act.wait_ge(s["t_mm"], 2 * (k * UNITS + u + 1))
            nc.scalar.copy(eT[u // 2 % 2][:, 4:6, (u % 2) * P:(u % 2 + 1) * P],
                           ps[:, T_BANK + 1, 0:2 * P].rearrange("p (j q) -> p j q", q=P)).then_inc(s["t_act"], 1)
            if u >= 3 and u % 2:
                output_copy(act, k, (u - 3) // 2)
        output_copy(act, k, H1 - 1)

    def output_copy(act, k, h):
        act.wait_ge(s["pv_mm"], k * H1 + h + 1)
        if h >= 2 or at(k, 1):
            act.wait_ge(s["wo_mm"], k * H1 + h - 1)
        nc.scalar.copy(OT[h % 2][:, :], ps[0:DH + 1, O_BANK, 0:SQ]).then_inc(s["ot"], 1)

    def vector_step(dve, st, k):
        first = not (isinstance(k, int) and k == B)
        if first:
            dve.wait_ge(s["batch"], 2 * (k + 1))
        for i in range(1, NJOB, 2):
            if i == 5 and at(k, 1):
                st.wait()
            if first:
                job_out(dve, k, i)
            if i == 1 and at(k, 1):
                output_add(dve, st, k - 1, H1 - 1)
            if i == 3 and at(k, 1):
                dve.wait_ge(s["y_added"], k * H1)
                for q in range(QT):
                    st.mark(nc.vector.bn_stats(stats[:, q, :], y[:, q, :]))
            if i == 5 and at(k, 1):
                for q in range(QT):
                    ins = nc.vector.bn_aggr(mv[:, q, :], stats[:, q, :])
                ins.then_inc(s["ystat"], 1)

        def row_min(u):
            dve.wait_ge(s["s_mm"], k * UNITS + u + 1)
            nc.vector.tensor_reduce(mn[:, u % 2:u % 2 + 1], ps[:, 2 * (u % 2):2 * (u % 2) + 2, 0:NK1 // 2], AX.XY,
                                    ALU.min).then_inc(s["row_min"], 1)
        if first:
            row_min(0)
        for u in range(UNITS):
            if first and u + 1 < UNITS:
                row_min(u + 1)
            if first:
                dve.wait_ge(s["t_mm"], 2 * (k * UNITS + u) + 1)
                nc.vector.tensor_copy(eT[u // 2 % 2][:, 0:4, (u % 2) * P:(u % 2 + 1) * P],
                                      ps[:, T_BANK, :].rearrange("p (j q) -> p j q", q=P)).then_inc(s["t_dve"], 1)
            if u == 1 and at(k, 1):
                dve.wait_ge(s["yr"], k)
                for q in range(QT):
                    st.mark(nc.vector.tensor_scalar(yn[:, q, :], y[:, q, :], mv[:, q, 0:1], rstd[:, q:q + 1], ALU.subtract, ALU.mult))
                st.wait()
                st.done(nc.vector.tensor_tensor(yn[:, :, :], yn[:, :, :],
                                                gout[:, :].rearrange("p (a d) -> p a d", a=1).to_broadcast([P, QT, D]), ALU.mult))
                xs = X[:, bass.ds((k - 1) * QT, QT), :]
                nc.vector.tensor_tensor(xs, xs, yn[:, :, :], ALU.add).then_inc(s["yn"], 1)
            if first and u >= 4 and u % 2 == 0:
                output_add(dve, st, k, (u - 4) // 2)
        if first:
            output_add(dve, st, k, H1 - 2)

    def output_add(dve, st, k, h):
        dve.wait_ge(s["wo_mm"], k * H1 + h + 1)
        o = ps[:, Y_BANK, 0:QT * (D + 1)].rearrange("p (q d) -> p q d", q=QT)
        st.done(nc.vector.reciprocal(rz[:, :], o[:, :, D]))
        if h:
            dve.wait_ge(s["y_added"], k * H1 + h)
        for q in range(QT):
            if h == 0:
                ins = nc.vector.tensor_scalar(y[:, q, :], o[:, q, 0:D], rz[:, q:q + 1], None, ALU.mult)
            else:
                ins = nc.vector.scalar_tensor_tensor(y[:, q, :], o[:, q, 0:D], rz[:, q:q + 1], y[:, q, :], ALU.mult, ALU.add)
        ins.then_inc(s["y_added"], 1)

    with nc.Block() as block:
        @block.gpsimd
        def _(pool):
            st = Steps(pool, s["pstep"])

            def batch(b):
                if b:
                    pool.wait_ge(s["job_mm"], b * NJOB)
                nc.gpsimd.tensor_copy(LTb[:, :], LT[:, b, :]).then_inc(s["batch"], 1)
                if b:
                    pool.wait_ge(s["job_act"], 4 * b)
                    pool.wait_ge(s["job_dve"], 4 * b)
                nc.gpsimd.tensor_copy(mkb[:, :], mask01[:, b * KT:(b + 1) * KT]).then_inc(s["batch"], 1)
            nc.gpsimd.memset(V[:, KT:KJ, :, DH:DH + 1], 1.0).then_inc(s["pstep"], 1)
            st.n += 1
            st.wait()
            batch(0)
            for b in range(B + 1):
                if b < B:
                    if b:
                        pool.wait_ge(s["pv_mm"], b * H1)
                    nc.gpsimd.tensor_copy(
                        V[:, 0:KT, :, DH:DH + 1].rearrange("p j h c -> p j (h c)"),
                        mask01[:, b * KT:(b + 1) * KT].rearrange("p (j a) -> p j a", a=1).to_broadcast([P, KT, H1])).then_inc(s["ones"], 1)
                if b:
                    pool.wait_ge(s["ystat"], b)
                    st.done(nc.gpsimd.tensor_scalar(rtmp[:, 0:QT], mv[:, 0:QT, 1], LN_EPS, None, ALU.add))
                    if b >= 2:
                        pool.wait_ge(s["yn"], b - 1)
                    nc.gpsimd.tensor_tensor(rstd[:, 0:QT], rtmp[:, 0:QT], mhalf[:, 0:QT], ALU.pow).then_inc(s["yr"], 1)
                if b + 1 < B:
                    batch(b + 1)

        @block.tensor
        def _(pe):
            tensor_step(pe, 0)
            with pe.Fori(1, B) as k:
                tensor_step(pe, k)
            project_mm(pe, B - 1, H1 - 1)

        @block.scalar
        def _(act):
            scalar_step(act, 0)
            with act.Fori(1, B) as k:
                scalar_step(act, k)

        @block.vector
        def _(dve):
            st = Steps(dve, s["dstep"])
            vector_step(dve, st, 0)
            with st.loop(1, B, 1, 5 + H1) as k:
                vector_step(dve, st, k)
            vector_step(dve, st, B)


def experts1(env, stack):
    nc, dram, sem, X, ps = env["nc"], env["dram"], env["sem"], env["X"], env["ps"]
    identf, stats, mv, rstd, rtmp, mhalf = (env[n] for n in ("identf", "stats", "mv", "rstd", "rtmp", "mhalf"))

    def sb(name, shape, dt=F32):
        return env["sb"](stack, name, shape, dt)

    NE = E1 + 1
    W1, W3, W2 = (sb(n, [P, NE, D]) for n in ("W1d", "W3d", "W2d"))
    rw = sb("rw", [P, E1])
    rank, biasB = sb("rankD", [P, E1]), sb("biasB", [P, E1])
    Xn = sb("XnD", [P, NT, D])
    XnT = sb("XnTD", [P, NT * P])
    L, ex, k1, k2, key, G = (sb(n, [P, NT, E1]) for n in ("LD", "exD", "k1D", "k2D", "keyD", "GD"))
    mx, den, kmx = (sb(n, [P, NT]) for n in ("mxD", "denD", "kmxD"))
    silu = [sb(f"siluD{i}", [P, 512]) for i in range(3)]
    hid = [sb(f"hidD{i}", [P, 512]) for i in range(3)]
    s = {n: sem("d_" + n) for n in (
        "small", "weights", "steps", "psteps", "stats", "rstd", "xn", "t_mm", "xt", "l_mm", "shifted", "exps",
        "h_mm", "silu", "hid", "y_mm", "y_added")}

    with nc.Block() as block:
        @block.sync
        def _(sp):
            for t, n in ((rw, "router_w"), (rank, "rank")):
                sp.dma_start(t[:, :], dram[n]).then_inc(s["small"], 16)
            sp.dma_start(biasB[:, :], dram["expert_bias"].to_broadcast([P, E1])).then_inc(s["small"], 16)
            for t, n in ((W1, "w1"), (W3, "w3"), (W2, "w2")):
                sp.dma_start(t[:, 0:E1, :], dram[n].rearrange("e d f -> d e f")).then_inc(s["weights"], 16)
                sp.dma_start(t[:, E1, :], dram["s" + n]).then_inc(s["weights"], 16)

        @block.gpsimd
        def _(pool):
            st = Steps(pool, s["psteps"])
            pool.wait_ge(s["stats"], 1)
            st.done(nc.gpsimd.tensor_scalar(rtmp[:, 0:NT], mv[:, 0:NT, 1], LN_EPS, None, ALU.add))
            nc.gpsimd.tensor_tensor(rstd[:, 0:NT], rtmp[:, 0:NT], mhalf[:, 0:NT], ALU.pow).then_inc(s["rstd"], 1)

        @block.tensor
        def _(pe):
            for g in range(4):
                pe.wait_ge(s["xn"], 4 * (g + 1))
                for i in range(4):
                    mm = nc.tensor.transpose(ps[:, g, i * P:(i + 1) * P], Xn[:, 4 * g + i, :], identf[:, :])
                mm.then_inc(s["t_mm"], 1)
            pe.wait_ge(s["small"], 16 * 3)
            for t in range(NT):
                if t % 4 == 0:
                    pe.wait_ge(s["xt"], t // 4 + 1)
                mm = nc.tensor.matmul(ps[:, 4, t * E1:(t + 1) * E1], XnT[:, t * P:(t + 1) * P], rw[:, :], start=True, stop=True)
            mm.then_inc(s["l_mm"], 1)

        @block.scalar
        def _(act):
            for g in range(4):
                act.wait_ge(s["t_mm"], g + 1)
                nc.scalar.copy(XnT[:, g * 512:(g + 1) * 512], ps[:, g, :]).then_inc(s["xt"], 1)
            act.wait_ge(s["shifted"], 1)
            nc.scalar.activation(ex[:, :, :], ex[:, :, :], ACT.Exp).then_inc(s["exps"], 1)

        @block.vector
        def _(dve):
            st = Steps(dve, s["steps"])
            layer_norm_stats(dve, st, nc, X, range(NT), stats, mv)
            nc.vector.memset(kmx[:, :], 0.0).then_inc(s["stats"], 1)
            dve.wait_ge(s["rstd"], 1)
            for t in range(NT):
                nc.vector.tensor_scalar(Xn[:, t, :], X[:, t, :], mv[:, t, 0:1], rstd[:, t:t + 1],
                                        ALU.subtract, ALU.mult).then_inc(s["xn"], 1)

            def over_experts(a):
                return a[:, :].rearrange("p (t a) -> p t a", a=1).to_broadcast([P, NT, E1])

            def over_tiles(a):
                return a[:, :].rearrange("p (a e) -> p a e", a=1).to_broadcast([P, NT, E1])

            def first_of_max(dst, src):
                st.done(nc.vector.tensor_reduce(mx[:, :], src[:, :, :], AX.X, ALU.max))
                st.done(nc.vector.tensor_tensor(key[:, :, :], src[:, :, :], over_experts(mx), ALU.is_equal))
                st.done(nc.vector.tensor_tensor(key[:, :, :], key[:, :, :], over_tiles(rank), ALU.mult))
                st.done(nc.vector.tensor_reduce(kmx[:, :], key[:, :, :], AX.X, ALU.max))
                st.done(nc.vector.tensor_tensor(dst[:, :, :], key[:, :, :], over_experts(kmx), ALU.is_equal))
            dve.wait_ge(s["l_mm"], 1)
            st.done(nc.vector.tensor_copy(L[:, :, :].rearrange("p t e -> p (t e)"), ps[:, 4, 0:NT * E1]))
            st.done(nc.vector.tensor_reduce(mx[:, :], L[:, :, :], AX.X, ALU.max))
            nc.vector.tensor_tensor(ex[:, :, :], L[:, :, :], over_experts(mx), ALU.subtract).then_inc(s["shifted"], 1)
            dve.wait_ge(s["small"], 16 * 3)
            dve.wait_ge(s["exps"], 1)
            st.done(nc.vector.tensor_reduce(den[:, :], ex[:, :, :], AX.X, ALU.add))
            st.done(nc.vector.reciprocal(den[:, :], den[:, :]))
            st.done(nc.vector.tensor_tensor(ex[:, :, :], ex[:, :, :], over_experts(den), ALU.mult))
            st.done(nc.vector.tensor_tensor(L[:, :, :], ex[:, :, :], over_tiles(biasB), ALU.add))
            first_of_max(k1, L)
            st.done(nc.vector.scalar_tensor_tensor(L[:, :, :], k1[:, :, :], -3e38, L[:, :, :], ALU.mult, ALU.add))
            first_of_max(k2, L)
            st.done(nc.vector.tensor_tensor(k1[:, :, :], k1[:, :, :], k2[:, :, :], ALU.add))
            st.done(nc.vector.tensor_tensor(G[:, :, :], k1[:, :, :], ex[:, :, :], ALU.mult))

    def y_wait(g, e):
        return g * NE + e - (0 if e == 0 else 2 if e == 1 else 1)

    with nc.Block() as block:
        @block.tensor
        def _(pe):
            pe.wait_ge(s["weights"], 16 * 6)

            def up(g, e):
                n, peeled = g * NE + e, isinstance(g, int) and g == 0
                if not (peeled and e < 3):
                    pe.wait_ge(s["hid"], n - 2)
                for i, w in enumerate((W1, W3)):
                    nc.tensor.matmul(ps[:, 3 * i + e % 3, :], w[:, e, :], XnT[:, bass.ds(g * 512, 512)],
                                     start=True, stop=True).then_inc(s["h_mm"], 1)

            def down(g, e):
                pe.wait_ge(s["hid"], g * NE + e + 1)
                if not (isinstance(g, int) and g == 0 and e < 2):
                    pe.wait_ge(s["y_added"], y_wait(g, e))
                for t in range(4):
                    mm = nc.tensor.matmul(ps[:, 6 + e % 2, t * P:(t + 1) * P], hid[e % 3][:, t * P:(t + 1) * P],
                                          W2[:, e, :], start=True, stop=True)
                mm.then_inc(s["y_mm"], 1)

            def group(g):
                up(g, 0)
                up(g, 1)
                for e in range(NE):
                    if e + 2 < NE:
                        up(g, e + 2)
                    down(g, e)
            group(0)
            with pe.Fori(1, 4) as g:
                group(g)

        @block.scalar
        def _(act):
            def group(g):
                for e in range(NE):
                    n = g * NE + e
                    act.wait_ge(s["h_mm"], 2 * n + 1)
                    if not (isinstance(g, int) and g == 0 and e < 3):
                        act.wait_ge(s["hid"], n - 2)
                    nc.scalar.activation(silu[e % 3][:, :], ps[:, e % 3, :], ACT.Silu).then_inc(s["silu"], 1)
            group(0)
            with act.Fori(1, 4) as g:
                group(g)

        @block.vector
        def _(dve):
            def hidden(g, e):
                n = g * NE + e
                dve.wait_ge(s["silu"], n + 1)
                dve.wait_ge(s["h_mm"], 2 * n + 2)
                if not (isinstance(g, int) and g == 0 and e < 3):
                    dve.wait_ge(s["y_mm"], n - 2)
                nc.vector.tensor_tensor(hid[e % 3][:, :], silu[e % 3][:, :], ps[:, 3 + e % 3, :], ALU.mult).then_inc(s["hid"], 1)

            def group(g):
                hidden(g, 0)
                for e in range(NE):
                    if e + 1 < NE:
                        hidden(g, e + 1)
                    dve.wait_ge(s["y_mm"], g * NE + e + 1)
                    if not (isinstance(g, int) and g == 0 and e == 0):
                        dve.wait_ge(s["y_added"], g * NE + e)
                    yb = ps[:, 6 + e % 2, :]
                    if e == E1:
                        x = X[:, bass.ds(g * 4, 4), :]
                        i = nc.vector.tensor_tensor(x, x, yb.rearrange("p (t d) -> p t d", t=4), ALU.add)
                    else:
                        for t in range(4):
                            x = X[:, bass.ds(g * 4 + t, 1), :].rearrange("p a d -> p (a d)")
                            gate = G[:, bass.ds(g * 4 + t, 1), e:e + 1].rearrange("p a d -> p (a d)")
                            i = nc.vector.scalar_tensor_tensor(x, yb[:, t * P:(t + 1) * P], gate, x, ALU.mult, ALU.add)
                    i.then_inc(s["y_added"], 1)
            group(0)
            with dve.Fori(1, 4) as g:
                group(g)


def kernel(**inputs):
    import numpy as np
    import concourse.bacc as bacc
    from concourse.bass_utils import run_bass_kernel_spmd as run

    v = {k: np.asarray(a) for k, a in inputs.items()}
    perm = np.arange(D).reshape(PAIRS, 2, DK).transpose(1, 2, 0).reshape(-1)
    w = lambda a: np.ascontiguousarray(a)
    sel = np.zeros((2, DK, PAIRS, 2, PAIRS), np.float32)
    for half in range(2):
        for pair in range(PAIRS):
            sel[half, :, pair, half, pair] = 1
    arrays = {
        "x": w(v["x"].reshape(B * SQ, D)),
        "ctx": w(v["ctx_1024"].reshape(B * SK, D)),
        "ctxT": w(v["ctx_1024"].transpose(2, 0, 1)),
        "mask": w(v["mask_BxS2_bk1"]).view(np.int32).reshape(1, B * SK // 4),
        "ident": np.eye(P, dtype=np.float32),
        "sel": sel.reshape(P, H0),
        "wq0T": w(v["L0_xattn_Wq"][perm].T), "bq0": w(v["L0_xattn_bq"][perm].reshape(D, 1)),
        "wk0T": w(v["L0_xattn_Wk"][perm].T), "bk0": w(v["L0_xattn_bk"][perm].reshape(D, 1)),
        "wv0T": w(v["L0_xattn_Wv"].T), "bv0": w(v["L0_xattn_bv"].reshape(1, D)),
        "wo0T": w(v["L0_xattn_Wo"].T), "bo0": w(v["L0_xattn_bo"].reshape(1, D)),
        "tw1T": w(v["L0_xattn_w1"].T), "tb1": w(v["L0_xattn_b1"].reshape(64, 1)),
        "tw2T": w(v["L0_xattn_w2"].T), "tb2": w(v["L0_xattn_b2"].reshape(64, 1)),
        "rms_w": w(v["L0_ffn_rms_w"].reshape(D, 1)), "gate_wT": w(v["L0_ffn_gate_w"].T),
        "rank": np.tile(np.arange(E0, 0, -1, dtype=np.float32), (P, 1)),
        "eb1": w(v["L0_ffn_b1"].reshape(E0 * FC, P).T), "eb2": w(v["L0_ffn_b2"]),
        "eW1": w(v["L0_ffn_W1"]), "eW2": w(v["L0_ffn_W2"]),
        "maskc": w(v["mask_BxS2_bk1"].reshape(B * KT, P).T).view(np.int32),
        "wq1": w(v["L1_xattn_Wq"]), "wkv1": w(v["L1_xattn_Wkv"]), "wo1": w(v["L1_xattn_Wo"]),
        "lnx_g": w(v["L1_xattn_ln_x_g"].reshape(D, 1)), "lnx_b": w(v["L1_xattn_ln_x_b"].reshape(D, 1)),
        "lnl_g": w(v["L1_xattn_ln_l_g"].reshape(D, 1)), "lnl_b": w(v["L1_xattn_ln_l_b"].reshape(D, 1)),
        "lno_g": w(v["L1_xattn_ln_o_g"].reshape(1, D)), "lno_b": w(v["L1_xattn_ln_o_b"].reshape(1, D)),
        "router_w": w(v["L1_ffn_router_w"]), "expert_bias": w(v["L1_ffn_expert_bias"].reshape(1, E1)),
        "w1": w(v["L1_ffn_w1"]), "w2": w(v["L1_ffn_w2"]), "w3": w(v["L1_ffn_w3"]),
        "sw1": w(v["L1_ffn_sw1"]), "sw2": w(v["L1_ffn_sw2"]), "sw3": w(v["L1_ffn_sw3"]),
        "tw3": w(np.broadcast_to(v["L0_xattn_w3"].reshape(64, 1), (64, P))), "tb3": w(v["L0_xattn_b3"].reshape(1, 1)),
    }
    nc = bacc.Bacc("TRN2", target_bir_lowering=False, num_devices=1)
    dram = {n: nc.dram_tensor("in_" + n, a.shape, mybir.dt.from_np(a.dtype), kind="ExternalInput").ap()
            for n, a in arrays.items()}
    out = nc.dram_tensor("out", [B * SQ, D], F32, kind="ExternalOutput").ap()
    build(nc, dram, out)
    r = run(nc, [{"in_" + n: a for n, a in arrays.items()}], core_ids=[0])
    return r.results[0]["out"].reshape(B, SQ, D)
```

```python
from contextlib import ExitStack, contextmanager

import concourse.bass as bass
from concourse import mybir

F32 = mybir.dt.float32
BF16 = mybir.dt.bfloat16
U8 = mybir.dt.uint8
I32 = mybir.dt.int32
ACT = mybir.ActivationFunctionType
ALU = mybir.AluOpType
AX = mybir.AxisListType

P = 128
B, SQ, SK, D = 8, 256, 512, 128
NT = B * SQ // P
QT, KT = SQ // P, SK // P
H0, DK = 16, 8
PAIRS = H0 // 2
ROWS = 6 * DK
MAXROWS = 3
LAG = 4
H1, DH = 8, 64
INNER = H1 * DH
NK1 = SK + SQ
KJ = NK1 // P
E0, F0 = 8, 512
FC = F0 // P
E1 = 8
LN_EPS, RMS_EPS = 1e-5, 1e-6
LOG_T_MIN, LOG_T_MAX = -2.302585092994046, 2.302585092994046
PARTS = [(0, 0), (1, 0), (2, 0), (0, 1), (0, 2), (1, 1)]


class Steps:

    def __init__(self, eng, sem):
        self.eng, self.sem, self.n, self.base = eng, sem, 0, 0

    @contextmanager
    def loop(self, start, end, step, per_turn):
        before, turns = self.n, (end - start) // step
        with self.eng.Fori(start, end, step) as i:
            self.base = (i - start) * (per_turn // step) if start else i * (per_turn // step)
            yield i
        assert self.n - before == per_turn and per_turn % step == 0, (self.n - before, per_turn)
        self.base = 0
        self.n = before + turns * per_turn

    def mark(self, ins):
        self.n += 1
        ins.then_inc(self.sem, 1)

    def wait(self):
        self.eng.wait_ge(self.sem, self.base + self.n)

    def done(self, ins):
        self.mark(ins)
        self.wait()


def layer_norm_stats(dve, steps, nc, src, tile_ids, stats, mv):
    for t in tile_ids:
        steps.mark(nc.vector.bn_stats(stats[:, t, :], src[:, t, :]))
    steps.wait()
    for t in tile_ids:
        steps.mark(nc.vector.bn_aggr(mv[:, t, :], stats[:, t, :]))
    steps.wait()


def stream_stats(dve, steps, env, tiles, ready):
    nc = env["nc"]
    for t in tiles:
        steps.mark(nc.vector.bn_stats(env["stats"][:, t, :], env["X"][:, t, :]))
    steps.wait()
    for t in tiles:
        nc.vector.bn_aggr(env["xmv"][:, t, :], env["stats"][:, t, :]).then_inc(ready, 1)


def stream_scales(pool, steps, env, t0, t1, eps, last):
    nc, r2 = env["nc"], env["rtmp2"][:, t0:t1]
    v, r1, r, mh = env["xmv"][:, t0:t1, 1], env["rtmp"][:, t0:t1], env["xr"][:, t0:t1], env["mhalf"][:, t0:t1]
    steps.done(nc.gpsimd.tensor_scalar(r1, v, LN_EPS, None, ALU.add))
    if eps is None:
        nc.gpsimd.tensor_tensor(r, r1, mh, ALU.pow).then_inc(last, 1)
        return
    steps.done(nc.gpsimd.tensor_tensor(r1, r1, mh, ALU.pow))
    steps.done(nc.gpsimd.tensor_tensor(r2, r1, r1, ALU.mult))
    steps.done(nc.gpsimd.tensor_tensor(r2, r2, v, ALU.mult))
    steps.done(nc.gpsimd.tensor_scalar(r2, r2, eps, None, ALU.add))
    steps.done(nc.gpsimd.tensor_tensor(r2, r2, mh, ALU.pow))
    nc.gpsimd.tensor_tensor(r, r1, r2, ALU.mult).then_inc(last, 1)


def stream_normed(env, t):
    return env["nc"].vector.tensor_scalar(env["Xn"][:, t, :], env["X"][:, t, :], env["xmv"][:, t, 0:1],
                                          env["xr"][:, t:t + 1], ALU.subtract, ALU.mult)


def build(nc, dram, out, upto=99):
    es = ExitStack()
    with es:
        def sb(stack, name, shape, dt=F32):
            return stack.enter_context(nc.sbuf_tensor(name, shape, dt))

        def sem(name):
            return es.enter_context(nc.semaphore(name))

        X = sb(es, "X", [P, NT, D])
        identf = sb(es, "identf", [P, P])
        identb = sb(es, "identb", [P, P], BF16)
        stats = sb(es, "stats", [P, 48, 6])
        mv = sb(es, "mv", [P, 48, 2])
        Xn = sb(es, "Xn", [P, NT, D])
        xmv = sb(es, "xmv", [P, NT, 2])
        xr = sb(es, "xr", [P, NT])
        rtmp2 = sb(es, "rtmp2", [P, NT])
        rstd = sb(es, "rstd", [P, 48])
        rtmp = sb(es, "rtmp", [P, 48])
        mhalf = sb(es, "mhalf", [P, 48])
        ps = es.enter_context(nc.psum_tensor("ps", [P, 8, 512], F32))
        env = dict(nc=nc, dram=dram, es=es, sb=sb, sem=sem, X=X, identf=identf, identb=identb, stats=stats,
                   mv=mv, rstd=rstd, rtmp=rtmp, mhalf=mhalf, ps=ps, Xn=Xn, xmv=xmv, xr=xr, rtmp2=rtmp2)
        env["W1"] = sb(es, "W1", [P, E0, F0])
        env["W2"] = sb(es, "W2", [P, E0, FC, D])
        env["w_loaded"] = sem("w_loaded")
        with ExitStack() as la:
            attention0(env, la)
        attention1_tensors(env, es)
        if upto >= 2:
            with ExitStack() as lb:
                experts0(env, lb)
        if upto >= 3:
            with ExitStack() as lc:
                attention1(env, lc)
        if upto >= 4:
            with ExitStack() as ld:
                experts1(env, ld)
        stored = sem("stored")
        with nc.Block() as block:
            @block.sync
            def _(sp):
                sp.dma_start(out.rearrange("(t p) d -> p t d", p=P), X[:, :, :]).then_inc(stored, 16)
                sp.wait_ge(stored, 16)


def attention0(env, stack):
    nc, dram, sem, X, ps = env["nc"], env["dram"], env["sem"], env["X"], env["ps"]
    identf, identb, stats, mv = env["identf"], env["identb"], env["stats"], env["mv"]
    rstd, rtmp, mhalf = env["rstd"], env["rtmp"], env["mhalf"]

    def sb(name, shape, dt=F32):
        return env["sb"](stack, name, shape, dt)

    C = 1.0 / DK ** 0.5
    Qf = sb("Qf", [P, B, SQ])
    Kf = sb("Kf", [P, B, SK])
    V = sb("V", [P, B * KT, H0, DK + 1])
    qsum, ksum = sb("qsum", [P, B]), sb("ksum", [P, B])
    sel, prodsel = sb("sel", [P, H0]), sb("prodsel", [P, B, H0])
    Qp, Kp = sb("Qp", [P, 3, SQ], BF16), sb("Kp", [P, 3, SK], BF16)
    qres, kres = sb("qres", [P, SQ]), sb("kres", [P, SK])
    Q1 = [sb(f"Q1_{i}", [P, PAIRS, SQ], BF16) for i in range(2)]
    K1 = [sb(f"K1_{i}", [P, PAIRS, SK], BF16) for i in range(2)]
    Q2 = [sb(f"Q2_{i}", [P, PAIRS, SQ], BF16) for i in range(2)]
    K2 = [sb(f"K2_{i}", [P, PAIRS, SK], BF16) for i in range(2)]
    boB = sb("boB", [P, D])
    woT = sb("woT", [P, D])
    w1c = sb("w1c", [P, 3, 64])
    w2T = sb("w2T", [64, 64])
    b1c, b2c = sb("b1c", [64, 1]), sb("b2c", [64, 1])
    w3c, b3c = sb("w3c", [64, P]), sb("b3c", [P, 1])

    Vw = [sb(f"Vw{i}", [P, KT, H0, 32]) for i in range(2)]
    parts_ready = sem("parts_ready")
    loaded = {n: sem(f"ld0_{n}") for n in ("x0", "x1", "ctx0", "ctx1", "ctx2", "ctx4", "ctx6", "wk", "wq", "wv", "ident", "consts")}
    s = {n: sem("a0_" + n) for n in (
        "stack1", "stack2", "max_rows", "s1_ready", "s1_min", "e1_ready", "e1_used", "s2_ready", "e2_ready",
        "pv_done", "v_ready", "maxp_ready", "maxp_mm", "maxp_out", "f_ready", "m1_mm", "g1", "m2_mm", "g2",
        "m3_mm", "logt_ready", "invt_ready", "t_ready", "ot_out", "ot_mm", "on_ready", "on_mm", "on_out", "wo_mm", "x_added",
        "dstep", "pstep", "x_stats", "x_scales")}
    N1, N2, NM = 24 * 16, 3 * 16, 2 * 16

    def load_stack1(sp, par, which):
        parts, stack_, x = (Kp, K1[par], 1) if which == "K" else (Qp, Q1[par], 0)
        for c, pair in enumerate(PARTS):
            for half in range(2):
                r = 64 * half + DK * c
                sp.dma_start(stack_[r:r + DK, :, :], parts[64 * half:64 * half + 64, pair[x], :]).then_inc(s["stack1"], 16)

    with ExitStack() as pro:
        def pb(name, shape, dt=F32):
            return env["sb"](pro, name, shape, dt)
        ctxT = pb("ctxT", [P, B, SK])
        Xn = env["Xn"]
        XnT = pb("XnT", [P, NT * P])
        wqT, wkT, wvT = pb("wqT", [P, D]), pb("wkT", [P, D]), pb("wvT", [P, D])
        bqc, bkc, bqn = pb("bqc", [P, 1]), pb("bkc", [P, 1]), pb("bqn", [P, 1])
        bvB = pb("bvB", [P, D])
        steps0, rs_ready, k_mm, v_mm = sem("steps0"), sem("rs_ready"), sem("k_mm"), sem("v_mm")
        xn_ready, t_mm, xt_ready, q_mm, q_out, k_out, v_out = (
            sem(n) for n in ("xn_ready", "t_mm", "xt_ready", "q_mm", "q_out", "k_out", "v_out"))
        bq_neg, pool0, mv_ready = sem("bq_neg"), sem("pool0"), sem("mv_ready")
        ones_set, steps1 = sem("ones_set"), sem("steps1")

        with nc.Block() as block:
            @block.sync
            def _(sp):
                xt = dram["x"].rearrange("(t p) d -> p t d", p=P)
                sp.dma_start(X[:, 0:QT, :], xt[:, 0:QT, :]).then_inc(loaded["x0"], 16)
                sp.dma_start(wkT[:, :], dram["wk0T"]).then_inc(loaded["wk"], 16)
                sp.dma_start(ctxT[:, 0:1, :], dram["ctxT"][:, 0:1, :]).then_inc(loaded["ctx0"], 16)
                sp.dma_start(bkc[:, :], dram["bk0"]).then_inc(loaded["wk"], 16)
                sp.dma_start(identf[:, :], dram["ident"]).then_inc(loaded["ident"], 16)
                sp.dma_start(wqT[:, :], dram["wq0T"]).then_inc(loaded["wq"], 16)
                sp.dma_start(bqc[:, :], dram["bq0"]).then_inc(loaded["wq"], 16)
                sp.dma_start(wvT[:, :], dram["wv0T"]).then_inc(loaded["wv"], 16)
                sp.dma_start(bvB[:, :], dram["bv0"].to_broadcast([P, D])).then_inc(loaded["wv"], 16)
                sp.dma_start(ctxT[:, 1:2, :], dram["ctxT"][:, 1:2, :]).then_inc(loaded["ctx1"], 16)
                sp.dma_start(X[:, QT:NT, :], xt[:, QT:NT, :]).then_inc(loaded["x1"], 16)
                for b in range(2, B, 2):
                    sp.dma_start(ctxT[:, b:b + 2, :], dram["ctxT"][:, b:b + 2, :]).then_inc(loaded[f"ctx{b}"], 16)
                sp.wait_ge(ones_set, 1)
                for n, which in enumerate("KQ"):
                    sp.wait_ge(parts_ready, n + 1)
                    load_stack1(sp, 0, which)

            @block.gpsimd
            def _(pool):
                nc.gpsimd.memset(K1[0][:, :, :], 1.0).then_inc(ones_set, 1)
                nc.gpsimd.memset(mhalf[:, :], -0.5).then_inc(pool0, 1)
                for n, (t0, t1) in enumerate(((0, QT), (QT, NT))):
                    pool.wait_ge(mv_ready, n + 1)
                    nc.gpsimd.tensor_scalar(rtmp[:, t0:t1], mv[:, t0:t1, 1], LN_EPS, None, ALU.add).then_inc(pool0, 1)
                    pool.wait_ge(pool0, n + 2)
                    nc.gpsimd.tensor_tensor(rstd[:, t0:t1], rtmp[:, t0:t1], mhalf[:, t0:t1], ALU.pow).then_inc(rs_ready, 1)
                    if n == 0:
                        for dst, src in ((boB[:, :], dram["bo0"].to_broadcast([P, D])), (woT[:, :], dram["wo0T"]), (sel[:, :], dram["sel"]),
                                         (w1c[:, 0, :], dram["tw1T"][0:1, :].to_broadcast([P, 64])),
                                         (w1c[:, 1, :], dram["tw1T"][1:2, :].to_broadcast([P, 64])),
                                         (w1c[:, 2, :], dram["tw1T"][2:3, :].to_broadcast([P, 64])),
                                         (w2T[:, :], dram["tw2T"]), (b1c[:, :], dram["tb1"]), (b2c[:, :], dram["tb2"]),
                                         (w3c[:, :], dram["tw3"]), (b3c[:, :], dram["tb3"].to_broadcast([P, 1]))):
                            pool.dma_start(dst, src).then_inc(loaded["consts"], 16)
                nc.gpsimd.memset(K1[1][:, :, :], 1.0).then_inc(ones_set, 1)
                for i in range(2):
                    nc.gpsimd.memset(Vw[i][:, :, :, :], 0.0).then_inc(ones_set, 1)

            @block.tensor
            def _(pe):
                def keys(b):
                    if b < 2 or b % 2 == 0:
                        pe.wait_ge(loaded[f"ctx{b}"], 16)
                    if b >= 2:
                        pe.wait_ge(k_out, b - 1)
                    nc.tensor.matmul(ps[:, b % 2, :], wkT[:, :], ctxT[:, b, :], start=True, stop=True).then_inc(k_mm, 1)

                def values0(b):
                    if b >= 2:
                        pe.wait_ge(v_out, b - 1)
                    for j in range(KT):
                        mm = nc.tensor.matmul(ps[:, 4 + b % 2, j * P:(j + 1) * P], ctxT[:, b, j * P:(j + 1) * P],
                                              wvT[:, :], start=True, stop=True)
                    mm.then_inc(v_mm, 1)
                pe.wait_ge(loaded["wk"], 32)
                keys(0)
                pe.wait_ge(loaded["ident"], 16)
                pe.wait_ge(xn_ready, QT)
                for i in range(QT):
                    mm = nc.tensor.transpose(ps[:, 2, i * P:(i + 1) * P], Xn[:, i, :], identf[:, :])
                mm.then_inc(t_mm, 1)
                pe.wait_ge(loaded["wq"], 32)
                pe.wait_ge(xt_ready, 1)
                nc.tensor.matmul(ps[:, 6, 0:SQ], wqT[:, :], XnT[:, 0:SQ], start=True, stop=True).then_inc(q_mm, 1)
                pe.wait_ge(loaded["wv"], 32)
                values0(0)
                for b in range(1, B):
                    keys(b)
                    values0(b)
                for g in range(4):
                    pe.wait_ge(xn_ready, 4 * (g + 1))
                    if g == 2:
                        pe.wait_ge(q_out, 1)
                    for i in range(QT if g == 0 else 0, 4):
                        mm = nc.tensor.transpose(ps[:, (2, 3, 6, 7)[g], i * P:(i + 1) * P], Xn[:, 4 * g + i, :], identf[:, :])
                    mm.then_inc(t_mm, 1)
                for g in range(4):
                    pe.wait_ge(xt_ready, g + 2)
                    if g < 2:
                        pe.wait_ge(k_out, B)
                    if g >= 2:
                        pe.wait_ge(v_out, B)
                    c0 = SQ if g == 0 else 0
                    nc.tensor.matmul(ps[:, (0, 1, 4, 5)[g], c0:512], wqT[:, :], XnT[:, g * 512 + c0:(g + 1) * 512],
                                     start=True, stop=True).then_inc(q_mm, 1)

            @block.scalar
            def _(act):
                def keys_out(b):
                    act.wait_ge(k_mm, b + 1)
                    nc.scalar.activation(Kf[:, b, :], ps[:, b % 2, :], ACT.Identity, bias=bkc[:, :],
                                         accum_out=ksum[:, b:b + 1]).then_inc(k_out, 1)

                def queries_out(b, bank, c0):
                    nc.scalar.activation(Qf[:, b, :], ps[:, bank, c0:c0 + SQ], ACT.Identity,
                                         bias=bqn[:, :], scale=-C, accum_out=qsum[:, b:b + 1]).then_inc(q_out, 1)
                act.wait_ge(loaded["wk"], 32)
                keys_out(0)
                act.wait_ge(t_mm, 1)
                nc.scalar.copy(XnT[:, 0:SQ], ps[:, 2, 0:SQ]).then_inc(xt_ready, 1)
                act.wait_ge(loaded["wq"], 32)
                nc.scalar.mul(bqn[:, :], bqc[:, :], -C).then_inc(bq_neg, 1)
                act.wait_ge(bq_neg, 1)
                act.wait_ge(q_mm, 1)
                queries_out(0, 6, 0)
                for b in range(1, B):
                    keys_out(b)
                for g in range(4):
                    act.wait_ge(t_mm, g + 2)
                    c0 = SQ if g == 0 else 0
                    nc.scalar.copy(XnT[:, g * 512 + c0:(g + 1) * 512], ps[:, (2, 3, 6, 7)[g], c0:512]).then_inc(xt_ready, 1)
                for b in range(1, B):
                    g = b // 2
                    act.wait_ge(q_mm, g + 2)
                    queries_out(b, (0, 1, 4, 5)[g], (b % 2) * SQ)

            @block.vector
            def _(dve):
                st, st2 = Steps(dve, steps0), Steps(dve, steps1)
                dve.wait_ge(loaded["x0"], 16)
                for t in range(QT):
                    st.mark(nc.vector.bn_stats(stats[:, t, :], X[:, t, :]))
                st.wait()
                for t in range(QT):
                    i = nc.vector.bn_aggr(mv[:, t, :], stats[:, t, :])
                i.then_inc(mv_ready, 1)
                dve.wait_ge(mv_ready, 1)
                dve.wait_ge(rs_ready, 1)

                def normed(t):
                    nc.vector.tensor_scalar(Xn[:, t, :], X[:, t, :], mv[:, t, 0:1], rstd[:, t:t + 1],
                                            ALU.subtract, ALU.mult).then_inc(xn_ready, 1)

                def split(full, parts, res):
                    st2.done(nc.vector.tensor_copy(parts[:, 0, :], full))
                    st2.done(nc.vector.tensor_tensor(res[:, :], full, parts[:, 0, :], ALU.subtract))
                    st2.done(nc.vector.tensor_copy(parts[:, 1, :], res[:, :]))
                    nc.vector.tensor_tensor(parts[:, 2, :], res[:, :], parts[:, 1, :], ALU.subtract).then_inc(parts_ready, 1)
                for t in range(QT):
                    normed(t)
                dve.wait_ge(k_out, 1)
                split(Kf[:, 0, :], Kp, kres)
                dve.wait_ge(q_out, 1)
                split(Qf[:, 0, :], Qp, qres)
                nc.vector.memset(V[:, :, :, DK:DK + 1], 1.0).then_inc(ones_set, 1)
                dve.wait_ge(loaded["wv"], 32)

                def v_evac(b):
                    dve.wait_ge(v_mm, b + 1)
                    nc.vector.tensor_tensor(
                        V[:, b * KT:(b + 1) * KT, :, 0:DK],
                        ps[:, 4 + b % 2, :].rearrange("p (j h d) -> p j h d", j=KT, h=H0),
                        bvB[:, :].rearrange("p (a h d) -> p a h d", a=1, h=H0).to_broadcast([P, KT, H0, DK]),
                        ALU.add).then_inc(v_out, 1)
                for b in range(2):
                    v_evac(b)
                dve.wait_ge(loaded["x1"], 16)
                for t in range(QT, NT):
                    st.mark(nc.vector.bn_stats(stats[:, t, :], X[:, t, :]))
                v_evac(2)
                st.wait()
                for t in range(QT, NT):
                    i = nc.vector.bn_aggr(mv[:, t, :], stats[:, t, :])
                i.then_inc(mv_ready, 1)
                dve.wait_ge(mv_ready, 2)
                for b in (3, 4):
                    v_evac(b)
                dve.wait_ge(rs_ready, 2)
                for t in range(QT, NT):
                    normed(t)
                    if t % 5 == 4:
                        v_evac(t // 5 + 5)
                dve.wait_ge(loaded["ident"], 16)
                nc.vector.tensor_copy(identb[:, :], identf[:, :]).then_inc(steps0, 1)
                dve.wait_ge(loaded["consts"], 16 * 11)
                dve.wait_ge(xn_ready, NT)
                nc.vector.tensor_tensor(X[:, :, :], X[:, :, :],
                                        boB[:, :].rearrange("p (a d) -> p a d", a=1).to_broadcast([P, NT, D]),
                                        ALU.add).then_inc(steps0, 1)
                for f, c in enumerate((-1.0 / (SQ * SK), -1.0 / SQ, 1.0 / (SQ * (SK - 1.0) * (SK / 2) ** 2))):
                    nc.vector.tensor_scalar(w1c[:, f, :], w1c[:, f, :], c, None, ALU.mult).then_inc(steps0, 1)
                dve.wait_ge(q_out, B)
                for b in range(B):
                    nc.vector.tensor_scalar(prodsel[:, b, :], sel[:, :], qsum[:, b:b + 1], ksum[:, b:b + 1],
                                            ALU.mult, ALU.mult).then_inc(steps0, 1)

    RB = ROWS + MAXROWS
    minv = [sb(f"minv{i}", [P, 2, PAIRS, QT]) for i in range(2)]
    bst = sb("bst", [P, H0 * QT, 6])
    e1 = [sb(f"e1_{i}", [P, QT, SK]) for i in range(4)]
    e2 = [sb(f"e2_{i}", [P, KT, SQ]) for i in range(2)]
    maxp = sb("maxp", [P, 2, MAXROWS, PAIRS, QT], BF16)
    maxres = sb("maxres", [P, 2, PAIRS * QT])
    NROW = 2 * MAXROWS * PAIRS * QT
    maxpT = sb("maxpT", [NROW, P], BF16)
    vs = [sb(f"vs{i}", [P, H0 * QT]) for i in range(8)]
    h1, h2 = sb("h1", [64, H0]), sb("h2", [64, H0])
    logt, invt = sb("logt", [P, H0]), sb("invt", [P, H0])
    tscale = [sb(f"tscale{i}", [P, H0]) for i in range(2)]
    OT = [sb(f"OT{i}", [P, 2 * SQ]) for i in range(2)]
    rz = sb("rz", [P, 2, QT, 4])
    On = sb("On", [P, QT, D])
    OnT = sb("OnT", [P, QT * P])

    S1_BANKS, S2_BANK, O_BANK, M_BANK = (0, 2), 4, 6, 7
    def at(k, n):
        return k >= n if isinstance(k, int) else True

    def is_last(k):
        return isinstance(k, int) and k == B - 1

    def has(k, g):
        return at(k, 1) and not (isinstance(k, int) and k > B) if g >= 0 else at(k, 2)

    def buf(par, g):
        return 1 - par if g >= 0 else par

    def sync_step(sp, k, par):
        if at(k, 2):
            sp.wait_ge(s["s2_ready"], (k - 1) * H0)
        if at(k, 1):
            sp.wait_ge(s["stack2"], k * N2)
        sp.wait_ge(s["stack1"], (k + 1) * N1)
        sp.dma_start(K2[par][:, :, :], K1[par][:, :, :]).then_inc(s["stack2"], 16)
        for half in range(2):
            r = slice(64 * half, 64 * half + ROWS)
            sp.dma_start(Q2[par][r, :, :], Q1[par][r, :, :]).then_inc(s["stack2"], 16)
        if not is_last(k):
            sp.wait_ge(parts_ready, 2 * (k + 2))
            if at(k, 1):
                sp.wait_ge(s["s1_ready"], k * H0)
            for which in ("K", "Q"):
                load_stack1(sp, 1 - par, which)
        sp.wait_ge(s["maxp_out"], k + 1)
        for half in range(2):
            sp.dma_start(Q2[par][64 * half + ROWS:64 * half + RB, :, :],
                         maxpT[half * NROW // 2:(half + 1) * NROW // 2, :]).then_inc(s["max_rows"], 16)

    def gpsimd_step(pool, st, k, par):
        if not is_last(k):
            pool.wait_ge(s["stack1"], (k + 1) * N1)
            for full, parts, res in ((Kf, Kp, kres), (Qf, Qp, qres)):
                src = full[:, k + 1, :]
                st.done(nc.gpsimd.tensor_copy(parts[:, 0, :], src))
                st.done(nc.gpsimd.tensor_tensor(res[:, :], src, parts[:, 0, :], ALU.subtract))
                st.done(nc.gpsimd.tensor_copy(parts[:, 1, :], res[:, :]))
                nc.gpsimd.tensor_tensor(parts[:, 2, :], res[:, :], parts[:, 1, :], ALU.subtract).then_inc(parts_ready, 1)
        if at(k, 2):
            pool.wait_ge(s["pv_done"], (k - 1) * H0)
        nc.gpsimd.tensor_copy(Vw[par][:, :, :, 0:DK + 1].rearrange("p j h c -> p (j h) c"),
                              V[:, k * KT:(k + 1) * KT, :, :].rearrange("p j h c -> p (j h) c")).then_inc(s["v_ready"], 1)

    def tensor_step(pe, k, par):
        first, temper = not (isinstance(k, int) and k >= B), has(k, 0)
        if isinstance(k, int) and k == 0:
            score1(pe, 0, par, 0)
        for h in range(LAG + 1 if isinstance(k, int) and k > B else H0):
            g = h - LAG
            if first and h + 1 < H0:
                score1(pe, k, par, h + 1)
            if first and h + 1 == H0 and not is_last(k):
                score1(pe, k + 1, 1 - par, 0)
            if temper and h == 0:
                maxima_transpose(pe, k)
            if temper and h == 1:
                temperature_mm1(pe, k, par)
            if has(k, g):
                score2(pe, k, par, g)
            if temper and h == 2:
                temperature_mm2(pe, k)
            if has(k, g - 1):
                values(pe, k, par, g - 1)
            if temper and h == 2:
                temperature_mm3(pe, k)
            if at(k, 2) and h == LAG + 2:
                output_transpose(pe, k, 1)
            if at(k, 2) and h == LAG + 4:
                normed_transpose(pe, k)
            if at(k, 2) and h == LAG + 6:
                project_mm(pe, k)
            if temper and h == LAG + 10:
                output_transpose(pe, k, 0)

    def maxima_transpose(pe, k):
        pe.wait_ge(s["maxp_ready"], k)
        if at(k, 2):
            pe.wait_ge(s["on_ready"], 2 * k - 3)
        nc.tensor.transpose(ps[0:NROW, M_BANK, 0:64].bitcast(BF16),
                            maxp[:, :, :, :, :].rearrange("p a b c d -> p (a b c d)"),
                            identb[:, :]).then_inc(s["maxp_mm"], 1)

    def score1(pe, k, par, h):
        base, pair = 64 * (h % 2), h // 2
        if h == 0:
            pe.wait_ge(s["stack1"], (k + 1) * N1)
        if h >= 2 or at(k, 1):
            pe.wait_ge(s["e1_ready"], k * H0 + h - 1)
        for q in range(QT):
            mm = nc.tensor.matmul(ps[:, S1_BANKS[h % 2] + q, :], Q1[par][base:base + ROWS, pair, q * P:(q + 1) * P],
                                  K1[par][base:base + ROWS, pair, :], start=True, stop=True)
        mm.then_inc(s["s1_ready"], 1)

    def score2(pe, k, par, g):
        base, pair = 64 * (g % 2), g % H0 // 2
        if g == 0:
            pe.wait_ge(s["stack2"], k * N2)
            pe.wait_ge(s["max_rows"], k * NM)
        if g >= 1 or at(k, 2):
            pe.wait_ge(s["e2_ready"], (k - 1) * H0 + g)
        for j in range(KT):
            mm = nc.tensor.matmul(ps[:, S2_BANK + j // 2, (j % 2) * SQ:(j % 2 + 1) * SQ],
                                  K2[buf(par, g)][base:base + RB, pair, j * P:(j + 1) * P],
                                  Q2[buf(par, g)][base:base + RB, pair, :], start=True, stop=True)
        mm.then_inc(s["s2_ready"], 1)

    def values(pe, k, par, g):
        pe.wait_ge(s["e2_ready"], (k - 1) * H0 + g + 1)
        if g == 0:
            pe.wait_ge(s["v_ready"], k)
        if g % 8 == 0 and (g or at(k, 2)):
            pe.wait_ge(s["ot_out"], 2 * (k - 1) + g // 8)
        r, c = 32 * (g % 4), (g // 4) % 2 * SQ
        for j in range(KT):
            mm = nc.tensor.matmul(ps[r:r + 32, O_BANK, c:c + SQ], Vw[buf(par, g)][:, j, g % H0, :], e2[g % 2][:, j, :],
                                  start=(j == 0), stop=(j == KT - 1))
        mm.then_inc(s["pv_done"], 1)

    def temperature_mm1(pe, k, par):
        pe.wait_ge(s["f_ready"], k)
        pe.wait_ge(s["maxp_out"], k)
        o = ps[0:64, M_BANK, 64:64 + H0]
        fmin = minv[1 - par][:, :, :, :].rearrange("p a b q -> p (a b) q")
        fvar = vs[7][:, :].rearrange("p (u q) -> p u q", q=QT)
        nc.tensor.matmul(o, w1c[:, 0, :], prodsel[:, k - 1, :] if isinstance(k, int) else
                         prodsel[:, bass.ds(k - 1, 1), :].rearrange("p a h -> p (a h)"), start=True, stop=False)
        for q in range(QT):
            nc.tensor.matmul(o, w1c[:, 1, :], fmin[:, :, q], start=False, stop=False)
            mm = nc.tensor.matmul(o, w1c[:, 2, :], fvar[:, :, q], start=False, stop=(q == QT - 1))
        mm.then_inc(s["m1_mm"], 1)

    def temperature_mm2(pe, k):
        pe.wait_ge(loaded["consts"], 16 * 11)
        pe.wait_ge(s["g1"], k)
        nc.tensor.matmul(ps[0:64, M_BANK, 96:96 + H0], w2T[:, :], h1[:, :], start=True, stop=True).then_inc(s["m2_mm"], 1)

    def temperature_mm3(pe, k):
        pe.wait_ge(loaded["consts"], 16 * 11)
        pe.wait_ge(s["g2"], k)
        nc.tensor.matmul(ps[:, M_BANK, 128:128 + H0], w3c[:, :], h2[:, :], start=True, stop=True).then_inc(s["m3_mm"], 1)

    def output_transpose(pe, k, half):
        pe.wait_ge(s["ot_out"], 2 * k - 1 - half)
        if half and isinstance(k, int) and k > B:
            pe.wait_ge(s["on_ready"], 2 * k - 3)
        elif half or not at(k, 2):
            pe.wait_ge(s["logt_ready"], k)
        else:
            pe.wait_ge(s["x_added"], k - 1)
        for i in range(4):
            mm = nc.tensor.transpose(ps[:, M_BANK, i * P:(i + 1) * P], OT[half][:, i * P:(i + 1) * P], identf[:, :])
        mm.then_inc(s["ot_mm"], 1)

    def normed_transpose(pe, k):
        pe.wait_ge(s["on_ready"], 2 * (k - 1))
        for q in range(QT):
            mm = nc.tensor.transpose(ps[:, M_BANK, q * P:(q + 1) * P], On[:, q, :], identf[:, :])
        mm.then_inc(s["on_mm"], 1)

    def project_mm(pe, k):
        pe.wait_ge(s["on_out"], k - 1)
        for q in range(QT):
            mm = nc.tensor.matmul(ps[:, M_BANK, q * P:(q + 1) * P], OnT[:, q * P:(q + 1) * P], woT[:, :],
                                  start=True, stop=True)
        mm.then_inc(s["wo_mm"], 1)

    def output_evac(act, k, half):
        act.wait_ge(s["pv_done"], (k - 1) * H0 + (0 if half else 8))
        if at(k, 2 + half):
            act.wait_ge(s["ot_mm"], 2 * k - 3 - half)
        nc.scalar.copy(OT[half][:, :], ps[:, O_BANK, :]).then_inc(s["ot_out"], 1)

    def scalar_step(act, k, par):
        first, temper = not (isinstance(k, int) and k >= B), has(k, 0)
        for h in range(LAG + 1 if isinstance(k, int) and k > B else H0):
            g = h - LAG
            if first:
                act.wait_ge(s["s1_min"], k * H0 + h + 1)
                if h >= 4 or at(k, 1):
                    act.wait_ge(s["e1_used"], k * H0 + h - 3)
                for q in range(QT):
                    a = nc.scalar.activation(e1[h % 4][:, q, :], ps[:, S1_BANKS[h % 2] + q, :], ACT.Exp, scale=-1.0,
                                             bias=minv[par][:, h % 2, h // 2, q:q + 1])
                a.then_inc(s["e1_ready"], 1)
            if temper and h == 0:
                act.wait_ge(s["maxp_mm"], k)
                if at(k, 2):
                    act.wait_ge(s["max_rows"], (k - 1) * NM)
                nc.scalar.copy(maxpT[:, :], ps[0:NROW, M_BANK, 0:64].bitcast(BF16)).then_inc(s["maxp_out"], 1)
            if at(k, 2) and h == LAG + 1:
                output_evac(act, k, 1)
            if temper and h == LAG + 9:
                output_evac(act, k, 0)
            if temper and h == LAG - 1:
                act.wait_ge(s["logt_ready"], k)
                nc.scalar.activation(invt[:, :], logt[:, :], ACT.Exp, scale=-1.0).then_inc(s["invt_ready"], 1)
            if has(k, g):
                act.wait_ge(s["s2_ready"], (k - 1) * H0 + g + 1)
                if g >= 2 or at(k, 2):
                    act.wait_ge(s["pv_done"], (k - 1) * H0 + g - 1)
                if g == 0:
                    act.wait_ge(s["t_ready"], k)
                c = (g % 2) * PAIRS + g % H0 // 2
                nc.scalar.activation(e2[g % 2][:, :, :].rearrange("p j q -> p (j q)"),
                                     ps[:, S2_BANK:S2_BANK + 2, :].rearrange("p a b -> p (a b)"), ACT.Exp,
                                     scale=tscale[buf(par, g)][:, c:c + 1]).then_inc(s["e2_ready"], 1)
            if temper and h == 1:
                act.wait_ge(s["m1_mm"], k)
                nc.scalar.activation(h1[:, :], ps[0:64, M_BANK, 64:64 + H0], ACT.Gelu, bias=b1c[:, :]).then_inc(s["g1"], 1)
                act.wait_ge(s["m2_mm"], k)
                nc.scalar.activation(h2[:, :], ps[0:64, M_BANK, 96:96 + H0], ACT.Gelu, bias=b2c[:, :]).then_inc(s["g2"], 1)

    def vector_step(dve, st, k, par):
        first, temper = not (isinstance(k, int) and k >= B), has(k, 0)
        if isinstance(k, int) and k == 0:
            row_min(dve, k, par, 0)
        for h in range(H0):
            if first and h + 1 < H0:
                row_min(dve, k, par, h + 1)
            if first and h + 1 == H0:
                if not is_last(k):
                    row_min(dve, k + 1, 1 - par, 0)
                max_parts(dve, st, k, par)
            if first:
                dve.wait_ge(s["e1_ready"], k * H0 + h + 1)
                for q in range(QT):
                    i = nc.vector.bn_stats(bst[:, ((h % 2) * PAIRS + h // 2) * QT + q, :], e1[h % 4][:, q, :])
                i.then_inc(s["e1_used"], 1)
            if temper and h == LAG - 2:
                dve.wait_ge(s["m3_mm"], k)
                st.done(nc.vector.tensor_scalar(logt[:, :], ps[:, M_BANK, 128:128 + H0], b3c[:, :], LOG_T_MIN, ALU.add, ALU.max))
                nc.vector.tensor_scalar(logt[:, :], logt[:, :], LOG_T_MAX, None, ALU.min).then_inc(s["logt_ready"], 1)
            if temper and h == LAG - 1:
                dve.wait_ge(s["invt_ready"], k)
                nc.vector.tensor_scalar(tscale[1 - par][:, :], invt[:, :], -(DK ** 0.5) / 2.0, None, ALU.mult).then_inc(s["t_ready"], 1)
            if at(k, 2) and h == LAG + 3:
                output_norm(dve, st, k, 1)
            if at(k, 2) and h == LAG + 5:
                normed_copy(dve, k)
            if at(k, 2) and h == LAG + 7:
                output_add(dve, k)
            if temper and h == LAG + 10:
                output_norm(dve, st, k, 0)
        if first:
            variances(dve, st, k)

    def row_min(dve, k, par, h):
        dve.wait_ge(s["s1_ready"], k * H0 + h + 1)
        nc.vector.tensor_reduce(minv[par][:, h % 2, h // 2, :], ps[:, S1_BANKS[h % 2]:S1_BANKS[h % 2] + QT, :], AX.X,
                                ALU.min).then_inc(s["s1_min"], 1)

    def max_parts(dve, st, k, par):
        dve.wait_ge(s["s1_min"], (k + 1) * H0)
        m = [minv[par][:, a, :, :].rearrange("p c q -> p (c q)") for a in range(2)]
        part = [[maxp[:, a, i, :, :].rearrange("p c q -> p (c q)") for i in range(3)] for a in range(2)]
        for a in range(2):
            st.mark(nc.vector.tensor_scalar(part[a][0], m[a], -1.0, None, ALU.mult))
        st.wait()
        for a in range(2):
            st.mark(nc.vector.scalar_tensor_tensor(maxres[:, a, :], m[a], -1.0, part[a][0], ALU.mult, ALU.subtract))
        st.wait()
        for a in range(2):
            st.mark(nc.vector.tensor_copy(part[a][1], maxres[:, a, :]))
        st.wait()
        for a in range(2):
            i = nc.vector.tensor_tensor(part[a][2], maxres[:, a, :], part[a][1], ALU.subtract)
        i.then_inc(s["maxp_ready"], 1)

    def variances(dve, st, k):
        dve.wait_ge(s["e1_used"], (k + 1) * H0)
        m, d, m2, dd, r, r2, v, f = (x[:, :] for x in vs)
        st.mark(nc.vector.tensor_tensor(m, bst[:, :, 1], bst[:, :, 4], ALU.add))
        st.mark(nc.vector.tensor_tensor(d, bst[:, :, 1], bst[:, :, 4], ALU.subtract))
        st.mark(nc.vector.tensor_tensor(m2, bst[:, :, 2], bst[:, :, 5], ALU.add))
        st.wait()
        st.mark(nc.vector.tensor_tensor(dd, d, d, ALU.mult))
        st.mark(nc.vector.reciprocal(r, m))
        st.wait()
        st.mark(nc.vector.scalar_tensor_tensor(v, dd, SK / 4.0, m2, ALU.mult, ALU.add))
        st.mark(nc.vector.tensor_tensor(r2, r, r, ALU.mult))
        st.wait()
        nc.vector.tensor_tensor(f, v, r2, ALU.mult).then_inc(s["f_ready"], 1)

    def output_norm(dve, st, k, half):
        dve.wait_ge(s["ot_mm"], 2 * k - 1 - half)
        o = ps[:, M_BANK, :].rearrange("p (c q h r) -> p c q h r", c=2, q=QT, h=4)
        for q in range(QT):
            st.mark(nc.vector.reciprocal(rz[:, :, q, :], o[:, :, q, :, DK]))
        st.wait()
        if half == 0 and at(k, 2):
            dve.wait_ge(s["on_mm"], k - 1)
        for q in range(QT):
            i = nc.vector.tensor_tensor(
                On[:, q, half * 64:half * 64 + 64].rearrange("p (c h d) -> p c h d", c=2, h=4), o[:, :, q, :, 0:DK],
                rz[:, :, q, :].rearrange("p c (h a) -> p c h a", a=1).to_broadcast([P, 2, 4, DK]), ALU.mult)
        i.then_inc(s["on_ready"], 1)

    def normed_copy(dve, k):
        dve.wait_ge(s["on_mm"], k - 1)
        nc.vector.tensor_copy(OnT[:, :], ps[:, M_BANK, 0:QT * P]).then_inc(s["on_out"], 1)

    def output_add(dve, k):
        dve.wait_ge(s["wo_mm"], k - 1)
        xs = X[:, bass.ds((k - 2) * QT, QT), :]
        nc.vector.tensor_tensor(xs, xs, ps[:, M_BANK, 0:QT * P].rearrange("p (q d) -> p q d", q=QT),
                                ALU.add).then_inc(s["x_added"], 1)

    with nc.Block() as block:
        @block.sync
        def _(sp):
            sp.dma_start(env["W1"][:, :, :], dram["eW1"].rearrange("e d f -> d e f")).then_inc(env["w_loaded"], 16)
            sp.dma_start(env["W2"][:, :, :, :].rearrange("p e c d -> p (e c) d"),
                         dram["eW2"].rearrange("e (c p) d -> p (e c) d", p=P)).then_inc(env["w_loaded"], 16)
            for k in range(B):
                sync_step(sp, k, k % 2)

        @block.gpsimd
        def _(pool):
            st = Steps(pool, s["pstep"])
            for k in range(B):
                gpsimd_step(pool, st, k, k % 2)
            pool.wait_ge(s["x_stats"], NT - QT)
            stream_scales(pool, st, env, 0, NT - QT, RMS_EPS, s["x_scales"])
            pool.wait_ge(s["x_stats"], NT)
            stream_scales(pool, st, env, NT - QT, NT, RMS_EPS, s["x_scales"])

        @block.tensor
        def _(pe):
            for k in (0, 1):
                tensor_step(pe, k, k % 2)
            with pe.Fori(2, B - 2, 2) as i:
                tensor_step(pe, i, 0)
                tensor_step(pe, i + 1, 1)
            for k in (B - 2, B - 1, B):
                tensor_step(pe, k, k % 2)
            tensor_step(pe, B + 1, (B + 1) % 2)
            output_transpose(pe, B + 1, 1)
            normed_transpose(pe, B + 1)
            project_mm(pe, B + 1)

        @block.scalar
        def _(act):
            for k in (0, 1):
                scalar_step(act, k, k % 2)
            with act.Fori(2, B - 2, 2) as i:
                scalar_step(act, i, 0)
                scalar_step(act, i + 1, 1)
            for k in (B - 2, B - 1, B):
                scalar_step(act, k, k % 2)
            scalar_step(act, B + 1, (B + 1) % 2)
            output_evac(act, B + 1, 1)

        @block.vector
        def _(dve):
            st = Steps(dve, s["dstep"])
            for k in (0, 1):
                vector_step(dve, st, k, k % 2)
            with st.loop(2, B - 2, 2, 2 * 18) as i:
                vector_step(dve, st, i, 0)
                vector_step(dve, st, i + 1, 1)
            for k in (B - 2, B - 1, B):
                vector_step(dve, st, k, k % 2)
            dve.wait_ge(s["x_added"], B - 1)
            stream_stats(dve, st, env, range(NT - QT), s["x_stats"])
            output_norm(dve, st, B + 1, 1)
            normed_copy(dve, B + 1)
            dve.wait_ge(s["x_scales"], 1)
            for t in range(NT - QT):
                stream_normed(env, t)
            output_add(dve, B + 1)
            dve.wait_ge(s["x_added"], B)
            stream_stats(dve, st, env, range(NT - QT, NT), s["x_stats"])
            dve.wait_ge(s["x_scales"], 2)
            for t in range(NT - QT, NT):
                stream_normed(env, t)


def experts0(env, stack):
    nc, dram, sem, X, ps = env["nc"], env["dram"], env["sem"], env["X"], env["ps"]
    identf, stats, mv, rstd, rtmp, mhalf = (env[n] for n in ("identf", "stats", "mv", "rstd", "rtmp", "mhalf"))
    c = env["c"]

    def sb(name, shape, dt=F32):
        return env["sb"](stack, name, shape, dt)

    W1, W2 = env["W1"], env["W2"]
    b1t = sb("b1t", [P, E0 * FC])
    b2t = sb("b2t", [E0, D])
    rmsw = sb("rmsw", [P, 1])
    gwT = sb("gwT", [P, E0])
    rank = sb("rank", [P, E0])
    Xn = env["Xn"]
    XnT = sb("XnTB", [P, NT * P])
    L, ex, key, G = (sb(n, [P, NT, E0]) for n in ("LB", "exB", "keyB", "GB"))
    mx, den, kmx = (sb(n, [P, NT]) for n in ("mxB", "denB", "kmxB"))
    GT = sb("GTB", [E0, NT * P])
    hT = [sb(f"hTB{i}", [P, 512]) for i in range(8)]
    s = {n: sem("b_" + n) for n in (
        "small", "bias_added", "steps", "psteps", "t_mm", "xt", "l_mm", "l_out", "shifted", "exps",
        "gates", "gt_mm", "gt_out", "bias_mm", "h_mm", "h_out", "y_mm", "y_added", "c_stats", "c_scales", "c_norm", "c_mm",
        "c_out", "x_stats", "x_scales", "inv", "wo_cleared")}

    HB, YB, GB_BANK, BB_BANK = 0, 4, 6, 7

    def load_layer1(sp):
        d = env["d"]
        sp.dma_start(c["CN"][:, :, :], dram["ctx"].rearrange("(t p) d -> p t d", p=P)).then_inc(c["loaded_ctx"], 16)
        for n, m in (("gx", "lnx_g"), ("bx", "lnx_b"), ("gl", "lnl_g"), ("bl", "lnl_b")):
            sp.dma_start(c[n][:, :], dram[m]).then_inc(c["loaded_norm"], 16)
        sp.dma_start(c["maskB"][:, :], dram["mask"].to_broadcast([P, B * SK // 4])).then_inc(c["loaded_mask"], 16)
        sp.dma_start(c["maskc"][:, :], dram["maskc"]).then_inc(c["loaded_mask"], 16)
        for n, m in (("wq", "wq1"), ("wkv", "wkv1")):
            sp.dma_start(c[n][:, :], dram[m]).then_inc(c["loaded_w"], 16)
        for n, m in (("gout", "lno_g"), ("bout", "lno_b")):
            sp.dma_start(c[n][:, :], dram[m].to_broadcast([P, D])).then_inc(c["loaded_w"], 16)
        for t, n in ((d["rw"], "router_w"), (d["rank"], "rank")):
            sp.dma_start(t[:, :], dram[n]).then_inc(d["loaded_small"], 16)
        sp.dma_start(d["biasB"][:, :], dram["expert_bias"].to_broadcast([P, E1])).then_inc(d["loaded_small"], 16)
        for n in ("w1", "w3", "w2"):
            sp.dma_start(d[n][:, 0:E1, :], dram[n].rearrange("e d f -> d e f")).then_inc(d["loaded_w"], 16)
            sp.dma_start(d[n][:, E1, :], dram["s" + n]).then_inc(d["loaded_w"], 16)
        sp.wait_ge(s["wo_cleared"], 1)
        sp.dma_start(c["wo"][0:DH, :, 0:D], dram["wo1"].rearrange("(h p) d -> p h d", p=DH)).then_inc(c["loaded_w"], 16)

    def over_experts(a):
        return a[:, :].rearrange("p (t a) -> p t a", a=1).to_broadcast([P, NT, E0])

    with nc.Block() as block:
        @block.sync
        def _(sp):
            for t, n in ((rmsw, "rms_w"), (gwT, "gate_wT"), (rank, "rank"), (b1t, "eb1"), (b2t, "eb2")):
                sp.dma_start(t[:, :], dram[n]).then_inc(s["small"], 16)
            load_layer1(sp)

        @block.tensor
        def _(pe):
            for g in range(4):
                for i in range(4):
                    mm = nc.tensor.transpose(ps[:, g, i * P:(i + 1) * P], Xn[:, 4 * g + i, :], identf[:, :])
                mm.then_inc(s["t_mm"], 1)
            pe.wait_ge(s["small"], 16 * 5)
            for t in range(NT):
                if t % 4 == 0:
                    pe.wait_ge(s["xt"], t // 4 + 1)
                mm = nc.tensor.matmul(ps[:, 4, t * E0:(t + 1) * E0], XnT[:, t * P:(t + 1) * P], gwT[:, :], start=True, stop=True)
            mm.then_inc(s["l_mm"], 1)
            pe.wait_ge(env["w_loaded"], 32)

            def gates_transpose(i):
                pe.wait_ge(s["gates"], 1)
                for t in range(4):
                    mm = nc.tensor.transpose(ps[0:E0, GB_BANK, t * P:(t + 1) * P], G[:, 4 * i + t, :], identf[:, :])
                mm.then_inc(s["gt_mm"], 1)

            def bias_mm(i):
                pe.wait_ge(s["gt_out"], i + 1)
                if i:
                    pe.wait_ge(s["bias_added"], i)
                for t in range(4):
                    mm = nc.tensor.matmul(ps[:, BB_BANK, t * P:(t + 1) * P], GT[:, (4 * i + t) * P:(4 * i + t + 1) * P], b2t[:, :],
                                          start=True, stop=True)
                mm.then_inc(s["bias_mm"], 1)

            def up(g, e):
                for f in range(FC):
                    n = g * (E0 * FC) + e * FC + f
                    if not (isinstance(g, int) and g == 0 and e == 0):
                        pe.wait_ge(s["h_out"], n - FC + 1)
                    nc.tensor.matmul(ps[:, HB + f, :], W1[:, e, f * P:(f + 1) * P], XnT[:, bass.ds(g * 512, 512)],
                                     start=True, stop=True).then_inc(s["h_mm"], 1)

            def down(g, e):
                pe.wait_ge(s["h_out"], g * (E0 * FC) + e * FC + FC)
                if not (isinstance(g, int) and g == 0 and e < 2):
                    pe.wait_ge(s["y_added"], g * E0 + e - 1)
                elif e == 0:
                    pe.wait_ge(s["l_out"], 1)
                for t in range(4):
                    for f in range(FC):
                        mm = nc.tensor.matmul(ps[:, YB + e % 2, t * P:(t + 1) * P], hT[(e % 2) * FC + f][:, t * P:(t + 1) * P],
                                              W2[:, e, f, :], start=(f == 0), stop=(f == FC - 1))
                mm.then_inc(s["y_mm"], 1)

            def group(g, context=False):
                up(g, 0)
                for e in range(E0):
                    if e + 1 < E0:
                        up(g, e + 1)
                    down(g, e)
                    if isinstance(g, int) and g == 0:
                        if 3 <= e < 7:
                            bias_mm(e - 3)
                        if 2 <= e < 6:
                            gates_transpose(e - 2)
                    if context:
                        pe.wait_ge(s["c_norm"], KT * (e + 1))
                        if e >= 2:
                            pe.wait_ge(s["c_out"], e - 1)
                        for j in range(KT):
                            mm = nc.tensor.transpose(ps[:, 6 + e % 2, j * P:(j + 1) * P], c["CN"][:, KT * e + j, :], identf[:, :])
                        mm.then_inc(s["c_mm"], 1)
            group(0)
            with pe.Fori(1, 3) as g:
                group(g)
            group(3, context=True)

        @block.scalar
        def _(act):
            act.wait_ge(s["small"], 16 * 5)
            for g in range(4):
                act.wait_ge(s["t_mm"], g + 1)
                nc.scalar.activation(XnT[:, g * 512:(g + 1) * 512], ps[:, g, :], ACT.Identity, scale=rmsw[:, :]).then_inc(s["xt"], 1)
            act.wait_ge(s["shifted"], 1)
            nc.scalar.activation(ex[:, :, :], ex[:, :, :], ACT.Exp).then_inc(s["exps"], 1)

            def context_out(b):
                act.wait_ge(s["c_mm"], b + 1)
                nc.scalar.activation(c["LT"][:, b, 0:SK], ps[:, 6 + b % 2, :], ACT.Identity, scale=c["gx"][:, :],
                                     bias=c["bx"][:, :]).then_inc(s["c_out"], 1)

            def group(g, context=False):
                for e in range(E0):
                    for f in range(FC):
                        act.wait_ge(s["h_mm"], g * (E0 * FC) + e * FC + f + 1)
                        if f == 0 and not (isinstance(g, int) and g == 0 and e < 2):
                            act.wait_ge(s["y_mm"], g * E0 + e - 1)
                        nc.scalar.activation(hT[(e % 2) * FC + f][:, :], ps[:, HB + f, :], ACT.Silu,
                                             bias=b1t[:, e * FC + f:e * FC + f + 1]).then_inc(s["h_out"], 1)
                    if isinstance(g, int) and g == 0 and 3 <= e < 7:
                        act.wait_ge(s["gt_mm"], e - 2)
                        nc.scalar.copy(GT[:, (e - 3) * 512:(e - 2) * 512], ps[0:E0, GB_BANK, :]).then_inc(s["gt_out"], 1)
                    if context and e:
                        context_out(e - 1)
            group(0)
            with act.Fori(1, 3) as g:
                group(g)
            act.wait_ge(c["loaded_norm"], 16 * 4)
            group(3, context=True)
            context_out(B - 1)

        @block.vector
        def _(dve):
            st = Steps(dve, s["steps"])
            rk = rank[:, :].rearrange("p (a e) -> p a e", a=1).to_broadcast([P, NT, E0])
            dve.wait_ge(s["l_mm"], 1)
            nc.vector.tensor_copy(L[:, :, :].rearrange("p t e -> p (t e)"), ps[:, 4, 0:NT * E0]).then_inc(s["l_out"], 1)
            dve.wait_ge(s["l_out"], 1)
            st.done(nc.vector.tensor_reduce(mx[:, :], L[:, :, :], AX.X, ALU.max))
            nc.vector.tensor_tensor(ex[:, :, :], L[:, :, :], over_experts(mx), ALU.subtract).then_inc(s["shifted"], 1)
            dve.wait_ge(s["small"], 16 * 5)
            st.done(nc.vector.tensor_tensor(key[:, :, :], L[:, :, :], over_experts(mx), ALU.is_equal))
            st.done(nc.vector.tensor_tensor(key[:, :, :], key[:, :, :], rk, ALU.mult))
            st.done(nc.vector.tensor_reduce(kmx[:, :], key[:, :, :], AX.X, ALU.max))
            st.done(nc.vector.tensor_tensor(key[:, :, :], key[:, :, :], over_experts(kmx), ALU.is_equal))
            dve.wait_ge(s["exps"], 1)
            st.done(nc.vector.tensor_reduce(den[:, :], ex[:, :, :], AX.X, ALU.add))
            st.done(nc.vector.reciprocal(den[:, :], den[:, :]))
            nc.vector.tensor_tensor(G[:, :, :], key[:, :, :], over_experts(den), ALU.mult).then_inc(s["gates"], 1)
            dve.wait_ge(s["gates"], 1)

            def group(g):
                for e in range(E0):
                    if g == 1:
                        tiles = range(KT * e, KT * (e + 1))
                        for t in tiles:
                            st.mark(nc.vector.bn_stats(stats[:, NT + t, :], c["CN"][:, t, :]))
                        st.wait()
                        for t in tiles:
                            nc.vector.bn_aggr(mv[:, t, :], stats[:, NT + t, :]).then_inc(s["c_stats"], 1)
                    if g == 3:
                        for t in range(KT * e, KT * (e + 1)):
                            nc.vector.tensor_scalar(c["CN"][:, t, :], c["CN"][:, t, :], mv[:, t, 0:1], rstd[:, t:t + 1],
                                                    ALU.subtract, ALU.mult).then_inc(s["c_norm"], 1)
                    dve.wait_ge(s["y_mm"], g * E0 + e + 1)
                    if g or e:
                        dve.wait_ge(s["y_added"], g * E0 + e)
                    if (g, e) in ((0, 4), (1, 0)):
                        dve.wait_ge(s["bias_added"], 1 if g == 0 else 4)
                    for t in range(4):
                        x = X[:, 4 * g + t, :]
                        i = nc.vector.scalar_tensor_tensor(x, ps[:, YB + e % 2, t * P:(t + 1) * P], G[:, 4 * g + t, e:e + 1], x,
                                                           ALU.mult, ALU.add)
                    i.then_inc(s["y_added"], 1)
                    if g == 0 and 3 <= e < 7:
                        b = e - 3
                        dve.wait_ge(s["bias_mm"], b + 1)
                        dve.wait_ge(s["y_added"], e + 1)
                        nc.vector.tensor_tensor(X[:, 4 * b:4 * b + 4, :], X[:, 4 * b:4 * b + 4, :],
                                                ps[:, BB_BANK, :].rearrange("p (t d) -> p t d", t=4), ALU.add).then_inc(s["bias_added"], 1)

            def tail(g):
                dve.wait_ge(s["y_added"], (g + 1) * E0)
                stream_stats(dve, st, env, range(4 * g, 4 * g + 4), s["x_stats"])
            for g in range(4):
                if g == 1:
                    dve.wait_ge(c["loaded_ctx"], 16)
                if g == 2:
                    dve.wait_ge(c["loaded_mask"], 32)
                    nc.vector.tensor_scalar(c["invB"][:, :], c["maskB"][:, :].bitcast(U8), 0.0, None, ALU.is_equal).then_inc(s["inv"], 1)
                if g == 3:
                    dve.wait_ge(s["c_scales"], 1)
                group(g)
                tail(g)

        @block.gpsimd
        def _(pool):
            st = Steps(pool, s["psteps"])
            wo = c["wo"]
            st.done(nc.gpsimd.memset(wo[:, :, :], 0.0))
            nc.gpsimd.memset(wo[DH:DH + 1, :, D:D + 1], 1.0).then_inc(s["wo_cleared"], 1)
            pool.wait_ge(s["wo_cleared"], 1)
            pool.wait_ge(c["loaded_mask"], 32)
            st.done(nc.gpsimd.tensor_scalar(c["mask01"][:, :], c["maskc"][:, :].bitcast(U8), 0.0, None, ALU.add))
            for g in range(4):
                pool.wait_ge(s["x_stats"], 4 * (g + 1))
                stream_scales(pool, st, env, 4 * g, 4 * (g + 1), LN_EPS, s["x_scales"])
                if g == 1:
                    pool.wait_ge(s["x_scales"], g + 1)
                    pool.wait_ge(s["c_stats"], B * KT)
                    st.done(nc.gpsimd.tensor_scalar(rtmp[:, NT:NT + B * KT], mv[:, 0:B * KT, 1], LN_EPS, None, ALU.add))
                    nc.gpsimd.tensor_tensor(rstd[:, 0:B * KT], rtmp[:, NT:NT + B * KT], mhalf[:, 0:B * KT],
                                            ALU.pow).then_inc(s["c_scales"], 1)


def attention1_tensors(env, stack):
    c, sem = {}, env["sem"]

    def sb(name, shape, dt=F32):
        c[name] = env["sb"](stack, "c_" + name, shape, dt)
    sb("CN", [P, B * KT, D])
    sb("LT", [P, B, NK1])
    sb("wq", [P, INNER])
    sb("wkv", [P, 2 * INNER])
    sb("wo", [DH + 1, H1, D + 1])
    for n in ("gout", "bout"):
        sb(n, [P, D])
    for n in ("gx", "bx", "gl", "bl"):
        sb(n, [P, 1])
    sb("maskB", [P, B * SK // 4], I32)
    sb("maskc", [P, B * KT // 4], I32)
    sb("invB", [P, B * SK], U8)
    sb("mask01", [P, B * KT])
    for n in ("loaded_ctx", "loaded_norm", "loaded_mask", "loaded_w"):
        c[n] = sem("c_" + n)
    env["c"] = c
    d = {"rw": env["sb"](stack, "rw", [P, E1]), "rank": env["sb"](stack, "rankD", [P, E1]),
         "biasB": env["sb"](stack, "biasB", [P, E1])}
    for n in ("w1", "w3", "w2"):
        d[n] = env["sb"](stack, n + "D", [P, E1 + 1, D])
    for n in ("loaded_small", "loaded_w"):
        d[n] = sem("d_" + n)
    env["d"] = d


def attention1(env, stack):
    nc, dram, sem, X, ps = env["nc"], env["dram"], env["sem"], env["X"], env["ps"]
    identf, stats, mv, rstd, rtmp, mhalf = (env[n] for n in ("identf", "stats", "mv", "rstd", "rtmp", "mhalf"))

    def sb(name, shape, dt=F32):
        return env["sb"](stack, name, shape, dt)

    c = env["c"]
    LT, wq, wkv, wo, gout, bout, mask01, invB = (c[n] for n in ("LT", "wq", "wkv", "wo", "gout", "bout", "mask01", "invB"))
    s = {n: sem("c_" + n) for n in ("xn", "t_mm", "lt", "filled")}

    with nc.Block() as block:
        @block.tensor
        def _(pe):
            for g in range(NT // 4):
                pe.wait_ge(s["xn"], 4 * (g + 1))
                for i in range(4):
                    mm = nc.tensor.transpose(ps[:, g, i * P:(i + 1) * P], env["Xn"][:, 4 * g + i, :], identf[:, :])
                mm.then_inc(s["t_mm"], 1)

        @block.scalar
        def _(act):
            act.wait_ge(c["loaded_norm"], 16 * 4)
            for g in range(NT // 4):
                act.wait_ge(s["t_mm"], g + 1)
                nc.scalar.activation(LT[:, 2 * g:2 * g + 2, SK:NK1], ps[:, g, :].rearrange("p (a q) -> p a q", a=2),
                                     ACT.Identity, scale=c["gl"][:, :], bias=c["bl"][:, :]).then_inc(s["lt"], 1)

        @block.vector
        def _(dve):
            for t in range(NT):
                stream_normed(env, t).then_inc(s["xn"], 1)
            for b in range(B):
                dve.wait_ge(s["lt"], b // 2 + 1)
                nc.vector.copy_predicated(LT[:, b, 0:SK], invB[:, b * SK:(b + 1) * SK],
                                          LT[:, b, SK:SK + 1].to_broadcast([P, SK])).then_inc(s["filled"], 1)

    LTb = sb("LTb", [P, NK1])
    mkb = sb("mkb", [P, KT])
    Q = sb("Qc", [P, INNER // P, SQ])
    K = sb("Kc", [P, INNER // P, NK1])
    V = sb("Vc", [P, KJ, H1, DH + 1])
    mn, rz = sb("mnc", [P, 2]), sb("rzc", [P, QT])
    e = [sb(f"ec{i}", [P, 2, NK1 // 2]) for i in range(2)]
    eT = [sb(f"eTc{i}", [P, KJ, SQ]) for i in range(2)]
    OT = [sb(f"OTc{i}", [DH + 1, SQ]) for i in range(2)]
    y, yn = sb("yc", [P, QT, D]), sb("ync", [P, QT, D])
    xs, xsmv, xsr = sb("xsc", [P, QT, D]), sb("xsmv", [P, QT, 2]), sb("xsr", [P, QT])
    T_BANK, O_BANK, Y_BANK = 4, 6, 7
    SCALE = 1.0 / DH
    UNITS, NJOB = H1 * QT, 8
    s = {n: sem("c1_" + n) for n in (
        "batch", "ones", "job_mm", "job_act", "job_dve", "s_mm", "row_min", "exp", "t_mm", "t_dve", "t_act",
        "pv_mm", "ot", "wo_mm", "y_added", "ystat", "yr", "yn", "x_out", "xstat", "xr", "xn",
        "dstep", "pstep")}

    def at(k, n):
        return k >= n if isinstance(k, int) else True

    def job_mm(pe, k, i):
        if i >= 3:
            pe.wait_ge(s["job_act" if (i - 3) % 2 == 0 else "job_dve"], k * 4 + (i - 3) // 2 + 1)
        bank = 2 * (i % 3)
        for a in range(2):
            if i < 3:
                j = 2 * i + a
                mm = nc.tensor.matmul(ps[:, bank + a, :], LTb[:, j * P:(j + 1) * P], wkv[:, INNER:2 * INNER], start=True, stop=True)
            elif i == 3:
                for c in (2 * a, 2 * a + 1):
                    mm = nc.tensor.matmul(ps[:, bank + a, (c % 2) * SQ:(c % 2 + 1) * SQ], wq[:, c * P:(c + 1) * P],
                                          LTb[:, SK:NK1], start=True, stop=True)
            else:
                c = i - 4
                mm = nc.tensor.matmul(ps[:, bank + a, 0:NK1 // 2], wkv[:, c * P:(c + 1) * P],
                                      LTb[:, a * NK1 // 2:(a + 1) * NK1 // 2], start=True, stop=True)
        mm.then_inc(s["job_mm"], 1)

    def job_out(eng, k, i):
        eng.wait_ge(s["job_mm"], k * NJOB + i + 1)
        bank, on_act = 2 * (i % 3), i % 2 == 0
        if i < 3:
            for a in range(2):
                j = 2 * i + a
                src, dst = ps[:, bank + a, :].rearrange("p (h d) -> p h d", h=H1), V[:, j, :, 0:DH]
                if on_act:
                    ins = nc.scalar.activation(dst, src, ACT.Copy, scale=mkb[:, j:j + 1] if j < KT else 1.0)
                else:
                    ins = nc.vector.tensor_scalar(dst, src, mkb[:, j:j + 1], None, ALU.mult)
        elif i == 3:
            ins = nc.vector.tensor_scalar(Q[:, :, :].rearrange("p (a c) q -> p a (c q)", a=2), ps[:, bank:bank + 2, :],
                                          -SCALE, None, ALU.mult)
        else:
            src, dst = ps[:, bank:bank + 2, 0:NK1 // 2], K[:, i - 4, :].rearrange("p (a k) -> p a k", a=2)
            ins = nc.scalar.copy(dst, src) if on_act else nc.vector.tensor_copy(dst, src)
        ins.then_inc(s["job_act" if on_act else "job_dve"], 1)

    def score(pe, k, u):
        h, q = u // 2, u % 2
        r = slice(64 * (h % 2), 64 * (h % 2) + DH)
        if u == 0:
            pe.wait_ge(s["job_act"], k * 4 + 4)
        elif u == 1:
            pe.wait_ge(s["job_dve"], k * 4 + 4)
        else:
            pe.wait_ge(s["exp"], k * UNITS + u - 1)
        for a in range(2):
            mm = nc.tensor.matmul(ps[:, 2 * (u % 2) + a, 0:NK1 // 2], Q[r, h // 2, q * P:(q + 1) * P],
                                  K[r, h // 2, a * NK1 // 2:(a + 1) * NK1 // 2], start=True, stop=True)
        mm.then_inc(s["s_mm"], 1)

    def transpose(pe, k, u):
        pe.wait_ge(s["exp"], k * UNITS + u + 1)
        if u:
            pe.wait_ge(s["t_dve"], k * UNITS + u)
            pe.wait_ge(s["t_act"], k * UNITS + u)
        for j in range(KJ):
            mm = nc.tensor.transpose(ps[:, T_BANK + j // 4, (j % 4) * P:(j % 4 + 1) * P],
                                     e[u % 2][:, j // 3, (j % 3) * P:(j % 3 + 1) * P], identf[:, :])
            if j == 3:
                mm.then_inc(s["t_mm"], 1)
        mm.then_inc(s["t_mm"], 1)

    def values(pe, k, h, half):
        if half == 0:
            if h == 0:
                pe.wait_ge(s["ones"], k + 1)
            pe.wait_ge(s["t_dve"], k * UNITS + 2 * h + 2)
            pe.wait_ge(s["t_act"], k * UNITS + 2 * h + 2)
            if h or at(k, 1):
                pe.wait_ge(s["ot"], k * H1 + h)
        for j in range(3 * half, 3 * half + 3):
            mm = nc.tensor.matmul(ps[0:DH + 1, O_BANK, 0:SQ], V[:, j, h, :], eT[h % 2][:, j, :],
                                  start=(j == 0), stop=(j == KJ - 1))
        if half:
            mm.then_inc(s["pv_mm"], 1)

    def project_mm(pe, k, h):
        pe.wait_ge(s["ot"], k * H1 + h + 1)
        if h or at(k, 1):
            pe.wait_ge(s["y_added"], k * H1 + h)
        for q in range(QT):
            mm = nc.tensor.matmul(ps[:, Y_BANK, q * (D + 1):(q + 1) * (D + 1)], OT[h % 2][:, q * P:(q + 1) * P], wo[:, h, :],
                                  start=True, stop=True)
        mm.then_inc(s["wo_mm"], 1)

    def tensor_step(pe, k):
        pe.wait_ge(s["batch"], 2 * (k + 1))
        for i in range(NJOB):
            job_mm(pe, k, i)
            if i == 0 and at(k, 1):
                project_mm(pe, k - 1, H1 - 1)
        score(pe, k, 0)
        for u in range(UNITS):
            if u + 1 < UNITS:
                score(pe, k, u + 1)
            transpose(pe, k, u)
            if u >= 2:
                values(pe, k, (u - 2) // 2, u % 2)
            if u >= 4 and u % 2 == 0:
                project_mm(pe, k, (u - 4) // 2)
        project_mm(pe, k, H1 - 2)
        for half in range(2):
            values(pe, k, H1 - 1, half)

    def scalar_step(act, k):
        act.wait_ge(s["batch"], 2 * (k + 1))
        for i in range(0, NJOB, 2):
            job_out(act, k, i)

        def exps(u):
            act.wait_ge(s["row_min"], k * UNITS + u + 1)
            if u >= 2:
                act.wait_ge(s["t_mm"], 2 * (k * UNITS + u - 1))
            nc.scalar.activation(e[u % 2][:, :, :], ps[:, 2 * (u % 2):2 * (u % 2) + 2, 0:NK1 // 2], ACT.Exp, scale=-1.0,
                                 bias=mn[:, u % 2:u % 2 + 1]).then_inc(s["exp"], 1)
        exps(0)
        for u in range(UNITS):
            if u + 1 < UNITS:
                exps(u + 1)
            act.wait_ge(s["t_mm"], 2 * (k * UNITS + u + 1))
            nc.scalar.copy(eT[u // 2 % 2][:, 4:6, (u % 2) * P:(u % 2 + 1) * P],
                           ps[:, T_BANK + 1, 0:2 * P].rearrange("p (j q) -> p j q", q=P)).then_inc(s["t_act"], 1)
            if u >= 3 and u % 2:
                output_copy(act, k, (u - 3) // 2)
        output_copy(act, k, H1 - 1)

    def output_copy(act, k, h):
        act.wait_ge(s["pv_mm"], k * H1 + h + 1)
        if h >= 2 or at(k, 1):
            act.wait_ge(s["wo_mm"], k * H1 + h - 1)
        nc.scalar.copy(OT[h % 2][:, :], ps[0:DH + 1, O_BANK, 0:SQ]).then_inc(s["ot"], 1)

    def vector_step(dve, st, k):
        first = not (isinstance(k, int) and k == B)
        if first:
            dve.wait_ge(s["batch"], 2 * (k + 1))
        for i in range(1, NJOB, 2):
            if i == 5 and at(k, 1):
                st.wait()
            if first:
                job_out(dve, k, i)
            if i == 1 and at(k, 1):
                output_add(dve, st, k - 1, H1 - 1)
            if i == 3 and at(k, 1):
                dve.wait_ge(s["y_added"], k * H1)
                for q in range(QT):
                    st.mark(nc.vector.bn_stats(stats[:, q, :], y[:, q, :]))
            if i == 5 and at(k, 1):
                for q in range(QT):
                    ins = nc.vector.bn_aggr(mv[:, q, :], stats[:, q, :])
                ins.then_inc(s["ystat"], 1)

        def row_min(u):
            dve.wait_ge(s["s_mm"], k * UNITS + u + 1)
            nc.vector.tensor_reduce(mn[:, u % 2:u % 2 + 1], ps[:, 2 * (u % 2):2 * (u % 2) + 2, 0:NK1 // 2], AX.XY,
                                    ALU.min).then_inc(s["row_min"], 1)
        if first:
            row_min(0)
        for u in range(UNITS):
            if first and u + 1 < UNITS:
                row_min(u + 1)
            if first:
                dve.wait_ge(s["t_mm"], 2 * (k * UNITS + u) + 1)
                nc.vector.tensor_copy(eT[u // 2 % 2][:, 0:4, (u % 2) * P:(u % 2 + 1) * P],
                                      ps[:, T_BANK, :].rearrange("p (j q) -> p j q", q=P)).then_inc(s["t_dve"], 1)
            if u == 1 and at(k, 1):
                dve.wait_ge(s["yr"], k)
                for q in range(QT):
                    st.mark(nc.vector.tensor_scalar(yn[:, q, :], y[:, q, :], mv[:, q, 0:1], rstd[:, q:q + 1], ALU.subtract, ALU.mult))
                st.wait()
                st.done(nc.vector.tensor_tensor(yn[:, :, :], yn[:, :, :],
                                                gout[:, :].rearrange("p (a d) -> p a d", a=1).to_broadcast([P, QT, D]), ALU.mult))
                st.done(nc.vector.tensor_tensor(yn[:, :, :], yn[:, :, :],
                                                bout[:, :].rearrange("p (a d) -> p a d", a=1).to_broadcast([P, QT, D]), ALU.add))
                x_old = X[:, bass.ds((k - 1) * QT, QT), :]
                nc.vector.tensor_tensor(xs[:, :, :], x_old, yn[:, :, :], ALU.add).then_inc(s["yn"], 1)
            if u == 2 and at(k, 1):
                dve.wait_ge(s["yn"], k)
                x_old = X[:, bass.ds((k - 1) * QT, QT), :]
                nc.vector.tensor_tensor(x_old, x_old, yn[:, :, :], ALU.add).then_inc(s["x_out"], 1)
                for q in range(QT):
                    st.mark(nc.vector.bn_stats(stats[:, 2 + q, :], xs[:, q, :]))
                st.wait()
            if u == 3 and at(k, 1):
                for q in range(QT):
                    ins = nc.vector.bn_aggr(xsmv[:, q, :], stats[:, 2 + q, :])
                ins.then_inc(s["xstat"], 1)
            if u == 6 and at(k, 1):
                dve.wait_ge(s["xr"], k)
                for q in range(QT):
                    ins = nc.vector.tensor_scalar(env["Xn"][:, bass.ds((k - 1) * QT + q, 1), :].rearrange("p a d -> p (a d)"),
                                                  xs[:, q, :], xsmv[:, q, 0:1], xsr[:, q:q + 1], ALU.subtract, ALU.mult)
                ins.then_inc(s["xn"], 1)
            if first and u >= 4 and u % 2 == 0:
                output_add(dve, st, k, (u - 4) // 2)
        if first:
            output_add(dve, st, k, H1 - 2)

    def output_add(dve, st, k, h):
        dve.wait_ge(s["wo_mm"], k * H1 + h + 1)
        o = ps[:, Y_BANK, 0:QT * (D + 1)].rearrange("p (q d) -> p q d", q=QT)
        st.done(nc.vector.reciprocal(rz[:, :], o[:, :, D]))
        if h:
            dve.wait_ge(s["y_added"], k * H1 + h)
        for q in range(QT):
            if h == 0:
                ins = nc.vector.tensor_scalar(y[:, q, :], o[:, q, 0:D], rz[:, q:q + 1], None, ALU.mult)
            else:
                ins = nc.vector.scalar_tensor_tensor(y[:, q, :], o[:, q, 0:D], rz[:, q:q + 1], y[:, q, :], ALU.mult, ALU.add)
        ins.then_inc(s["y_added"], 1)

    with nc.Block() as block:
        @block.gpsimd
        def _(pool):
            st = Steps(pool, s["pstep"])

            def batch(b):
                if b:
                    pool.wait_ge(s["job_mm"], b * NJOB)
                nc.gpsimd.tensor_copy(LTb[:, :], LT[:, b, :]).then_inc(s["batch"], 1)
                if b:
                    pool.wait_ge(s["job_act"], 4 * b)
                    pool.wait_ge(s["job_dve"], 4 * b)
                nc.gpsimd.tensor_copy(mkb[:, :], mask01[:, b * KT:(b + 1) * KT]).then_inc(s["batch"], 1)
            nc.gpsimd.memset(V[:, KT:KJ, :, DH:DH + 1], 1.0).then_inc(s["pstep"], 1)
            st.n += 1
            st.wait()
            batch(0)
            for b in range(B + 1):
                if b < B:
                    if b:
                        pool.wait_ge(s["pv_mm"], b * H1)
                    nc.gpsimd.tensor_copy(
                        V[:, 0:KT, :, DH:DH + 1].rearrange("p j h c -> p j (h c)"),
                        mask01[:, b * KT:(b + 1) * KT].rearrange("p (j a) -> p j a", a=1).to_broadcast([P, KT, H1])).then_inc(s["ones"], 1)
                if b:
                    pool.wait_ge(s["ystat"], b)
                    st.done(nc.gpsimd.tensor_scalar(rtmp[:, 0:QT], mv[:, 0:QT, 1], LN_EPS, None, ALU.add))
                    if b >= 2:
                        pool.wait_ge(s["yn"], b - 1)
                    nc.gpsimd.tensor_tensor(rstd[:, 0:QT], rtmp[:, 0:QT], mhalf[:, 0:QT], ALU.pow).then_inc(s["yr"], 1)
                    pool.wait_ge(s["yr"], b)
                    pool.wait_ge(s["xstat"], b)
                    st.done(nc.gpsimd.tensor_scalar(rtmp[:, 2:2 + QT], xsmv[:, :, 1], LN_EPS, None, ALU.add))
                    if b >= 2:
                        pool.wait_ge(s["xn"], b - 1)
                    nc.gpsimd.tensor_tensor(xsr[:, :], rtmp[:, 2:2 + QT], mhalf[:, 0:QT], ALU.pow).then_inc(s["xr"], 1)
                    pool.wait_ge(s["xr"], b)
                if b + 1 < B:
                    batch(b + 1)

        @block.tensor
        def _(pe):
            pe.wait_ge(c["loaded_w"], 16 * 5)
            tensor_step(pe, 0)
            with pe.Fori(1, B) as k:
                tensor_step(pe, k)
            project_mm(pe, B - 1, H1 - 1)

        @block.scalar
        def _(act):
            scalar_step(act, 0)
            with act.Fori(1, B) as k:
                scalar_step(act, k)

        @block.vector
        def _(dve):
            dve.wait_ge(c["loaded_w"], 16 * 5)
            st = Steps(dve, s["dstep"])
            vector_step(dve, st, 0)
            with st.loop(1, B, 1, 8 + H1) as k:
                vector_step(dve, st, k)
            vector_step(dve, st, B)


def experts1(env, stack):
    nc, dram, sem, X, ps = env["nc"], env["dram"], env["sem"], env["X"], env["ps"]
    identf, stats, mv, rstd, rtmp, mhalf = (env[n] for n in ("identf", "stats", "mv", "rstd", "rtmp", "mhalf"))

    def sb(name, shape, dt=F32):
        return env["sb"](stack, name, shape, dt)

    NE = E1 + 1
    d, Xn = env["d"], env["Xn"]
    W1, W3, W2, rw, rank, biasB = (d[n] for n in ("w1", "w3", "w2", "rw", "rank", "biasB"))
    XnT = sb("XnTD", [P, NT * P])
    L, ex, k1, k2, key, G = (sb(n, [P, NT, E1]) for n in ("LD", "exD", "k1D", "k2D", "keyD", "GD"))
    mx, den, kmx = (sb(n, [P, NT]) for n in ("mxD", "denD", "kmxD"))
    silu = [sb(f"siluD{i}", [P, 512]) for i in range(3)]
    hid = [sb(f"hidD{i}", [P, 512]) for i in range(3)]
    s = {n: sem("d_" + n) for n in (
        "steps", "t_mm", "xt", "l_mm", "l_out", "shifted", "exps",
        "h_mm", "silu", "hid", "y_mm", "y_added")}

    L_BANK = 7

    def y_wait(g, e):
        return g * NE + e - (0 if e == 0 else 2 if e == 1 else 1)

    with nc.Block() as block:
        @block.tensor
        def _(pe):
            for g in range(4):
                for i in range(4):
                    mm = nc.tensor.transpose(ps[:, g, i * P:(i + 1) * P], Xn[:, 4 * g + i, :], identf[:, :])
                mm.then_inc(s["t_mm"], 1)
            pe.wait_ge(d["loaded_small"], 16 * 3)
            for t in range(NT):
                if t % 4 == 0:
                    pe.wait_ge(s["xt"], t // 4 + 1)
                mm = nc.tensor.matmul(ps[:, L_BANK, t * E1:(t + 1) * E1], XnT[:, t * P:(t + 1) * P], rw[:, :], start=True, stop=True)
            mm.then_inc(s["l_mm"], 1)
            pe.wait_ge(d["loaded_w"], 16 * 6)

            def up(g, e):
                n, peeled = g * NE + e, isinstance(g, int) and g == 0
                if not (peeled and e < 3):
                    pe.wait_ge(s["hid"], n - 2)
                for i, w in enumerate((W1, W3)):
                    nc.tensor.matmul(ps[:, 3 * i + e % 3, :], w[:, e, :], XnT[:, bass.ds(g * 512, 512)],
                                     start=True, stop=True).then_inc(s["h_mm"], 1)

            def down(g, e):
                pe.wait_ge(s["hid"], g * NE + e + 1)
                if not (isinstance(g, int) and g == 0 and e < 2):
                    pe.wait_ge(s["y_added"], y_wait(g, e))
                elif e == 1:
                    pe.wait_ge(s["l_out"], 1)
                for t in range(4):
                    mm = nc.tensor.matmul(ps[:, 6 + e % 2, t * P:(t + 1) * P], hid[e % 3][:, t * P:(t + 1) * P],
                                          W2[:, e, :], start=True, stop=True)
                mm.then_inc(s["y_mm"], 1)

            def group(g):
                up(g, 0)
                up(g, 1)
                for e in range(NE):
                    if e + 2 < NE:
                        up(g, e + 2)
                    down(g, e)
            group(0)
            with pe.Fori(1, 4) as g:
                group(g)

        @block.scalar
        def _(act):
            for g in range(4):
                act.wait_ge(s["t_mm"], g + 1)
                nc.scalar.copy(XnT[:, g * 512:(g + 1) * 512], ps[:, g, :]).then_inc(s["xt"], 1)
            act.wait_ge(s["shifted"], 1)
            nc.scalar.activation(ex[:, :, :], ex[:, :, :], ACT.Exp).then_inc(s["exps"], 1)

            def group(g):
                for e in range(NE):
                    n = g * NE + e
                    act.wait_ge(s["h_mm"], 2 * n + 1)
                    if not (isinstance(g, int) and g == 0 and e < 3):
                        act.wait_ge(s["hid"], n - 2)
                    nc.scalar.activation(silu[e % 3][:, :], ps[:, e % 3, :], ACT.Silu).then_inc(s["silu"], 1)
            group(0)
            with act.Fori(1, 4) as g:
                group(g)

        @block.vector
        def _(dve):
            st = Steps(dve, s["steps"])

            def hidden(g, e):
                n = g * NE + e
                dve.wait_ge(s["silu"], n + 1)
                dve.wait_ge(s["h_mm"], 2 * n + 2)
                if not (isinstance(g, int) and g == 0 and e < 3):
                    dve.wait_ge(s["y_mm"], n - 2)
                nc.vector.tensor_tensor(hid[e % 3][:, :], silu[e % 3][:, :], ps[:, 3 + e % 3, :], ALU.mult).then_inc(s["hid"], 1)

            def over_experts(a):
                return a[:, :].rearrange("p (t a) -> p t a", a=1).to_broadcast([P, NT, E1])

            def over_tiles(a):
                return a[:, :].rearrange("p (a e) -> p a e", a=1).to_broadcast([P, NT, E1])

            def first_of_max(dst, src):
                st.done(nc.vector.tensor_reduce(mx[:, :], src[:, :, :], AX.X, ALU.max))
                st.done(nc.vector.tensor_tensor(key[:, :, :], src[:, :, :], over_experts(mx), ALU.is_equal))
                st.done(nc.vector.tensor_tensor(key[:, :, :], key[:, :, :], over_tiles(rank), ALU.mult))
                st.done(nc.vector.tensor_reduce(kmx[:, :], key[:, :, :], AX.X, ALU.max))
                st.done(nc.vector.tensor_tensor(dst[:, :, :], key[:, :, :], over_experts(kmx), ALU.is_equal))

            def group(g):
                if not (isinstance(g, int) and g == 0):
                    hidden(g, 0)
                for e in range(NE):
                    if e + 1 < NE:
                        hidden(g, e + 1)
                    dve.wait_ge(s["y_mm"], g * NE + e + 1)
                    if not (isinstance(g, int) and g == 0 and e == 0):
                        dve.wait_ge(s["y_added"], g * NE + e)
                    yb = ps[:, 6 + e % 2, :]
                    if e == E1:
                        x = X[:, bass.ds(g * 4, 4), :]
                        i = nc.vector.tensor_tensor(x, x, yb.rearrange("p (t d) -> p t d", t=4), ALU.add)
                    else:
                        for t in range(4):
                            x = X[:, bass.ds(g * 4 + t, 1), :].rearrange("p a d -> p (a d)")
                            gate = G[:, bass.ds(g * 4 + t, 1), e:e + 1].rearrange("p a d -> p (a d)")
                            i = nc.vector.scalar_tensor_tensor(x, yb[:, t * P:(t + 1) * P], gate, x, ALU.mult, ALU.add)
                    i.then_inc(s["y_added"], 1)
            dve.wait_ge(s["l_mm"], 1)
            nc.vector.tensor_copy(L[:, :, :].rearrange("p t e -> p (t e)"), ps[:, L_BANK, 0:NT * E1]).then_inc(s["l_out"], 1)
            dve.wait_ge(s["l_out"], 1)
            st.done(nc.vector.tensor_reduce(mx[:, :], L[:, :, :], AX.X, ALU.max))
            nc.vector.tensor_tensor(ex[:, :, :], L[:, :, :], over_experts(mx), ALU.subtract).then_inc(s["shifted"], 1)
            hidden(0, 0)
            dve.wait_ge(d["loaded_small"], 16 * 3)
            dve.wait_ge(s["exps"], 1)
            st.done(nc.vector.tensor_reduce(den[:, :], ex[:, :, :], AX.X, ALU.add))
            st.done(nc.vector.reciprocal(den[:, :], den[:, :]))
            st.done(nc.vector.tensor_tensor(ex[:, :, :], ex[:, :, :], over_experts(den), ALU.mult))
            st.done(nc.vector.tensor_tensor(L[:, :, :], ex[:, :, :], over_tiles(biasB), ALU.add))
            first_of_max(k1, L)
            st.done(nc.vector.scalar_tensor_tensor(L[:, :, :], k1[:, :, :], -3e38, L[:, :, :], ALU.mult, ALU.add))
            first_of_max(k2, L)
            st.done(nc.vector.tensor_tensor(k1[:, :, :], k1[:, :, :], k2[:, :, :], ALU.add))
            st.done(nc.vector.tensor_tensor(G[:, :, :], k1[:, :, :], ex[:, :, :], ALU.mult))
            group(0)
            with dve.Fori(1, 4) as g:
                group(g)


def kernel(**inputs):
    import numpy as np
    import concourse.bacc as bacc
    from concourse.bass_utils import run_bass_kernel_spmd as run

    v = {k: np.asarray(a) for k, a in inputs.items()}
    perm = np.arange(D).reshape(PAIRS, 2, DK).transpose(1, 2, 0).reshape(-1)
    w = lambda a: np.ascontiguousarray(a)
    sel = np.zeros((2, DK, PAIRS, 2, PAIRS), np.float32)
    for half in range(2):
        for pair in range(PAIRS):
            sel[half, :, pair, half, pair] = 1
    arrays = {
        "x": w(v["x"].reshape(B * SQ, D)),
        "ctx": w(v["ctx_1024"].reshape(B * SK, D)),
        "ctxT": w(v["ctx_1024"].transpose(2, 0, 1)),
        "mask": w(v["mask_BxS2_bk1"]).view(np.int32).reshape(1, B * SK // 4),
        "ident": np.eye(P, dtype=np.float32),
        "sel": sel.reshape(P, H0),
        "wq0T": w(v["L0_xattn_Wq"][perm].T), "bq0": w(v["L0_xattn_bq"][perm].reshape(D, 1)),
        "wk0T": w(v["L0_xattn_Wk"][perm].T), "bk0": w(v["L0_xattn_bk"][perm].reshape(D, 1)),
        "wv0T": w(v["L0_xattn_Wv"].T), "bv0": w(v["L0_xattn_bv"].reshape(1, D)),
        "wo0T": w(v["L0_xattn_Wo"].T), "bo0": w(v["L0_xattn_bo"].reshape(1, D)),
        "tw1T": w(v["L0_xattn_w1"].T), "tb1": w(v["L0_xattn_b1"].reshape(64, 1)),
        "tw2T": w(v["L0_xattn_w2"].T), "tb2": w(v["L0_xattn_b2"].reshape(64, 1)),
        "rms_w": w(v["L0_ffn_rms_w"].reshape(D, 1)), "gate_wT": w(v["L0_ffn_gate_w"].T),
        "rank": np.tile(np.arange(E0, 0, -1, dtype=np.float32), (P, 1)),
        "eb1": w(v["L0_ffn_b1"].reshape(E0 * FC, P).T), "eb2": w(v["L0_ffn_b2"]),
        "eW1": w(v["L0_ffn_W1"]), "eW2": w(v["L0_ffn_W2"]),
        "maskc": w(v["mask_BxS2_bk1"].reshape(B * KT, P).T).view(np.int32),
        "wq1": w(v["L1_xattn_Wq"]), "wkv1": w(v["L1_xattn_Wkv"]), "wo1": w(v["L1_xattn_Wo"]),
        "lnx_g": w(v["L1_xattn_ln_x_g"].reshape(D, 1)), "lnx_b": w(v["L1_xattn_ln_x_b"].reshape(D, 1)),
        "lnl_g": w(v["L1_xattn_ln_l_g"].reshape(D, 1)), "lnl_b": w(v["L1_xattn_ln_l_b"].reshape(D, 1)),
        "lno_g": w(v["L1_xattn_ln_o_g"].reshape(1, D)), "lno_b": w(v["L1_xattn_ln_o_b"].reshape(1, D)),
        "router_w": w(v["L1_ffn_router_w"]), "expert_bias": w(v["L1_ffn_expert_bias"].reshape(1, E1)),
        "w1": w(v["L1_ffn_w1"]), "w2": w(v["L1_ffn_w2"]), "w3": w(v["L1_ffn_w3"]),
        "sw1": w(v["L1_ffn_sw1"]), "sw2": w(v["L1_ffn_sw2"]), "sw3": w(v["L1_ffn_sw3"]),
        "tw3": w(np.broadcast_to(v["L0_xattn_w3"].reshape(64, 1), (64, P))), "tb3": w(v["L0_xattn_b3"].reshape(1, 1)),
    }
    nc = bacc.Bacc("TRN2", target_bir_lowering=False, num_devices=1)
    dram = {n: nc.dram_tensor("in_" + n, a.shape, mybir.dt.from_np(a.dtype), kind="ExternalInput").ap()
            for n, a in arrays.items()}
    out = nc.dram_tensor("out", [B * SQ, D], F32, kind="ExternalOutput").ap()
    build(nc, dram, out)
    r = run(nc, [{"in_" + n: a for n, a in arrays.items()}], core_ids=[0])
    return r.results[0]["out"].reshape(B, SQ, D)
```

```python
from contextlib import ExitStack, contextmanager

import numpy as np

import concourse.bass as bass
from concourse import mybir

F32 = mybir.dt.float32
F32R = mybir.dt.float32r
BF16 = mybir.dt.bfloat16
U8 = mybir.dt.uint8
I32 = mybir.dt.int32
ACT = mybir.ActivationFunctionType
ALU = mybir.AluOpType
AX = mybir.AxisListType

P = 128
B, SQ, SK, D = 8, 256, 512, 128
NT = B * SQ // P
QT, KT = SQ // P, SK // P
H0, DK = 16, 8
PAIRS = H0 // 2
ROWS = 6 * DK
MAXROWS = 3
LAG = 4
H1, DH = 8, 64
INNER = H1 * DH
NK1 = SK + SQ
KJ = NK1 // P
E0, F0 = 8, 512
FC = F0 // P
E1 = 8
LN_EPS, RMS_EPS = 1e-5, 1e-6
LOG_T_MIN, LOG_T_MAX = -2.302585092994046, 2.302585092994046
PARTS = [(0, 0), (1, 0), (2, 0), (0, 1), (0, 2), (1, 1)]


class Steps:

    def __init__(self, eng, sem):
        self.eng, self.sem, self.n, self.base = eng, sem, 0, 0

    @contextmanager
    def loop(self, start, end, step, per_turn):
        before, turns = self.n, (end - start) // step
        with self.eng.Fori(start, end, step) as i:
            self.base = (i - start) * (per_turn // step) if start else i * (per_turn // step)
            yield i
        assert self.n - before == per_turn and per_turn % step == 0, (self.n - before, per_turn)
        self.base = 0
        self.n = before + turns * per_turn

    def mark(self, ins):
        self.n += 1
        ins.then_inc(self.sem, 1)

    def wait(self):
        self.eng.wait_ge(self.sem, self.base + self.n)

    def done(self, ins):
        self.mark(ins)
        self.wait()


def layer_norm_stats(dve, steps, nc, src, tile_ids, stats, mv):
    for t in tile_ids:
        steps.mark(nc.vector.bn_stats(stats[:, t, :], src[:, t, :]))
    steps.wait()
    for t in tile_ids:
        steps.mark(nc.vector.bn_aggr(mv[:, t, :], stats[:, t, :]))
    steps.wait()


PASSES = ((0, 0), (0, 1), (1, 0))


def product(nc, out, lhsT, rhs):
    for n, (i, j) in enumerate(PASSES):
        mm = nc.tensor.matmul(out, lhsT(i), rhs(j), start=(n == 0), stop=(n == len(PASSES) - 1))
    return mm


def router_products(pe, nc, env, s, wp, XnT, banks, l_bank, hold):
    ps, ne = env["ps"], wp[0].shape[1]
    pe.wait_ge(s["rw_low"], 1)
    for g in range(4):
        pe.wait_ge(s["xt_low"], g + 1)
        if g >= 2:
            pe.wait_ge(s["lt_out"], g - 1)
        product(nc, ps[0:ne, banks[g % 2], :], lambda p: wp[p][:, :],
                lambda p: XnT[p][:, g * 512:(g + 1) * 512]).then_inc(s["lt_mm"], 1)
    for t in range(NT):
        if t % 4 == 0:
            pe.wait_ge(s["lt_out"], t // 4 + 1)
        mm = nc.tensor.transpose(ps[:, l_bank, t * ne:(t + 1) * ne], hold[t // 4][0:ne, (t % 4) * P:(t % 4 + 1) * P],
                                 env["identf"][0:ne, 0:ne])
    mm.then_inc(s["l_mm"], 1)


def router_copies(act, nc, env, s, ne, banks, hold):
    for g in range(4):
        act.wait_ge(s["lt_mm"], g + 1)
        nc.scalar.copy(hold[g][0:ne, :], env["ps"][0:ne, banks[g % 2], :]).then_inc(s["lt_out"], 1)


def router_weights(dve, nc, s, w, wp):
    nc.vector.tensor_copy(wp[0][:, :], w[:, :]).then_inc(s["rw_high"], 1)
    dve.wait_ge(s["rw_high"], 1)
    nc.vector.tensor_tensor(wp[1][:, :], w[:, :], wp[0][:, :].bitcast(F32), ALU.subtract).then_inc(s["rw_low"], 1)


def stream_stats(dve, steps, env, tiles, ready):
    nc = env["nc"]
    for t in tiles:
        steps.mark(nc.vector.bn_stats(env["stats"][:, t, :], env["X"][:, t, :]))
    steps.wait()
    for t in tiles:
        nc.vector.bn_aggr(env["xmv"][:, t, :], env["stats"][:, t, :]).then_inc(ready, 1)


def stream_scales(pool, steps, env, t0, t1, eps, last):
    nc, r2 = env["nc"], env["rtmp2"][:, t0:t1]
    v, r1, r, mh = env["xmv"][:, t0:t1, 1], env["rtmp"][:, t0:t1], env["xr"][:, t0:t1], env["mhalf"][:, t0:t1]
    steps.done(nc.gpsimd.tensor_scalar(r1, v, LN_EPS, None, ALU.add))
    if eps is None:
        nc.gpsimd.tensor_tensor(r, r1, mh, ALU.pow).then_inc(last, 1)
        return
    steps.done(nc.gpsimd.tensor_tensor(r1, r1, mh, ALU.pow))
    steps.done(nc.gpsimd.tensor_tensor(r2, r1, r1, ALU.mult))
    steps.done(nc.gpsimd.tensor_tensor(r2, r2, v, ALU.mult))
    steps.done(nc.gpsimd.tensor_scalar(r2, r2, eps, None, ALU.add))
    steps.done(nc.gpsimd.tensor_tensor(r2, r2, mh, ALU.pow))
    nc.gpsimd.tensor_tensor(r, r1, r2, ALU.mult).then_inc(last, 1)


def stream_normed(env, t):
    return env["nc"].vector.tensor_scalar(env["Xn"][:, t, :], env["X"][:, t, :], env["xmv"][:, t, 0:1],
                                          env["xr"][:, t:t + 1], ALU.subtract, ALU.mult)


def build(nc, dram, out, upto=99):
    es = ExitStack()
    with es:
        def sb(stack, name, shape, dt=F32):
            return stack.enter_context(nc.sbuf_tensor(name, shape, dt))

        def sem(name):
            return es.enter_context(nc.semaphore(name))

        X = sb(es, "X", [P, NT, D])
        identf = sb(es, "identf", [P, P])
        identb = sb(es, "identb", [P, P], BF16)
        stats = sb(es, "stats", [P, 48, 6])
        mv = sb(es, "mv", [P, 48, 2])
        Xn = sb(es, "Xn", [P, NT, D])
        xmv = sb(es, "xmv", [P, NT, 2])
        xr = sb(es, "xr", [P, NT])
        rtmp2 = sb(es, "rtmp2", [P, NT])
        rstd = sb(es, "rstd", [P, 48])
        rtmp = sb(es, "rtmp", [P, 48])
        mhalf = sb(es, "mhalf", [P, 48])
        ps = es.enter_context(nc.psum_tensor("ps", [P, 8, 512], F32))
        env = dict(nc=nc, dram=dram, es=es, sb=sb, sem=sem, X=X, identf=identf, identb=identb, stats=stats,
                   mv=mv, rstd=rstd, rtmp=rtmp, mhalf=mhalf, ps=ps, Xn=Xn, xmv=xmv, xr=xr, rtmp2=rtmp2)
        env["W1"] = sb(es, "W1", [P, E0, F0])
        env["W2"] = sb(es, "W2", [P, E0, FC, D])
        env["w_loaded"] = sem("w_loaded")
        with ExitStack() as la:
            attention0(env, la)
        attention1_tensors(env, es)
        if upto >= 2:
            with ExitStack() as lb:
                experts0(env, lb)
        for n in ("w1", "w3"):
            env["d"][n + "p"] = [sb(es, f"{n}p{i}", [P, E1 + 1, D], F32R) for i in range(2)]
        if upto >= 3:
            with ExitStack() as lc:
                attention1(env, lc)
        if upto >= 4:
            with ExitStack() as ld:
                experts1(env, ld)
        stored = sem("stored")
        with nc.Block() as block:
            @block.sync
            def _(sp):
                sp.dma_start(out.rearrange("(t p) d -> p t d", p=P), X[:, :, :]).then_inc(stored, 16)
                sp.wait_ge(stored, 16)


def attention0(env, stack):
    nc, dram, sem, X, ps = env["nc"], env["dram"], env["sem"], env["X"], env["ps"]
    identf, identb, stats, mv = env["identf"], env["identb"], env["stats"], env["mv"]
    rstd, rtmp, mhalf = env["rstd"], env["rtmp"], env["mhalf"]

    def sb(name, shape, dt=F32):
        return env["sb"](stack, name, shape, dt)

    C = 1.0 / DK ** 0.5
    Qf = sb("Qf", [P, B, SQ])
    Kf = sb("Kf", [P, B, SK])
    V = sb("V", [P, B * KT, H0, DK + 1])
    qsum, ksum = sb("qsum", [P, B]), sb("ksum", [P, B])
    sel, prodsel = sb("sel", [P, H0]), sb("prodsel", [P, B, H0])
    Qp, Kp = sb("Qp", [P, 3, SQ], BF16), sb("Kp", [P, 3, SK], BF16)
    qres, kres = sb("qres", [P, SQ]), sb("kres", [P, SK])
    Q1 = [sb(f"Q1_{i}", [P, PAIRS, SQ], BF16) for i in range(2)]
    K1 = [sb(f"K1_{i}", [P, PAIRS, SK], BF16) for i in range(2)]
    Q2 = [sb(f"Q2_{i}", [P, PAIRS, SQ], BF16) for i in range(2)]
    K2 = [sb(f"K2_{i}", [P, PAIRS, SK], BF16) for i in range(2)]
    boB = sb("boB", [P, D])
    woT = sb("woT", [P, D])
    w1c = sb("w1c", [P, 3, 64])
    w2T = sb("w2T", [64, 64])
    b1c, b2c = sb("b1c", [64, 1]), sb("b2c", [64, 1])
    w3c, b3c = sb("w3c", [64, P]), sb("b3c", [P, 1])

    Vw = [sb(f"Vw{i}", [P, KT, H0, 32]) for i in range(2)]
    parts_ready = sem("parts_ready")
    loaded = {n: sem(f"ld0_{n}") for n in ("x0", "x1", "ctx0", "ctx1", "ctx2", "ctx4", "ctx6", "wk", "wq", "wv", "ident", "consts")}
    s = {n: sem("a0_" + n) for n in (
        "stack1", "stack2", "max_rows", "s1_ready", "s1_min", "e1_ready", "e1_used", "s2_ready", "e2_ready",
        "pv_done", "v_ready", "maxp_ready", "maxp_mm", "maxp_out", "f_ready", "m1_mm", "g1", "m2_mm", "g2",
        "m3_mm", "logt_ready", "invt_ready", "t_ready", "ot_out", "ot_mm", "on_ready", "on_mm", "on_out", "wo_mm", "x_added",
        "dstep", "pstep", "x_stats", "x_scales")}
    N1, N2, NM = 24 * 16, 3 * 16, 2 * 16

    def load_stack1(sp, par, which):
        parts, stack_, x = (Kp, K1[par], 1) if which == "K" else (Qp, Q1[par], 0)
        for c, pair in enumerate(PARTS):
            for half in range(2):
                r = 64 * half + DK * c
                sp.dma_start(stack_[r:r + DK, :, :], parts[64 * half:64 * half + 64, pair[x], :]).then_inc(s["stack1"], 16)

    with ExitStack() as pro:
        def pb(name, shape, dt=F32):
            return env["sb"](pro, name, shape, dt)
        ctxT = pb("ctxT", [P, B, SK])
        Xn = env["Xn"]
        XnT = pb("XnT", [P, NT * P])
        wqT, wkT, wvT = pb("wqT", [P, D]), pb("wkT", [P, D]), pb("wvT", [P, D])
        bqc, bkc, bqn = pb("bqc", [P, 1]), pb("bkc", [P, 1]), pb("bqn", [P, 1])
        bvB = pb("bvB", [P, D])
        steps0, rs_ready, k_mm, v_mm = sem("steps0"), sem("rs_ready"), sem("k_mm"), sem("v_mm")
        xn_ready, t_mm, xt_ready, q_mm, q_out, k_out, v_out = (
            sem(n) for n in ("xn_ready", "t_mm", "xt_ready", "q_mm", "q_out", "k_out", "v_out"))
        bq_neg, pool0, mv_ready = sem("bq_neg"), sem("pool0"), sem("mv_ready")
        ones_set, steps1 = sem("ones_set"), sem("steps1")

        with nc.Block() as block:
            @block.sync
            def _(sp):
                xt = dram["x"].rearrange("(t p) d -> p t d", p=P)
                sp.dma_start(X[:, 0:QT, :], xt[:, 0:QT, :]).then_inc(loaded["x0"], 16)
                sp.dma_start(wkT[:, :], dram["wk0T"]).then_inc(loaded["wk"], 16)
                sp.dma_start(ctxT[:, 0:1, :], dram["ctxT"][:, 0:1, :]).then_inc(loaded["ctx0"], 16)
                sp.dma_start(bkc[:, :], dram["bk0"]).then_inc(loaded["wk"], 16)
                sp.dma_start(identf[:, :], dram["ident"]).then_inc(loaded["ident"], 16)
                sp.dma_start(wqT[:, :], dram["wq0T"]).then_inc(loaded["wq"], 16)
                sp.dma_start(bqc[:, :], dram["bq0"]).then_inc(loaded["wq"], 16)
                sp.dma_start(wvT[:, :], dram["wv0T"]).then_inc(loaded["wv"], 16)
                sp.dma_start(bvB[:, :], dram["bv0"].to_broadcast([P, D])).then_inc(loaded["wv"], 16)
                sp.dma_start(ctxT[:, 1:2, :], dram["ctxT"][:, 1:2, :]).then_inc(loaded["ctx1"], 16)
                sp.dma_start(X[:, QT:NT, :], xt[:, QT:NT, :]).then_inc(loaded["x1"], 16)
                for b in range(2, B, 2):
                    sp.dma_start(ctxT[:, b:b + 2, :], dram["ctxT"][:, b:b + 2, :]).then_inc(loaded[f"ctx{b}"], 16)
                sp.wait_ge(ones_set, 1)
                for n, which in enumerate("KQ"):
                    sp.wait_ge(parts_ready, n + 1)
                    load_stack1(sp, 0, which)

            @block.gpsimd
            def _(pool):
                nc.gpsimd.memset(K1[0][:, :, :], 1.0).then_inc(ones_set, 1)
                nc.gpsimd.memset(mhalf[:, :], -0.5).then_inc(pool0, 1)
                for n, (t0, t1) in enumerate(((0, QT), (QT, NT))):
                    pool.wait_ge(mv_ready, n + 1)
                    nc.gpsimd.tensor_scalar(rtmp[:, t0:t1], mv[:, t0:t1, 1], LN_EPS, None, ALU.add).then_inc(pool0, 1)
                    pool.wait_ge(pool0, n + 2)
                    nc.gpsimd.tensor_tensor(rstd[:, t0:t1], rtmp[:, t0:t1], mhalf[:, t0:t1], ALU.pow).then_inc(rs_ready, 1)
                    if n == 0:
                        for dst, src in ((boB[:, :], dram["bo0"].to_broadcast([P, D])), (woT[:, :], dram["wo0T"]), (sel[:, :], dram["sel"]),
                                         (w1c[:, 0, :], dram["tw1T"][0:1, :].to_broadcast([P, 64])),
                                         (w1c[:, 1, :], dram["tw1T"][1:2, :].to_broadcast([P, 64])),
                                         (w1c[:, 2, :], dram["tw1T"][2:3, :].to_broadcast([P, 64])),
                                         (w2T[:, :], dram["tw2T"]), (b1c[:, :], dram["tb1"]), (b2c[:, :], dram["tb2"]),
                                         (w3c[:, :], dram["tw3"]), (b3c[:, :], dram["tb3"].to_broadcast([P, 1]))):
                            pool.dma_start(dst, src).then_inc(loaded["consts"], 16)
                nc.gpsimd.memset(K1[1][:, :, :], 1.0).then_inc(ones_set, 1)
                for i in range(2):
                    nc.gpsimd.memset(Vw[i][:, :, :, :], 0.0).then_inc(ones_set, 1)

            @block.tensor
            def _(pe):
                def keys(b):
                    if b < 2 or b % 2 == 0:
                        pe.wait_ge(loaded[f"ctx{b}"], 16)
                    if b >= 2:
                        pe.wait_ge(k_out, b - 1)
                    nc.tensor.matmul(ps[:, b % 2, :], wkT[:, :], ctxT[:, b, :], start=True, stop=True).then_inc(k_mm, 1)

                def values0(b):
                    if b >= 2:
                        pe.wait_ge(v_out, b - 1)
                    for j in range(KT):
                        mm = nc.tensor.matmul(ps[:, 4 + b % 2, j * P:(j + 1) * P], ctxT[:, b, j * P:(j + 1) * P],
                                              wvT[:, :], start=True, stop=True)
                    mm.then_inc(v_mm, 1)
                pe.wait_ge(loaded["wk"], 32)
                keys(0)
                pe.wait_ge(loaded["ident"], 16)
                pe.wait_ge(xn_ready, QT)
                for i in range(QT):
                    mm = nc.tensor.transpose(ps[:, 2, i * P:(i + 1) * P], Xn[:, i, :], identf[:, :])
                mm.then_inc(t_mm, 1)
                pe.wait_ge(loaded["wq"], 32)
                pe.wait_ge(xt_ready, 1)
                nc.tensor.matmul(ps[:, 6, 0:SQ], wqT[:, :], XnT[:, 0:SQ], start=True, stop=True).then_inc(q_mm, 1)
                pe.wait_ge(loaded["wv"], 32)
                values0(0)
                for b in range(1, B):
                    keys(b)
                    values0(b)
                for g in range(4):
                    pe.wait_ge(xn_ready, 4 * (g + 1))
                    if g == 2:
                        pe.wait_ge(q_out, 1)
                    for i in range(QT if g == 0 else 0, 4):
                        mm = nc.tensor.transpose(ps[:, (2, 3, 6, 7)[g], i * P:(i + 1) * P], Xn[:, 4 * g + i, :], identf[:, :])
                    mm.then_inc(t_mm, 1)
                for g in range(4):
                    pe.wait_ge(xt_ready, g + 2)
                    if g < 2:
                        pe.wait_ge(k_out, B)
                    if g >= 2:
                        pe.wait_ge(v_out, B)
                    c0 = SQ if g == 0 else 0
                    nc.tensor.matmul(ps[:, (0, 1, 4, 5)[g], c0:512], wqT[:, :], XnT[:, g * 512 + c0:(g + 1) * 512],
                                     start=True, stop=True).then_inc(q_mm, 1)

            @block.scalar
            def _(act):
                def keys_out(b):
                    act.wait_ge(k_mm, b + 1)
                    nc.scalar.activation(Kf[:, b, :], ps[:, b % 2, :], ACT.Identity, bias=bkc[:, :],
                                         accum_out=ksum[:, b:b + 1]).then_inc(k_out, 1)

                def queries_out(b, bank, c0):
                    nc.scalar.activation(Qf[:, b, :], ps[:, bank, c0:c0 + SQ], ACT.Identity,
                                         bias=bqn[:, :], scale=-C, accum_out=qsum[:, b:b + 1]).then_inc(q_out, 1)
                act.wait_ge(loaded["wk"], 32)
                keys_out(0)
                act.wait_ge(t_mm, 1)
                nc.scalar.copy(XnT[:, 0:SQ], ps[:, 2, 0:SQ]).then_inc(xt_ready, 1)
                act.wait_ge(loaded["wq"], 32)
                nc.scalar.mul(bqn[:, :], bqc[:, :], -C).then_inc(bq_neg, 1)
                act.wait_ge(bq_neg, 1)
                act.wait_ge(q_mm, 1)
                queries_out(0, 6, 0)
                for b in range(1, B):
                    keys_out(b)
                for g in range(4):
                    act.wait_ge(t_mm, g + 2)
                    c0 = SQ if g == 0 else 0
                    nc.scalar.copy(XnT[:, g * 512 + c0:(g + 1) * 512], ps[:, (2, 3, 6, 7)[g], c0:512]).then_inc(xt_ready, 1)
                for b in range(1, B):
                    g = b // 2
                    act.wait_ge(q_mm, g + 2)
                    queries_out(b, (0, 1, 4, 5)[g], (b % 2) * SQ)

            @block.vector
            def _(dve):
                st, st2 = Steps(dve, steps0), Steps(dve, steps1)
                dve.wait_ge(loaded["x0"], 16)
                for t in range(QT):
                    st.mark(nc.vector.bn_stats(stats[:, t, :], X[:, t, :]))
                st.wait()
                for t in range(QT):
                    i = nc.vector.bn_aggr(mv[:, t, :], stats[:, t, :])
                i.then_inc(mv_ready, 1)
                dve.wait_ge(mv_ready, 1)
                dve.wait_ge(rs_ready, 1)

                def normed(t):
                    nc.vector.tensor_scalar(Xn[:, t, :], X[:, t, :], mv[:, t, 0:1], rstd[:, t:t + 1],
                                            ALU.subtract, ALU.mult).then_inc(xn_ready, 1)

                def split(full, parts, res):
                    st2.done(nc.vector.tensor_copy(parts[:, 0, :], full))
                    st2.done(nc.vector.tensor_tensor(res[:, :], full, parts[:, 0, :], ALU.subtract))
                    st2.done(nc.vector.tensor_copy(parts[:, 1, :], res[:, :]))
                    nc.vector.tensor_tensor(parts[:, 2, :], res[:, :], parts[:, 1, :], ALU.subtract).then_inc(parts_ready, 1)
                for t in range(QT):
                    normed(t)
                dve.wait_ge(k_out, 1)
                split(Kf[:, 0, :], Kp, kres)
                dve.wait_ge(q_out, 1)
                split(Qf[:, 0, :], Qp, qres)
                nc.vector.memset(V[:, :, :, DK:DK + 1], 1.0).then_inc(ones_set, 1)
                dve.wait_ge(loaded["wv"], 32)

                def v_evac(b):
                    dve.wait_ge(v_mm, b + 1)
                    nc.vector.tensor_tensor(
                        V[:, b * KT:(b + 1) * KT, :, 0:DK],
                        ps[:, 4 + b % 2, :].rearrange("p (j h d) -> p j h d", j=KT, h=H0),
                        bvB[:, :].rearrange("p (a h d) -> p a h d", a=1, h=H0).to_broadcast([P, KT, H0, DK]),
                        ALU.add).then_inc(v_out, 1)
                for b in range(2):
                    v_evac(b)
                dve.wait_ge(loaded["x1"], 16)
                for t in range(QT, NT):
                    st.mark(nc.vector.bn_stats(stats[:, t, :], X[:, t, :]))
                v_evac(2)
                st.wait()
                for t in range(QT, NT):
                    i = nc.vector.bn_aggr(mv[:, t, :], stats[:, t, :])
                i.then_inc(mv_ready, 1)
                dve.wait_ge(mv_ready, 2)
                for b in (3, 4):
                    v_evac(b)
                dve.wait_ge(rs_ready, 2)
                for t in range(QT, NT):
                    normed(t)
                    if t % 5 == 4:
                        v_evac(t // 5 + 5)
                dve.wait_ge(loaded["ident"], 16)
                nc.vector.tensor_copy(identb[:, :], identf[:, :]).then_inc(steps0, 1)
                dve.wait_ge(loaded["consts"], 16 * 11)
                dve.wait_ge(xn_ready, NT)
                nc.vector.tensor_tensor(X[:, :, :], X[:, :, :],
                                        boB[:, :].rearrange("p (a d) -> p a d", a=1).to_broadcast([P, NT, D]),
                                        ALU.add).then_inc(steps0, 1)
                for f, c in enumerate((-1.0 / (SQ * SK), -1.0 / SQ, 1.0 / (SQ * (SK - 1.0) * (SK / 2) ** 2))):
                    nc.vector.tensor_scalar(w1c[:, f, :], w1c[:, f, :], c, None, ALU.mult).then_inc(steps0, 1)
                dve.wait_ge(q_out, B)
                for b in range(B):
                    nc.vector.tensor_scalar(prodsel[:, b, :], sel[:, :], qsum[:, b:b + 1], ksum[:, b:b + 1],
                                            ALU.mult, ALU.mult).then_inc(steps0, 1)

    RB = ROWS + MAXROWS
    minv = [sb(f"minv{i}", [P, 2, PAIRS, QT]) for i in range(2)]
    bst = sb("bst", [P, H0 * QT, 6])
    e1 = [sb(f"e1_{i}", [P, QT, SK]) for i in range(4)]
    e2 = [sb(f"e2_{i}", [P, KT, SQ]) for i in range(2)]
    maxp = sb("maxp", [P, 2, MAXROWS, PAIRS, QT], BF16)
    maxres = sb("maxres", [P, 2, PAIRS * QT])
    NROW = 2 * MAXROWS * PAIRS * QT
    maxpT = sb("maxpT", [NROW, P], BF16)
    vs = [sb(f"vs{i}", [P, H0 * QT]) for i in range(8)]
    h1, h2 = sb("h1", [64, H0]), sb("h2", [64, H0])
    logt, invt = sb("logt", [P, H0]), sb("invt", [P, H0])
    tscale = [sb(f"tscale{i}", [P, H0]) for i in range(2)]
    OT = [sb(f"OT{i}", [P, 2 * SQ]) for i in range(2)]
    rz = sb("rz", [P, 2, QT, 4])
    On = sb("On", [P, QT, D])
    OnT = sb("OnT", [P, QT * P])

    S1_BANKS, S2_BANK, O_BANK, M_BANK = (0, 2), 4, 6, 7
    def at(k, n):
        return k >= n if isinstance(k, int) else True

    def is_last(k):
        return isinstance(k, int) and k == B - 1

    def has(k, g):
        return at(k, 1) and not (isinstance(k, int) and k > B) if g >= 0 else at(k, 2)

    def buf(par, g):
        return 1 - par if g >= 0 else par

    def sync_step(sp, k, par):
        if at(k, 2):
            sp.wait_ge(s["s2_ready"], (k - 1) * H0)
        if at(k, 1):
            sp.wait_ge(s["stack2"], k * N2)
        sp.wait_ge(s["stack1"], (k + 1) * N1)
        sp.dma_start(K2[par][:, :, :], K1[par][:, :, :]).then_inc(s["stack2"], 16)
        for half in range(2):
            r = slice(64 * half, 64 * half + ROWS)
            sp.dma_start(Q2[par][r, :, :], Q1[par][r, :, :]).then_inc(s["stack2"], 16)
        if not is_last(k):
            sp.wait_ge(parts_ready, 2 * (k + 2))
            if at(k, 1):
                sp.wait_ge(s["s1_ready"], k * H0)
            for which in ("K", "Q"):
                load_stack1(sp, 1 - par, which)
        sp.wait_ge(s["maxp_out"], k + 1)
        for half in range(2):
            sp.dma_start(Q2[par][64 * half + ROWS:64 * half + RB, :, :],
                         maxpT[half * NROW // 2:(half + 1) * NROW // 2, :]).then_inc(s["max_rows"], 16)

    def gpsimd_step(pool, st, k, par):
        if not is_last(k):
            pool.wait_ge(s["stack1"], (k + 1) * N1)
            for full, parts, res in ((Kf, Kp, kres), (Qf, Qp, qres)):
                src = full[:, k + 1, :]
                st.done(nc.gpsimd.tensor_copy(parts[:, 0, :], src))
                st.done(nc.gpsimd.tensor_tensor(res[:, :], src, parts[:, 0, :], ALU.subtract))
                st.done(nc.gpsimd.tensor_copy(parts[:, 1, :], res[:, :]))
                nc.gpsimd.tensor_tensor(parts[:, 2, :], res[:, :], parts[:, 1, :], ALU.subtract).then_inc(parts_ready, 1)
        if at(k, 2):
            pool.wait_ge(s["pv_done"], (k - 1) * H0)
        nc.gpsimd.tensor_copy(Vw[par][:, :, :, 0:DK + 1].rearrange("p j h c -> p (j h) c"),
                              V[:, k * KT:(k + 1) * KT, :, :].rearrange("p j h c -> p (j h) c")).then_inc(s["v_ready"], 1)

    def tensor_step(pe, k, par):
        first, temper = not (isinstance(k, int) and k >= B), has(k, 0)
        if isinstance(k, int) and k == 0:
            score1(pe, 0, par, 0)
        for h in range(LAG + 1 if isinstance(k, int) and k > B else H0):
            g = h - LAG
            if first and h + 1 < H0:
                score1(pe, k, par, h + 1)
            if first and h + 1 == H0 and not is_last(k):
                score1(pe, k + 1, 1 - par, 0)
            if temper and h == 0:
                maxima_transpose(pe, k)
            if temper and h == 1:
                temperature_mm1(pe, k, par)
            if has(k, g):
                score2(pe, k, par, g)
            if temper and h == 2:
                temperature_mm2(pe, k)
            if has(k, g - 1):
                values(pe, k, par, g - 1)
            if temper and h == 2:
                temperature_mm3(pe, k)
            if at(k, 2) and h == LAG + 2:
                output_transpose(pe, k, 1)
            if at(k, 2) and h == LAG + 4:
                normed_transpose(pe, k)
            if at(k, 2) and h == LAG + 6:
                project_mm(pe, k)
            if temper and h == LAG + 10:
                output_transpose(pe, k, 0)

    def maxima_transpose(pe, k):
        pe.wait_ge(s["maxp_ready"], k)
        if at(k, 2):
            pe.wait_ge(s["on_ready"], 2 * k - 3)
        nc.tensor.transpose(ps[0:NROW, M_BANK, 0:64].bitcast(BF16),
                            maxp[:, :, :, :, :].rearrange("p a b c d -> p (a b c d)"),
                            identb[:, :]).then_inc(s["maxp_mm"], 1)

    def score1(pe, k, par, h):
        base, pair = 64 * (h % 2), h // 2
        if h == 0:
            pe.wait_ge(s["stack1"], (k + 1) * N1)
        if h >= 2 or at(k, 1):
            pe.wait_ge(s["e1_ready"], k * H0 + h - 1)
        for q in range(QT):
            mm = nc.tensor.matmul(ps[:, S1_BANKS[h % 2] + q, :], Q1[par][base:base + ROWS, pair, q * P:(q + 1) * P],
                                  K1[par][base:base + ROWS, pair, :], start=True, stop=True)
        mm.then_inc(s["s1_ready"], 1)

    def score2(pe, k, par, g):
        base, pair = 64 * (g % 2), g % H0 // 2
        if g == 0:
            pe.wait_ge(s["stack2"], k * N2)
            pe.wait_ge(s["max_rows"], k * NM)
        if g >= 1 or at(k, 2):
            pe.wait_ge(s["e2_ready"], (k - 1) * H0 + g)
        for j in range(KT):
            mm = nc.tensor.matmul(ps[:, S2_BANK + j // 2, (j % 2) * SQ:(j % 2 + 1) * SQ],
                                  K2[buf(par, g)][base:base + RB, pair, j * P:(j + 1) * P],
                                  Q2[buf(par, g)][base:base + RB, pair, :], start=True, stop=True)
        mm.then_inc(s["s2_ready"], 1)

    def values(pe, k, par, g):
        pe.wait_ge(s["e2_ready"], (k - 1) * H0 + g + 1)
        if g == 0:
            pe.wait_ge(s["v_ready"], k)
        if g % 8 == 0 and (g or at(k, 2)):
            pe.wait_ge(s["ot_out"], 2 * (k - 1) + g // 8)
        r, c = 32 * (g % 4), (g // 4) % 2 * SQ
        for j in range(KT):
            mm = nc.tensor.matmul(ps[r:r + 32, O_BANK, c:c + SQ], Vw[buf(par, g)][:, j, g % H0, :], e2[g % 2][:, j, :],
                                  start=(j == 0), stop=(j == KT - 1))
        mm.then_inc(s["pv_done"], 1)

    def temperature_mm1(pe, k, par):
        pe.wait_ge(s["f_ready"], k)
        pe.wait_ge(s["maxp_out"], k)
        o = ps[0:64, M_BANK, 64:64 + H0]
        fmin = minv[1 - par][:, :, :, :].rearrange("p a b q -> p (a b) q")
        fvar = vs[7][:, :].rearrange("p (u q) -> p u q", q=QT)
        nc.tensor.matmul(o, w1c[:, 0, :], prodsel[:, k - 1, :] if isinstance(k, int) else
                         prodsel[:, bass.ds(k - 1, 1), :].rearrange("p a h -> p (a h)"), start=True, stop=False)
        for q in range(QT):
            nc.tensor.matmul(o, w1c[:, 1, :], fmin[:, :, q], start=False, stop=False)
            mm = nc.tensor.matmul(o, w1c[:, 2, :], fvar[:, :, q], start=False, stop=(q == QT - 1))
        mm.then_inc(s["m1_mm"], 1)

    def temperature_mm2(pe, k):
        pe.wait_ge(loaded["consts"], 16 * 11)
        pe.wait_ge(s["g1"], k)
        nc.tensor.matmul(ps[0:64, M_BANK, 96:96 + H0], w2T[:, :], h1[:, :], start=True, stop=True).then_inc(s["m2_mm"], 1)

    def temperature_mm3(pe, k):
        pe.wait_ge(loaded["consts"], 16 * 11)
        pe.wait_ge(s["g2"], k)
        nc.tensor.matmul(ps[:, M_BANK, 128:128 + H0], w3c[:, :], h2[:, :], start=True, stop=True).then_inc(s["m3_mm"], 1)

    def output_transpose(pe, k, half):
        pe.wait_ge(s["ot_out"], 2 * k - 1 - half)
        if half and isinstance(k, int) and k > B:
            pe.wait_ge(s["on_ready"], 2 * k - 3)
        elif half or not at(k, 2):
            pe.wait_ge(s["logt_ready"], k)
        else:
            pe.wait_ge(s["x_added"], k - 1)
        for i in range(4):
            mm = nc.tensor.transpose(ps[:, M_BANK, i * P:(i + 1) * P], OT[half][:, i * P:(i + 1) * P], identf[:, :])
        mm.then_inc(s["ot_mm"], 1)

    def normed_transpose(pe, k):
        pe.wait_ge(s["on_ready"], 2 * (k - 1))
        for q in range(QT):
            mm = nc.tensor.transpose(ps[:, M_BANK, q * P:(q + 1) * P], On[:, q, :], identf[:, :])
        mm.then_inc(s["on_mm"], 1)

    def project_mm(pe, k):
        pe.wait_ge(s["on_out"], k - 1)
        for q in range(QT):
            mm = nc.tensor.matmul(ps[:, M_BANK, q * P:(q + 1) * P], OnT[:, q * P:(q + 1) * P], woT[:, :],
                                  start=True, stop=True)
        mm.then_inc(s["wo_mm"], 1)

    def output_evac(act, k, half):
        act.wait_ge(s["pv_done"], (k - 1) * H0 + (0 if half else 8))
        if at(k, 2 + half):
            act.wait_ge(s["ot_mm"], 2 * k - 3 - half)
        nc.scalar.copy(OT[half][:, :], ps[:, O_BANK, :]).then_inc(s["ot_out"], 1)

    def scalar_step(act, k, par):
        first, temper = not (isinstance(k, int) and k >= B), has(k, 0)
        for h in range(LAG + 1 if isinstance(k, int) and k > B else H0):
            g = h - LAG
            if first:
                act.wait_ge(s["s1_min"], k * H0 + h + 1)
                if h >= 4 or at(k, 1):
                    act.wait_ge(s["e1_used"], k * H0 + h - 3)
                for q in range(QT):
                    a = nc.scalar.activation(e1[h % 4][:, q, :], ps[:, S1_BANKS[h % 2] + q, :], ACT.Exp, scale=-1.0,
                                             bias=minv[par][:, h % 2, h // 2, q:q + 1])
                a.then_inc(s["e1_ready"], 1)
            if temper and h == 0:
                act.wait_ge(s["maxp_mm"], k)
                if at(k, 2):
                    act.wait_ge(s["max_rows"], (k - 1) * NM)
                nc.scalar.copy(maxpT[:, :], ps[0:NROW, M_BANK, 0:64].bitcast(BF16)).then_inc(s["maxp_out"], 1)
            if at(k, 2) and h == LAG + 1:
                output_evac(act, k, 1)
            if temper and h == LAG + 9:
                output_evac(act, k, 0)
            if temper and h == LAG - 1:
                act.wait_ge(s["logt_ready"], k)
                nc.scalar.activation(invt[:, :], logt[:, :], ACT.Exp, scale=-1.0).then_inc(s["invt_ready"], 1)
            if has(k, g):
                act.wait_ge(s["s2_ready"], (k - 1) * H0 + g + 1)
                if g >= 2 or at(k, 2):
                    act.wait_ge(s["pv_done"], (k - 1) * H0 + g - 1)
                if g == 0:
                    act.wait_ge(s["t_ready"], k)
                c = (g % 2) * PAIRS + g % H0 // 2
                nc.scalar.activation(e2[g % 2][:, :, :].rearrange("p j q -> p (j q)"),
                                     ps[:, S2_BANK:S2_BANK + 2, :].rearrange("p a b -> p (a b)"), ACT.Exp,
                                     scale=tscale[buf(par, g)][:, c:c + 1]).then_inc(s["e2_ready"], 1)
            if temper and h == 1:
                act.wait_ge(s["m1_mm"], k)
                nc.scalar.activation(h1[:, :], ps[0:64, M_BANK, 64:64 + H0], ACT.Gelu, bias=b1c[:, :]).then_inc(s["g1"], 1)
                act.wait_ge(s["m2_mm"], k)
                nc.scalar.activation(h2[:, :], ps[0:64, M_BANK, 96:96 + H0], ACT.Gelu, bias=b2c[:, :]).then_inc(s["g2"], 1)

    def vector_step(dve, st, k, par):
        first, temper = not (isinstance(k, int) and k >= B), has(k, 0)
        if isinstance(k, int) and k == 0:
            row_min(dve, k, par, 0)
        for h in range(H0):
            if first and h + 1 < H0:
                row_min(dve, k, par, h + 1)
            if first and h + 1 == H0:
                if not is_last(k):
                    row_min(dve, k + 1, 1 - par, 0)
                max_parts(dve, st, k, par)
            if first:
                dve.wait_ge(s["e1_ready"], k * H0 + h + 1)
                for q in range(QT):
                    i = nc.vector.bn_stats(bst[:, ((h % 2) * PAIRS + h // 2) * QT + q, :], e1[h % 4][:, q, :])
                i.then_inc(s["e1_used"], 1)
            if temper and h == LAG - 2:
                dve.wait_ge(s["m3_mm"], k)
                st.done(nc.vector.tensor_scalar(logt[:, :], ps[:, M_BANK, 128:128 + H0], b3c[:, :], LOG_T_MIN, ALU.add, ALU.max))
                nc.vector.tensor_scalar(logt[:, :], logt[:, :], LOG_T_MAX, None, ALU.min).then_inc(s["logt_ready"], 1)
            if temper and h == LAG - 1:
                dve.wait_ge(s["invt_ready"], k)
                nc.vector.tensor_scalar(tscale[1 - par][:, :], invt[:, :], -(DK ** 0.5) / 2.0, None, ALU.mult).then_inc(s["t_ready"], 1)
            if at(k, 2) and h == LAG + 3:
                output_norm(dve, st, k, 1)
            if at(k, 2) and h == LAG + 5:
                normed_copy(dve, k)
            if at(k, 2) and h == LAG + 7:
                output_add(dve, k)
            if temper and h == LAG + 10:
                output_norm(dve, st, k, 0)
        if first:
            variances(dve, st, k)

    def row_min(dve, k, par, h):
        dve.wait_ge(s["s1_ready"], k * H0 + h + 1)
        nc.vector.tensor_reduce(minv[par][:, h % 2, h // 2, :], ps[:, S1_BANKS[h % 2]:S1_BANKS[h % 2] + QT, :], AX.X,
                                ALU.min).then_inc(s["s1_min"], 1)

    def max_parts(dve, st, k, par):
        dve.wait_ge(s["s1_min"], (k + 1) * H0)
        m = [minv[par][:, a, :, :].rearrange("p c q -> p (c q)") for a in range(2)]
        part = [[maxp[:, a, i, :, :].rearrange("p c q -> p (c q)") for i in range(3)] for a in range(2)]
        for a in range(2):
            st.mark(nc.vector.tensor_scalar(part[a][0], m[a], -1.0, None, ALU.mult))
        st.wait()
        for a in range(2):
            st.mark(nc.vector.scalar_tensor_tensor(maxres[:, a, :], m[a], -1.0, part[a][0], ALU.mult, ALU.subtract))
        st.wait()
        for a in range(2):
            st.mark(nc.vector.tensor_copy(part[a][1], maxres[:, a, :]))
        st.wait()
        for a in range(2):
            i = nc.vector.tensor_tensor(part[a][2], maxres[:, a, :], part[a][1], ALU.subtract)
        i.then_inc(s["maxp_ready"], 1)

    def variances(dve, st, k):
        dve.wait_ge(s["e1_used"], (k + 1) * H0)
        m, d, m2, dd, r, r2, v, f = (x[:, :] for x in vs)
        st.mark(nc.vector.tensor_tensor(m, bst[:, :, 1], bst[:, :, 4], ALU.add))
        st.mark(nc.vector.tensor_tensor(d, bst[:, :, 1], bst[:, :, 4], ALU.subtract))
        st.mark(nc.vector.tensor_tensor(m2, bst[:, :, 2], bst[:, :, 5], ALU.add))
        st.wait()
        st.mark(nc.vector.tensor_tensor(dd, d, d, ALU.mult))
        st.mark(nc.vector.reciprocal(r, m))
        st.wait()
        st.mark(nc.vector.scalar_tensor_tensor(v, dd, SK / 4.0, m2, ALU.mult, ALU.add))
        st.mark(nc.vector.tensor_tensor(r2, r, r, ALU.mult))
        st.wait()
        nc.vector.tensor_tensor(f, v, r2, ALU.mult).then_inc(s["f_ready"], 1)

    def output_norm(dve, st, k, half):
        dve.wait_ge(s["ot_mm"], 2 * k - 1 - half)
        o = ps[:, M_BANK, :].rearrange("p (c q h r) -> p c q h r", c=2, q=QT, h=4)
        for q in range(QT):
            st.mark(nc.vector.reciprocal(rz[:, :, q, :], o[:, :, q, :, DK]))
        st.wait()
        if half == 0 and at(k, 2):
            dve.wait_ge(s["on_mm"], k - 1)
        for q in range(QT):
            i = nc.vector.tensor_tensor(
                On[:, q, half * 64:half * 64 + 64].rearrange("p (c h d) -> p c h d", c=2, h=4), o[:, :, q, :, 0:DK],
                rz[:, :, q, :].rearrange("p c (h a) -> p c h a", a=1).to_broadcast([P, 2, 4, DK]), ALU.mult)
        i.then_inc(s["on_ready"], 1)

    def normed_copy(dve, k):
        dve.wait_ge(s["on_mm"], k - 1)
        nc.vector.tensor_copy(OnT[:, :], ps[:, M_BANK, 0:QT * P]).then_inc(s["on_out"], 1)

    def output_add(dve, k):
        dve.wait_ge(s["wo_mm"], k - 1)
        xs = X[:, bass.ds((k - 2) * QT, QT), :]
        nc.vector.tensor_tensor(xs, xs, ps[:, M_BANK, 0:QT * P].rearrange("p (q d) -> p q d", q=QT),
                                ALU.add).then_inc(s["x_added"], 1)

    with nc.Block() as block:
        @block.sync
        def _(sp):
            sp.dma_start(env["W1"][:, :, :], dram["eW1"].rearrange("e d f -> d e f")).then_inc(env["w_loaded"], 16)
            sp.dma_start(env["W2"][:, :, :, :].rearrange("p e c d -> p (e c) d"),
                         dram["eW2"].rearrange("e (c p) d -> p (e c) d", p=P)).then_inc(env["w_loaded"], 16)
            for k in range(B):
                sync_step(sp, k, k % 2)

        @block.gpsimd
        def _(pool):
            st = Steps(pool, s["pstep"])
            for k in range(B):
                gpsimd_step(pool, st, k, k % 2)
            pool.wait_ge(s["x_stats"], NT - QT)
            stream_scales(pool, st, env, 0, NT - QT, RMS_EPS, s["x_scales"])
            pool.wait_ge(s["x_stats"], NT)
            stream_scales(pool, st, env, NT - QT, NT, RMS_EPS, s["x_scales"])

        @block.tensor
        def _(pe):
            for k in (0, 1):
                tensor_step(pe, k, k % 2)
            with pe.Fori(2, B - 2, 2) as i:
                tensor_step(pe, i, 0)
                tensor_step(pe, i + 1, 1)
            for k in (B - 2, B - 1, B):
                tensor_step(pe, k, k % 2)
            tensor_step(pe, B + 1, (B + 1) % 2)
            output_transpose(pe, B + 1, 1)
            normed_transpose(pe, B + 1)
            project_mm(pe, B + 1)

        @block.scalar
        def _(act):
            for k in (0, 1):
                scalar_step(act, k, k % 2)
            with act.Fori(2, B - 2, 2) as i:
                scalar_step(act, i, 0)
                scalar_step(act, i + 1, 1)
            for k in (B - 2, B - 1, B):
                scalar_step(act, k, k % 2)
            scalar_step(act, B + 1, (B + 1) % 2)
            output_evac(act, B + 1, 1)

        @block.vector
        def _(dve):
            st = Steps(dve, s["dstep"])
            for k in (0, 1):
                vector_step(dve, st, k, k % 2)
            with st.loop(2, B - 2, 2, 2 * 18) as i:
                vector_step(dve, st, i, 0)
                vector_step(dve, st, i + 1, 1)
            for k in (B - 2, B - 1, B):
                vector_step(dve, st, k, k % 2)
            dve.wait_ge(s["x_added"], B - 1)
            stream_stats(dve, st, env, range(NT - QT), s["x_stats"])
            output_norm(dve, st, B + 1, 1)
            normed_copy(dve, B + 1)
            output_add(dve, B + 1)
            dve.wait_ge(s["x_added"], B)
            stream_stats(dve, st, env, range(NT - QT, NT), s["x_stats"])
            dve.wait_ge(s["x_scales"], 1)
            for t in range(NT - QT):
                stream_normed(env, t)
            dve.wait_ge(s["x_scales"], 2)
            for t in range(NT - QT, NT):
                stream_normed(env, t)


def experts0(env, stack):
    nc, dram, sem, X, ps = env["nc"], env["dram"], env["sem"], env["X"], env["ps"]
    identf, stats, mv, rstd, rtmp, mhalf = (env[n] for n in ("identf", "stats", "mv", "rstd", "rtmp", "mhalf"))
    c = env["c"]

    def sb(name, shape, dt=F32):
        return env["sb"](stack, name, shape, dt)

    W1, W2 = env["W1"], env["W2"]
    b1t = sb("b1t", [P, E0 * FC])
    b2t = sb("b2t", [E0, D])
    rmsw = sb("rmsw", [P, 1])
    gwT = sb("gwT", [P, E0])
    rank = sb("rank", [P, E0])
    Xn = env["Xn"]
    XnT = [sb(f"XnTB{i}", [P, NT * P], F32R) for i in range(2)]
    gwp = [sb(f"gwp{i}", [P, E0], F32R) for i in range(2)]
    W1p = [sb(f"W1p{i}", [P, E0, F0], F32R) for i in range(2)]
    L, ex, key, G = (sb(n, [P, NT, E0]) for n in ("LB", "exB", "keyB", "GB"))
    mx, den, kmx = (sb(n, [P, NT]) for n in ("mxB", "denB", "kmxB"))
    GT = sb("GTB", [E0, 512])
    hT = [sb(f"hTB{i}", [P, 512]) for i in range(8)]
    s = {n: sem("b_" + n) for n in (
        "small", "bias_added", "steps", "xt_low", "rw_high", "rw_low", "lt_mm", "lt_out", "w1_high", "w1_low", "psteps", "t_mm", "xt", "l_mm", "l_out", "shifted", "exps",
        "gates", "gt_mm", "gt_out", "bias_mm", "h_mm", "h_out", "y_mm", "y_added", "c_stats", "c_scales", "c_norm", "c_mm",
        "c_out", "x_stats", "x_scales", "inv", "wo_cleared")}

    HB, YB, GB_BANK, BB_BANK = 0, 4, 6, 7

    def load_layer1(sp):
        d = env["d"]
        sp.dma_start(c["CN"][:, :, :], dram["ctx"].rearrange("(t p) d -> p t d", p=P)).then_inc(c["loaded_ctx"], 16)
        for n, m in (("gx", "lnx_g"), ("bx", "lnx_b"), ("gl", "lnl_g"), ("bl", "lnl_b")):
            sp.dma_start(c[n][:, :], dram[m]).then_inc(c["loaded_norm"], 16)
        sp.dma_start(c["maskB"][:, :], dram["mask"].to_broadcast([P, B * SK // 4])).then_inc(c["loaded_mask"], 16)
        sp.dma_start(c["maskc"][:, :], dram["maskc"]).then_inc(c["loaded_mask"], 16)
        for n, m in (("wq", "wq1"), ("wkv", "wkv1")):
            sp.dma_start(c[n][:, :], dram[m]).then_inc(c["loaded_w"], 16)
        for n, m in (("gout", "lno_g"), ("bout", "lno_b")):
            sp.dma_start(c[n][:, :], dram[m].to_broadcast([P, D])).then_inc(c["loaded_w"], 16)
        for t, n in ((d["rw"], "router_w"), (d["rank"], "rank")):
            sp.dma_start(t[:, :], dram[n]).then_inc(d["loaded_small"], 16)
        sp.dma_start(d["biasB"][:, :], dram["expert_bias"].to_broadcast([P, E1])).then_inc(d["loaded_small"], 16)
        for n in ("w1", "w3", "w2"):
            sp.dma_start(d[n][:, 0:E1, :], dram[n].rearrange("e d f -> d e f")).then_inc(d["loaded_w"], 16)
            sp.dma_start(d[n][:, E1, :], dram["s" + n]).then_inc(d["loaded_w"], 16)
        sp.wait_ge(s["wo_cleared"], 1)
        sp.dma_start(c["wo"][0:DH, :, 0:D], dram["wo1"].rearrange("(h p) d -> p h d", p=DH)).then_inc(c["loaded_w"], 16)

    def over_experts(a):
        return a[:, :].rearrange("p (t a) -> p t a", a=1).to_broadcast([P, NT, E0])

    with nc.Block() as block:
        @block.sync
        def _(sp):
            for t, n in ((rmsw, "rms_w"), (gwT, "gate_wT"), (rank, "rank"), (b1t, "eb1"), (b2t, "eb2")):
                sp.dma_start(t[:, :], dram[n]).then_inc(s["small"], 16)
            load_layer1(sp)

        @block.tensor
        def _(pe):
            for g in range(4):
                for i in range(4):
                    mm = nc.tensor.transpose(ps[:, g, i * P:(i + 1) * P], Xn[:, 4 * g + i, :], identf[:, :])
                mm.then_inc(s["t_mm"], 1)
            router_products(pe, nc, env, s, gwp, XnT, (YB, YB + 1), GB_BANK, hT[4:8])
            pe.wait_ge(env["w_loaded"], 32)

            def gates_transpose(i):
                pe.wait_ge(s["gates"], 1)
                for t in range(4):
                    mm = nc.tensor.transpose(ps[0:E0, GB_BANK, t * P:(t + 1) * P], G[:, 4 * i + t, :], identf[:, :])
                mm.then_inc(s["gt_mm"], 1)

            def bias_mm(i):
                pe.wait_ge(s["gt_out"], i + 1)
                if i:
                    pe.wait_ge(s["bias_added"], i)
                for t in range(4):
                    mm = nc.tensor.matmul(ps[:, BB_BANK, t * P:(t + 1) * P], GT[:, t * P:(t + 1) * P], b2t[:, :],
                                          start=True, stop=True)
                mm.then_inc(s["bias_mm"], 1)

            def up(g, e):
                if isinstance(g, int) and g == 0:
                    pe.wait_ge(s["w1_low"], e + 1)
                for f in range(FC):
                    n = g * (E0 * FC) + e * FC + f
                    if not (isinstance(g, int) and g == 0 and e == 0):
                        pe.wait_ge(s["h_out"], n - FC + 1)
                    product(nc, ps[:, HB + f, :], lambda p: W1p[p][:, e, f * P:(f + 1) * P],
                            lambda p: XnT[p][:, bass.ds(g * 512, 512)]).then_inc(s["h_mm"], 1)

            def down(g, e):
                pe.wait_ge(s["h_out"], g * (E0 * FC) + e * FC + FC)
                if not (isinstance(g, int) and g == 0 and e < 2):
                    pe.wait_ge(s["y_added"], g * E0 + e - 1)
                for t in range(4):
                    for f in range(FC):
                        mm = nc.tensor.matmul(ps[:, YB + e % 2, t * P:(t + 1) * P], hT[(e % 2) * FC + f][:, t * P:(t + 1) * P],
                                              W2[:, e, f, :], start=(f == 0), stop=(f == FC - 1))
                mm.then_inc(s["y_mm"], 1)

            def group(g, context=False):
                up(g, 0)
                for e in range(E0):
                    if e + 1 < E0:
                        up(g, e + 1)
                    down(g, e)
                    if isinstance(g, int) and g == 0:
                        if 3 <= e < 7:
                            bias_mm(e - 3)
                        if 2 <= e < 6:
                            gates_transpose(e - 2)
                    if context:
                        pe.wait_ge(s["c_norm"], KT * (e + 1))
                        if e >= 2:
                            pe.wait_ge(s["c_out"], e - 1)
                        for j in range(KT):
                            mm = nc.tensor.transpose(ps[:, 6 + e % 2, j * P:(j + 1) * P], c["CN"][:, KT * e + j, :], identf[:, :])
                        mm.then_inc(s["c_mm"], 1)
            group(0)
            with pe.Fori(1, 3) as g:
                group(g)
            group(3, context=True)

        @block.scalar
        def _(act):
            act.wait_ge(s["small"], 16 * 5)
            for g in range(4):
                act.wait_ge(s["t_mm"], g + 1)
                nc.scalar.activation(XnT[0][:, g * 512:(g + 1) * 512], ps[:, g, :], ACT.Identity, scale=rmsw[:, :]).then_inc(s["xt"], 1)
            router_copies(act, nc, env, s, E0, (YB, YB + 1), hT[4:8])
            act.wait_ge(s["shifted"], 1)
            nc.scalar.activation(ex[:, :, :], ex[:, :, :], ACT.Exp).then_inc(s["exps"], 1)

            def context_out(b):
                act.wait_ge(s["c_mm"], b + 1)
                nc.scalar.activation(c["LT"][:, b, 0:SK], ps[:, 6 + b % 2, :], ACT.Identity, scale=c["gx"][:, :],
                                     bias=c["bx"][:, :]).then_inc(s["c_out"], 1)

            def group(g, context=False):
                for e in range(E0):
                    for f in range(FC):
                        act.wait_ge(s["h_mm"], g * (E0 * FC) + e * FC + f + 1)
                        if f == 0 and not (isinstance(g, int) and g == 0 and e < 2):
                            act.wait_ge(s["y_mm"], g * E0 + e - 1)
                        nc.scalar.activation(hT[(e % 2) * FC + f][:, :], ps[:, HB + f, :], ACT.Silu,
                                             bias=b1t[:, e * FC + f:e * FC + f + 1]).then_inc(s["h_out"], 1)
                    if isinstance(g, int) and g == 0 and 3 <= e < 7:
                        act.wait_ge(s["gt_mm"], e - 2)
                        nc.scalar.copy(GT[:, :], ps[0:E0, GB_BANK, :]).then_inc(s["gt_out"], 1)
                    if context and e:
                        context_out(e - 1)
            group(0)
            with act.Fori(1, 3) as g:
                group(g)
            act.wait_ge(c["loaded_norm"], 16 * 4)
            group(3, context=True)
            context_out(B - 1)

        @block.vector
        def _(dve):
            st = Steps(dve, s["steps"])
            dve.wait_ge(s["small"], 16 * 5)
            router_weights(dve, nc, s, gwT, gwp)
            for g in range(4):
                dve.wait_ge(s["xt"], g + 1)
                nc.vector.scalar_tensor_tensor(XnT[1][:, g * 512:(g + 1) * 512], ps[:, g, :], rmsw[:, :],
                                               XnT[0][:, g * 512:(g + 1) * 512].bitcast(F32), ALU.mult,
                                               ALU.subtract).then_inc(s["xt_low"], 1)
            rk = rank[:, :].rearrange("p (a e) -> p a e", a=1).to_broadcast([P, NT, E0])
            dve.wait_ge(s["l_mm"], 1)
            nc.vector.tensor_copy(L[:, :, :].rearrange("p t e -> p (t e)"), ps[:, GB_BANK, 0:NT * E0]).then_inc(s["l_out"], 1)
            dve.wait_ge(s["l_out"], 1)
            st.done(nc.vector.tensor_reduce(mx[:, :], L[:, :, :], AX.X, ALU.max))
            nc.vector.tensor_tensor(ex[:, :, :], L[:, :, :], over_experts(mx), ALU.subtract).then_inc(s["shifted"], 1)
            dve.wait_ge(s["small"], 16 * 5)
            st.done(nc.vector.tensor_tensor(key[:, :, :], L[:, :, :], over_experts(mx), ALU.is_equal))
            st.done(nc.vector.tensor_tensor(key[:, :, :], key[:, :, :], rk, ALU.mult))
            st.done(nc.vector.tensor_reduce(kmx[:, :], key[:, :, :], AX.X, ALU.max))
            st.done(nc.vector.tensor_tensor(key[:, :, :], key[:, :, :], over_experts(kmx), ALU.is_equal))
            dve.wait_ge(s["exps"], 1)
            st.done(nc.vector.tensor_reduce(den[:, :], ex[:, :, :], AX.X, ALU.add))
            st.done(nc.vector.reciprocal(den[:, :], den[:, :]))
            nc.vector.tensor_tensor(G[:, :, :], key[:, :, :], over_experts(den), ALU.mult).then_inc(s["gates"], 1)
            dve.wait_ge(s["gates"], 1)

            def group(g):
                for e in range(E0):
                    if g == 1:
                        tiles = range(KT * e, KT * (e + 1))
                        for t in tiles:
                            st.mark(nc.vector.bn_stats(stats[:, NT + t, :], c["CN"][:, t, :]))
                        st.wait()
                        for t in tiles:
                            nc.vector.bn_aggr(mv[:, t, :], stats[:, NT + t, :]).then_inc(s["c_stats"], 1)
                    if g == 3:
                        for t in range(KT * e, KT * (e + 1)):
                            nc.vector.tensor_scalar(c["CN"][:, t, :], c["CN"][:, t, :], mv[:, t, 0:1], rstd[:, t:t + 1],
                                                    ALU.subtract, ALU.mult).then_inc(s["c_norm"], 1)
                    dve.wait_ge(s["y_mm"], g * E0 + e + 1)
                    if g or e:
                        dve.wait_ge(s["y_added"], g * E0 + e)
                    if g == 3 and e < 6:
                        if e % 2 == 0:
                            dve.wait_ge(s["x_scales"], e // 2 + 1)
                        for t in (2 * e, 2 * e + 1):
                            stream_normed(env, t)
                    if (g, e) in ((0, 4), (1, 0)):
                        dve.wait_ge(s["bias_added"], 1 if g == 0 else 4)
                    for t in range(4):
                        x = X[:, 4 * g + t, :]
                        i = nc.vector.scalar_tensor_tensor(x, ps[:, YB + e % 2, t * P:(t + 1) * P], G[:, 4 * g + t, e:e + 1], x,
                                                           ALU.mult, ALU.add)
                    i.then_inc(s["y_added"], 1)
                    if g == 0 and 3 <= e < 7:
                        b = e - 3
                        dve.wait_ge(s["bias_mm"], b + 1)
                        dve.wait_ge(s["y_added"], e + 1)
                        nc.vector.tensor_tensor(X[:, 4 * b:4 * b + 4, :], X[:, 4 * b:4 * b + 4, :],
                                                ps[:, BB_BANK, :].rearrange("p (t d) -> p t d", t=4), ALU.add).then_inc(s["bias_added"], 1)

            def tail(g):
                dve.wait_ge(s["y_added"], (g + 1) * E0)
                stream_stats(dve, st, env, range(4 * g, 4 * g + 4), s["x_stats"])
            for g in range(4):
                if g == 1:
                    dve.wait_ge(c["loaded_ctx"], 16)
                if g == 2:
                    dve.wait_ge(c["loaded_mask"], 32)
                    nc.vector.tensor_scalar(c["invB"][:, :], c["maskB"][:, :].bitcast(U8), 0.0, None, ALU.is_equal).then_inc(s["inv"], 1)
                if g == 3:
                    dve.wait_ge(s["c_scales"], 1)
                group(g)
                tail(g)

        @block.gpsimd
        def _(pool):
            st = Steps(pool, s["psteps"])
            pool.wait_ge(env["w_loaded"], 32)
            for e in range(E0):
                nc.gpsimd.tensor_copy(W1p[0][:, e, :], W1[:, e, :]).then_inc(s["w1_high"], 1)
                pool.wait_ge(s["w1_high"], e + 1)
                nc.gpsimd.tensor_tensor(W1p[1][:, e, :], W1[:, e, :], W1p[0][:, e, :].bitcast(F32),
                                        ALU.subtract).then_inc(s["w1_low"], 1)
            pool.wait_ge(s["w1_low"], E0)
            wo = c["wo"]
            st.done(nc.gpsimd.memset(wo[:, :, :], 0.0))
            nc.gpsimd.memset(wo[DH:DH + 1, :, D:D + 1], 1.0).then_inc(s["wo_cleared"], 1)
            pool.wait_ge(s["wo_cleared"], 1)
            pool.wait_ge(c["loaded_mask"], 32)
            st.done(nc.gpsimd.tensor_scalar(c["mask01"][:, :], c["maskc"][:, :].bitcast(U8), 0.0, None, ALU.add))
            pool.wait_ge(c["loaded_w"], 16 * 5)
            for n in ("wq", "wkv"):
                w, (high, low) = c[n], c[n + "p"]
                st.done(nc.gpsimd.tensor_copy(high[:, :], w[:, :]))
                st.done(nc.gpsimd.tensor_tensor(low[:, :], w[:, :], high[:, :].bitcast(F32), ALU.subtract))
            for g in range(3):
                pool.wait_ge(s["x_stats"], 4 * (g + 1))
                stream_scales(pool, st, env, 4 * g, 4 * (g + 1), LN_EPS, s["x_scales"])
                if g == 1:
                    pool.wait_ge(s["x_scales"], g + 1)
                    pool.wait_ge(s["c_stats"], B * KT)
                    st.done(nc.gpsimd.tensor_scalar(rtmp[:, NT:NT + B * KT], mv[:, 0:B * KT, 1], LN_EPS, None, ALU.add))
                    nc.gpsimd.tensor_tensor(rstd[:, 0:B * KT], rtmp[:, NT:NT + B * KT], mhalf[:, 0:B * KT],
                                            ALU.pow).then_inc(s["c_scales"], 1)


def attention1_tensors(env, stack):
    c, sem = {}, env["sem"]

    def sb(name, shape, dt=F32):
        c[name] = env["sb"](stack, "c_" + name, shape, dt)
    sb("CN", [P, B * KT, D])
    sb("LT", [P, B, NK1])
    sb("wq", [P, INNER])
    sb("wkv", [P, 2 * INNER])
    for n, w in (("wq", INNER), ("wkv", 2 * INNER)):
        c[n + "p"] = [env["sb"](stack, f"c_{n}p{i}", [P, w], F32R) for i in range(2)]
    sb("wo", [DH + 1, H1, D + 1])
    for n in ("gout", "bout"):
        sb(n, [P, D])
    for n in ("gx", "bx", "gl", "bl"):
        sb(n, [P, 1])
    sb("maskB", [P, B * SK // 4], I32)
    sb("maskc", [P, B * KT // 4], I32)
    sb("invB", [P, B * SK], U8)
    sb("mask01", [P, B * KT])
    for n in ("loaded_ctx", "loaded_norm", "loaded_mask", "loaded_w"):
        c[n] = sem("c_" + n)
    env["c"] = c
    d = {"rw": env["sb"](stack, "rw", [P, E1]), "rank": env["sb"](stack, "rankD", [P, E1]),
         "biasB": env["sb"](stack, "biasB", [P, E1])}
    for n in ("w1", "w3", "w2"):
        d[n] = env["sb"](stack, n + "D", [P, E1 + 1, D])
    for n in ("loaded_small", "loaded_w"):
        d[n] = sem("d_" + n)
    env["d"] = d


def attention1(env, stack):
    nc, dram, sem, X, ps = env["nc"], env["dram"], env["sem"], env["X"], env["ps"]
    identf, stats, mv, rstd, rtmp, mhalf = (env[n] for n in ("identf", "stats", "mv", "rstd", "rtmp", "mhalf"))

    def sb(name, shape, dt=F32):
        return env["sb"](stack, name, shape, dt)

    c = env["c"]
    LT, wo, gout, bout, mask01, invB = (c[n] for n in ("LT", "wo", "gout", "bout", "mask01", "invB"))
    wq, wkv = c["wqp"], c["wkvp"]
    s0 = s = {n: sem("c_" + n) for n in ("x_scales", "xn", "t_mm", "lt", "filled")}

    def latents_mm(g, bank):
        for i in range(4):
            mm = nc.tensor.transpose(ps[:, bank, i * P:(i + 1) * P], env["Xn"][:, 4 * g + i, :], identf[:, :])
        mm.then_inc(s0["t_mm"], 1)

    def latents_out(act, g, bank):
        act.wait_ge(s0["t_mm"], g + 1)
        nc.scalar.activation(LT[:, 2 * g:2 * g + 2, SK:NK1], ps[:, bank, :].rearrange("p (a q) -> p a q", a=2),
                             ACT.Identity, scale=c["gl"][:, :], bias=c["bl"][:, :]).then_inc(s0["lt"], 1)

    def fill(dve, b):
        dve.wait_ge(s0["lt"], b // 2 + 1)
        nc.vector.copy_predicated(LT[:, b, 0:SK], invB[:, b * SK:(b + 1) * SK],
                                  LT[:, b, SK:SK + 1].to_broadcast([P, SK])).then_inc(s0["filled"], 1)

    LAST, FILLED = NT // 4 - 1, 2
    with nc.Block() as block:
        @block.tensor
        def _(pe):
            for g in range(LAST):
                latents_mm(g, g)

        @block.scalar
        def _(act):
            act.wait_ge(c["loaded_norm"], 16 * 4)
            for g in range(LAST):
                latents_out(act, g, g)

        @block.vector
        def _(dve):
            for b in range(FILLED):
                fill(dve, b)

    LTb = [sb(f"LTb{i}", [P, NK1], F32R) for i in range(2)]
    mkb = sb("mkb", [P, KT])
    Q = [sb(f"Qc{i}", [P, INNER // P, SQ], F32R) for i in range(2)]
    K = [sb(f"Kc{i}", [P, INNER // P, NK1], F32R) for i in range(2)]

    places = {n: [env[n][tuple([slice(None)] * r)].rearrange(p), 0] for n, r, p in
              (("W1", 3, "p e f -> p (e f)"), ("W2", 4, "p e c d -> p (e c d)"))}
    places["CN"] = [c["CN"][:, :, :].rearrange("p t d -> p (t d)"), 0]

    def over(place, pattern, **dims):
        size, (ap, at_) = int(np.prod(list(dims.values()))), places[place]
        places[place][1] += size
        return ap[:, at_:at_ + size].rearrange(pattern, **dims)
    V = over("W2", "p (j h d) -> p j h d", j=KJ, h=H1, d=DH + 1)
    mn, rz = sb("mnc", [P, 2]), sb("rzc", [P, QT])
    e = [over("W1", "p (a k) -> p a k", a=2, k=NK1 // 2) for _ in range(2)]
    eT = [over("CN", "p (j q) -> p j q", j=KJ, q=SQ) for _ in range(2)]
    OT = [sb(f"OTc{i}", [DH + 1, SQ]) for i in range(2)]
    y, yn, xs = (over("W1", "p (q d) -> p q d", q=QT, d=D) for _ in range(3))
    xsmv, xsr = sb("xsmv", [P, QT, 2]), sb("xsr", [P, QT])
    T_BANK, O_BANK, Y_BANK = 4, 6, 7
    SCALE = 1.0 / DH
    UNITS, NJOB = H1 * QT, 8
    s = {n: sem("c1_" + n) for n in (
        "first_high", "batch", "ones", "job_mm", "job_act", "job_dve", "s_mm", "row_min", "exp", "t_mm", "t_dve", "t_act",
        "pv_mm", "ot", "wo_mm", "y_added", "ystat", "yr", "yn", "x_out", "xstat", "xr", "xn",
        "dstep", "pstep")}

    def at(k, n):
        return k >= n if isinstance(k, int) else True

    def peeled(k, n):
        return isinstance(k, int) and k == n

    JOBS = (("Q", 0), ("K", 0), ("V", 0), ("K", 1), ("K", 2), ("V", 1), ("V", 2), ("K", 3))
    JOB_BANK = (2, 4, 0, 2, 4, 0, 2, O_BANK)

    def job_mm(pe, k, i):
        if JOB_BANK[i] == O_BANK and at(k, 1):
            pe.wait_ge(s["ot"], k * H1)
            pe.wait_ge(s["y_added"], k * H1)
        before = [j for j in range(i) if JOB_BANK[j] == JOB_BANK[i]]
        if before:
            pe.wait_ge(s["job_act"], k * NJOB + before[-1] + 1)
            pe.wait_ge(s["job_dve"], k * NJOB + before[-1] + 1)
        bank, (kind, m) = JOB_BANK[i], JOBS[i]
        for a in range(2):
            if kind == "V":
                j = 2 * m + a
                mm = product(nc, ps[:, bank + a, :], lambda p: LTb[p][:, j * P:(j + 1) * P], lambda p: wkv[p][:, INNER:2 * INNER])
            elif kind == "Q":
                for m in (2 * a, 2 * a + 1):
                    mm = product(nc, ps[:, bank + a, (m % 2) * SQ:(m % 2 + 1) * SQ], lambda p: wq[p][:, m * P:(m + 1) * P],
                                 lambda p: LTb[p][:, SK:NK1])
            else:
                mm = product(nc, ps[:, bank + a, 0:NK1 // 2], lambda p: wkv[p][:, m * P:(m + 1) * P],
                             lambda p: LTb[p][:, a * NK1 // 2:(a + 1) * NK1 // 2])
        mm.then_inc(s["job_mm"], 1)

    def job_views(i):
        bank, (kind, m) = JOB_BANK[i], JOBS[i]
        if kind == "Q":
            return (ps[:, bank:bank + 2, :], *(Q[p][:, :, :].rearrange("p (a c) q -> p a (c q)", a=2) for p in range(2)))
        return (ps[:, bank:bank + 2, 0:NK1 // 2], *(K[p][:, m, :].rearrange("p (a k) -> p a k", a=2) for p in range(2)))

    def job_act(act, k, i):
        act.wait_ge(s["job_mm"], k * NJOB + i + 1)
        kind, m = JOBS[i]
        if kind == "V":
            j = 2 * m
            ins = nc.scalar.activation(V[:, j, :, 0:DH], ps[:, JOB_BANK[i], :].rearrange("p (h d) -> p h d", h=H1), ACT.Copy,
                                       scale=mkb[:, j:j + 1] if j < KT else 1.0)
        else:
            src, high, _ = job_views(i)
            ins = nc.scalar.activation(high, src, ACT.Copy, scale=-SCALE if kind == "Q" else 1.0)
        ins.then_inc(s["job_act"], 1)

    def job_dve(dve, k, i):
        kind, m = JOBS[i]
        if kind == "V":
            j = 2 * m + 1
            dve.wait_ge(s["job_mm"], k * NJOB + i + 1)
            ins = nc.vector.tensor_scalar(V[:, j, :, 0:DH], ps[:, JOB_BANK[i] + 1, :].rearrange("p (h d) -> p h d", h=H1),
                                          mkb[:, j:j + 1] if j < KT else 1.0, None, ALU.mult)
        else:
            dve.wait_ge(s["job_act"], k * NJOB + i + 1)
            src, high, lo = job_views(i)
            if kind == "Q":
                ins = nc.vector.scalar_tensor_tensor(lo, src, -SCALE, high.bitcast(F32), ALU.mult, ALU.subtract)
            else:
                ins = nc.vector.tensor_tensor(lo, src, high.bitcast(F32), ALU.subtract)
        ins.then_inc(s["job_dve"], 1)

    def score(pe, k, u):
        h, q = u // 2, u % 2
        r = slice(64 * (h % 2), 64 * (h % 2) + DH)
        if u == 0:
            pe.wait_ge(s["job_act"], k * NJOB + 6)
            pe.wait_ge(s["job_dve"], k * NJOB + 6)
        elif u == 1:
            pe.wait_ge(s["job_act"], k * NJOB + 7)
            pe.wait_ge(s["job_dve"], k * NJOB + 7)
        else:
            pe.wait_ge(s["exp"], k * UNITS + u - 1)
        for a in range(2):
            mm = product(nc, ps[:, 2 * (u % 2) + a, 0:NK1 // 2], lambda p: Q[p][r, h // 2, q * P:(q + 1) * P],
                         lambda p: K[p][r, h // 2, a * NK1 // 2:(a + 1) * NK1 // 2])
        mm.then_inc(s["s_mm"], 1)

    def transpose(pe, k, u):
        pe.wait_ge(s["exp"], k * UNITS + u + 1)
        if u:
            pe.wait_ge(s["t_dve"], k * UNITS + u)
            pe.wait_ge(s["t_act"], k * UNITS + u)
        for j in range(KJ):
            mm = nc.tensor.transpose(ps[:, T_BANK + j // 4, (j % 4) * P:(j % 4 + 1) * P],
                                     e[u % 2][:, j // 3, (j % 3) * P:(j % 3 + 1) * P], identf[:, :])
            if j == 3:
                mm.then_inc(s["t_mm"], 1)
        mm.then_inc(s["t_mm"], 1)

    def values(pe, k, h, half):
        if half == 0:
            if h == 0:
                pe.wait_ge(s["ones"], k + 1)
            pe.wait_ge(s["t_dve"], k * UNITS + 2 * h + 2)
            pe.wait_ge(s["t_act"], k * UNITS + 2 * h + 2)
            if h or at(k, 1):
                pe.wait_ge(s["ot"], k * H1 + h)
        for j in range(3 * half, 3 * half + 3):
            mm = nc.tensor.matmul(ps[0:DH + 1, O_BANK, 0:SQ], V[:, j, h, :], eT[h % 2][:, j, :],
                                  start=(j == 0), stop=(j == KJ - 1))
        if half:
            mm.then_inc(s["pv_mm"], 1)

    def project_mm(pe, k, h):
        pe.wait_ge(s["ot"], k * H1 + h + 1)
        if peeled(k, 0) and h == 0:
            pe.wait_ge(s0["lt"], LAST + 1)
        if h or at(k, 1):
            pe.wait_ge(s["y_added"], k * H1 + h)
        for q in range(QT):
            mm = nc.tensor.matmul(ps[:, Y_BANK, q * (D + 1):(q + 1) * (D + 1)], OT[h % 2][:, q * P:(q + 1) * P], wo[:, h, :],
                                  start=True, stop=True)
        mm.then_inc(s["wo_mm"], 1)

    def tensor_step(pe, k):
        pe.wait_ge(s["batch"], 2 * (k + 1))
        for i in range(0 if peeled(k, 0) else 1, NJOB):
            if i == NJOB - 1:
                score(pe, k, 0)
                score(pe, k, 1)
            job_mm(pe, k, i)
            if i == 1 and at(k, 1):
                project_mm(pe, k - 1, H1 - 1)
        for u in range(UNITS):
            if 0 < u < UNITS - 1:
                score(pe, k, u + 1)
            transpose(pe, k, u)
            if u == 2:
                pe.wait_ge(s["job_act"], (k + 1) * NJOB)
                pe.wait_ge(s["job_dve"], (k + 1) * NJOB)
            if peeled(k, 0) and u == 2:
                pe.wait_ge(s0["xn"], 4)
                latents_mm(LAST, Y_BANK)
            if u >= 2:
                values(pe, k, (u - 2) // 2, u % 2)
            if u >= 4 and u % 2 == 0:
                project_mm(pe, k, (u - 4) // 2)
        if not peeled(k, B - 1):
            pe.wait_ge(s["batch"], 2 * (k + 2))
            job_mm(pe, k + 1, 0)
        project_mm(pe, k, H1 - 2)
        for half in range(2):
            values(pe, k, H1 - 1, half)

    def scalar_step(act, k):
        act.wait_ge(s["batch"], 2 * (k + 1))
        for i in range(0 if peeled(k, 0) else 1, NJOB - 1):
            job_act(act, k, i)

        def exps(u):
            act.wait_ge(s["row_min"], k * UNITS + u + 1)
            if u >= 2:
                act.wait_ge(s["t_mm"], 2 * (k * UNITS + u - 1))
            nc.scalar.activation(e[u % 2][:, :, :], ps[:, 2 * (u % 2):2 * (u % 2) + 2, 0:NK1 // 2], ACT.Exp, scale=-1.0,
                                 bias=mn[:, u % 2:u % 2 + 1]).then_inc(s["exp"], 1)
        exps(0)
        for u in range(UNITS):
            if u + 1 < UNITS:
                exps(u + 1)
            act.wait_ge(s["t_mm"], 2 * (k * UNITS + u + 1))
            nc.scalar.copy(eT[u // 2 % 2][:, 4:6, (u % 2) * P:(u % 2 + 1) * P],
                           ps[:, T_BANK + 1, 0:2 * P].rearrange("p (j q) -> p j q", q=P)).then_inc(s["t_act"], 1)
            if u == 0:
                job_act(act, k, NJOB - 1)
            if peeled(k, 0) and u == 2:
                latents_out(act, LAST, Y_BANK)
            if u >= 3 and u % 2:
                output_copy(act, k, (u - 3) // 2)
        if not peeled(k, B - 1):
            job_act(act, k + 1, 0)
        output_copy(act, k, H1 - 1)

    def output_copy(act, k, h):
        act.wait_ge(s["pv_mm"], k * H1 + h + 1)
        if h >= 2 or at(k, 1):
            act.wait_ge(s["wo_mm"], k * H1 + h - 1)
        nc.scalar.copy(OT[h % 2][:, :], ps[0:DH + 1, O_BANK, 0:SQ]).then_inc(s["ot"], 1)

    def vector_step(dve, st, k):
        first = not peeled(k, B)
        if first:
            dve.wait_ge(s["batch"], 2 * (k + 1))

        def row_min(u):
            dve.wait_ge(s["s_mm"], k * UNITS + u + 1)
            nc.vector.tensor_reduce(mn[:, u % 2:u % 2 + 1], ps[:, 2 * (u % 2):2 * (u % 2) + 2, 0:NK1 // 2], AX.XY,
                                    ALU.min).then_inc(s["row_min"], 1)
        for i in range(NJOB):
            if first and i == NJOB - 1:
                row_min(0)
            elif first and (i or peeled(k, 0)):
                job_dve(dve, k, i)
            if i == 2 and at(k, 1):
                output_add(dve, st, k - 1, H1 - 1)

        for u in range(UNITS):
            if u == 2 and at(k, 1):
                st.wait()
            if first and u + 1 < UNITS:
                row_min(u + 1)
            if u == 2 and at(k, 1):
                for q in range(QT):
                    ins = nc.vector.bn_aggr(mv[:, q, :], stats[:, q, :])
                ins.then_inc(s["ystat"], 1)
            if first:
                dve.wait_ge(s["t_mm"], 2 * (k * UNITS + u) + 1)
                nc.vector.tensor_copy(eT[u // 2 % 2][:, 0:4, (u % 2) * P:(u % 2 + 1) * P],
                                      ps[:, T_BANK, :].rearrange("p (j q) -> p j q", q=P)).then_inc(s["t_dve"], 1)
            if first and u == 1:
                job_dve(dve, k, NJOB - 1)
            if u == 1 and at(k, 1):
                dve.wait_ge(s["y_added"], k * H1)
                for q in range(QT):
                    st.mark(nc.vector.bn_stats(stats[:, q, :], y[:, q, :]))
            if u == 3 and at(k, 1):
                dve.wait_ge(s["yr"], k)
                for q in range(QT):
                    st.mark(nc.vector.tensor_scalar(yn[:, q, :], y[:, q, :], mv[:, q, 0:1], rstd[:, q:q + 1], ALU.subtract, ALU.mult))
                st.wait()
                st.done(nc.vector.tensor_tensor(yn[:, :, :], yn[:, :, :],
                                                gout[:, :].rearrange("p (a d) -> p a d", a=1).to_broadcast([P, QT, D]), ALU.mult))
                st.done(nc.vector.tensor_tensor(yn[:, :, :], yn[:, :, :],
                                                bout[:, :].rearrange("p (a d) -> p a d", a=1).to_broadcast([P, QT, D]), ALU.add))
                x_old = X[:, bass.ds((k - 1) * QT, QT), :]
                nc.vector.tensor_tensor(xs[:, :, :], x_old, yn[:, :, :], ALU.add).then_inc(s["yn"], 1)
            if u == 4 and at(k, 1):
                dve.wait_ge(s["yn"], k)
                x_old = X[:, bass.ds((k - 1) * QT, QT), :]
                nc.vector.tensor_tensor(x_old, x_old, yn[:, :, :], ALU.add).then_inc(s["x_out"], 1)
                for q in range(QT):
                    st.mark(nc.vector.bn_stats(stats[:, 2 + q, :], xs[:, q, :]))
                st.wait()
            if u == 5 and at(k, 1):
                for q in range(QT):
                    ins = nc.vector.bn_aggr(xsmv[:, q, :], stats[:, 2 + q, :])
                ins.then_inc(s["xstat"], 1)
            if u == 8 and at(k, 1):
                dve.wait_ge(s["xr"], k)
                for q in range(QT):
                    ins = nc.vector.tensor_scalar(env["Xn"][:, bass.ds((k - 1) * QT + q, 1), :].rearrange("p a d -> p (a d)"),
                                                  xs[:, q, :], xsmv[:, q, 0:1], xsr[:, q:q + 1], ALU.subtract, ALU.mult)
                ins.then_inc(s["xn"], 1)
            if peeled(k, 0) and u == 0:
                dve.wait_ge(s0["x_scales"], 1)
                for t in range(4 * LAST, NT):
                    stream_normed(env, t).then_inc(s0["xn"], 1)
            if peeled(k, 0) and u >= 5 and u % 2:
                fill(dve, FILLED + (u - 5) // 2)
            if first and u >= 4 and u % 2 == 0:
                output_add(dve, st, k, (u - 4) // 2)
        if first:
            output_add(dve, st, k, H1 - 2)
            if not peeled(k, B - 1):
                job_dve(dve, k + 1, 0)

    def output_add(dve, st, k, h):
        dve.wait_ge(s["wo_mm"], k * H1 + h + 1)
        o = ps[:, Y_BANK, 0:QT * (D + 1)].rearrange("p (q d) -> p q d", q=QT)
        st.done(nc.vector.reciprocal(rz[:, :], o[:, :, D]))
        if h:
            dve.wait_ge(s["y_added"], k * H1 + h)
        for q in range(QT):
            if h == 0:
                ins = nc.vector.tensor_scalar(y[:, q, :], o[:, q, 0:D], rz[:, q:q + 1], None, ALU.mult)
            else:
                ins = nc.vector.scalar_tensor_tensor(y[:, q, :], o[:, q, 0:D], rz[:, q:q + 1], y[:, q, :], ALU.mult, ALU.add)
        ins.then_inc(s["y_added"], 1)

    with nc.Block() as block:
        @block.gpsimd
        def _(pool):
            st = Steps(pool, s["pstep"])

            def batch(b):
                if b:
                    pool.wait_ge(s["job_mm"], b * NJOB)
                    st.done(nc.gpsimd.tensor_copy(LTb[0][:, :], LT[:, b, :]))
                    nc.gpsimd.tensor_tensor(LTb[1][:, :], LT[:, b, :], LTb[0][:, :].bitcast(F32), ALU.subtract).then_inc(s["batch"], 1)
                    pool.wait_ge(s["job_act"], NJOB * b)
                    pool.wait_ge(s["job_dve"], NJOB * b)
                pool.wait_ge(s["batch"], 2 * b + 1)
                nc.gpsimd.tensor_copy(mkb[:, :], mask01[:, b * KT:(b + 1) * KT]).then_inc(s["batch"], 1)
            st.done(nc.gpsimd.memset(V[:, KT:KJ, :, DH:DH + 1], 1.0))
            batch(0)
            for b in range(B + 1):
                if b < B:
                    if b:
                        pool.wait_ge(s["pv_mm"], b * H1)
                    nc.gpsimd.tensor_copy(
                        V[:, 0:KT, :, DH:DH + 1].rearrange("p j h c -> p j (h c)"),
                        mask01[:, b * KT:(b + 1) * KT].rearrange("p (j a) -> p j a", a=1).to_broadcast([P, KT, H1])).then_inc(s["ones"], 1)
                if b:
                    pool.wait_ge(s["ystat"], b)
                    st.done(nc.gpsimd.tensor_scalar(rtmp[:, 0:QT], mv[:, 0:QT, 1], LN_EPS, None, ALU.add))
                    if b >= 2:
                        pool.wait_ge(s["yn"], b - 1)
                    nc.gpsimd.tensor_tensor(rstd[:, 0:QT], rtmp[:, 0:QT], mhalf[:, 0:QT], ALU.pow).then_inc(s["yr"], 1)
                    pool.wait_ge(s["yr"], b)
                    pool.wait_ge(s["xstat"], b)
                    st.done(nc.gpsimd.tensor_scalar(rtmp[:, 2:2 + QT], xsmv[:, :, 1], LN_EPS, None, ALU.add))
                    if b >= 2:
                        pool.wait_ge(s["xn"], b - 1)
                    nc.gpsimd.tensor_tensor(xsr[:, :], rtmp[:, 2:2 + QT], mhalf[:, 0:QT], ALU.pow).then_inc(s["xr"], 1)
                    pool.wait_ge(s["xr"], b)
                else:
                    stream_scales(pool, st, env, 4 * LAST, NT, LN_EPS, s0["x_scales"])
                if b + 1 < B:
                    pool.wait_ge(s0["filled"], b + 2)
                    batch(b + 1)
                if b in (1, 2):
                    w, (high, low) = (env["d"][n] for n in (("w1", "w1p"), ("w3", "w3p"))[b - 1])
                    pool.wait_ge(env["d"]["loaded_w"], 16 * 6)
                    st.done(nc.gpsimd.tensor_copy(high[:, :, :], w[:, :, :]))
                    st.done(nc.gpsimd.tensor_tensor(low[:, :, :], w[:, :, :], high[:, :, :].bitcast(F32), ALU.subtract))

        @block.tensor
        def _(pe):
            pe.wait_ge(c["loaded_w"], 16 * 5)
            tensor_step(pe, 0)
            with pe.Fori(1, B - 1) as k:
                tensor_step(pe, k)
            tensor_step(pe, B - 1)
            project_mm(pe, B - 1, H1 - 1)

        @block.scalar
        def _(act):
            nc.scalar.copy(LTb[0][:, :], LT[:, 0, :]).then_inc(s["first_high"], 1)
            scalar_step(act, 0)
            with act.Fori(1, B - 1) as k:
                scalar_step(act, k)
            scalar_step(act, B - 1)

        @block.vector
        def _(dve):
            dve.wait_ge(s["first_high"], 1)
            nc.vector.tensor_tensor(LTb[1][:, :], LT[:, 0, :], LTb[0][:, :].bitcast(F32), ALU.subtract).then_inc(s["batch"], 1)
            dve.wait_ge(c["loaded_w"], 16 * 5)
            st = Steps(dve, s["dstep"])
            vector_step(dve, st, 0)
            with st.loop(1, B - 1, 1, 8 + H1) as k:
                vector_step(dve, st, k)
            vector_step(dve, st, B - 1)
            vector_step(dve, st, B)


def experts1(env, stack):
    nc, dram, sem, X, ps = env["nc"], env["dram"], env["sem"], env["X"], env["ps"]
    identf, stats, mv, rstd, rtmp, mhalf = (env[n] for n in ("identf", "stats", "mv", "rstd", "rtmp", "mhalf"))

    def sb(name, shape, dt=F32):
        return env["sb"](stack, name, shape, dt)

    NE = E1 + 1
    place = [E1, *range(E1)]
    d, Xn = env["d"], env["Xn"]
    W2, rw, rank, biasB = (d[n] for n in ("w2", "rw", "rank", "biasB"))
    W1, W3 = d["w1p"], d["w3p"]
    XnT = [sb(f"XnTD{i}", [P, NT * P], F32R) for i in range(2)]
    rwp = [sb(f"rwp{i}", [P, E1], F32R) for i in range(2)]
    L, ex, k1, k2, key, G = (sb(n, [P, NT, E1]) for n in ("LD", "exD", "k1D", "k2D", "keyD", "GD"))
    mx, den, kmx = (sb(n, [P, NT]) for n in ("mxD", "denD", "kmxD"))
    silu = [sb(f"siluD{i}", [P, 512]) for i in range(3)]
    hid = [sb(f"hidD{i}", [P, 512]) for i in range(3)]
    s = {n: sem("d_" + n) for n in (
        "steps", "t_mm", "xt", "xt_low", "rw_high", "rw_low", "lt_mm", "lt_out", "l_mm", "l_out", "shifted", "exps",
        "h_mm", "silu", "hid", "y_mm", "y_added")}

    L_BANK = 5

    def y_wait(g, e):
        return g * NE + e - (0 if e == 0 else 2 if e == 1 else 1)

    with nc.Block() as block:
        @block.tensor
        def _(pe):
            for g in range(4):
                for i in range(4):
                    mm = nc.tensor.transpose(ps[:, g, i * P:(i + 1) * P], Xn[:, 4 * g + i, :], identf[:, :])
                mm.then_inc(s["t_mm"], 1)
            router_products(pe, nc, env, s, rwp, XnT, (6, 7), L_BANK, silu[1:3] + hid[1:3])
            pe.wait_ge(d["loaded_w"], 16 * 6)

            def up(g, e):
                n, peeled = g * NE + e, isinstance(g, int) and g == 0
                if not (peeled and e < 3):
                    pe.wait_ge(s["hid"], n - 2)
                elif e == 2:
                    pe.wait_ge(s["l_out"], 1)
                for i, w in enumerate((W1, W3)):
                    product(nc, ps[:, 3 * i + e % 3, :], lambda p: w[p][:, place[e], :],
                            lambda p: XnT[p][:, bass.ds(g * 512, 512)]).then_inc(s["h_mm"], 1)

            def down(g, e):
                pe.wait_ge(s["hid"], g * NE + e + 1)
                if not (isinstance(g, int) and g == 0 and e < 2):
                    pe.wait_ge(s["y_added"], y_wait(g, e))
                for t in range(4):
                    mm = nc.tensor.matmul(ps[:, 6 + e % 2, t * P:(t + 1) * P], hid[e % 3][:, t * P:(t + 1) * P],
                                          W2[:, place[e], :], start=True, stop=True)
                mm.then_inc(s["y_mm"], 1)

            def group(g):
                up(g, 0)
                up(g, 1)
                for e in range(NE):
                    if e + 2 < NE:
                        up(g, e + 2)
                    down(g, e)
            group(0)
            with pe.Fori(1, 4) as g:
                group(g)

        @block.scalar
        def _(act):
            for g in range(4):
                act.wait_ge(s["t_mm"], g + 1)
                nc.scalar.copy(XnT[0][:, g * 512:(g + 1) * 512], ps[:, g, :]).then_inc(s["xt"], 1)
            router_copies(act, nc, env, s, E1, (6, 7), silu[1:3] + hid[1:3])
            act.wait_ge(s["shifted"], 1)
            nc.scalar.activation(ex[:, :, :], ex[:, :, :], ACT.Exp).then_inc(s["exps"], 1)

            def group(g):
                for e in range(NE):
                    n = g * NE + e
                    act.wait_ge(s["h_mm"], 2 * n + 1)
                    if not (isinstance(g, int) and g == 0 and e < 3):
                        act.wait_ge(s["hid"], n - 2)
                    nc.scalar.activation(silu[e % 3][:, :], ps[:, e % 3, :], ACT.Silu).then_inc(s["silu"], 1)
            group(0)
            with act.Fori(1, 4) as g:
                group(g)

        @block.vector
        def _(dve):
            st = Steps(dve, s["steps"])

            def hidden(g, e):
                n = g * NE + e
                dve.wait_ge(s["silu"], n + 1)
                dve.wait_ge(s["h_mm"], 2 * n + 2)
                if not (isinstance(g, int) and g == 0 and e < 3):
                    dve.wait_ge(s["y_mm"], n - 2)
                nc.vector.tensor_tensor(hid[e % 3][:, :], silu[e % 3][:, :], ps[:, 3 + e % 3, :], ALU.mult).then_inc(s["hid"], 1)

            def over_experts(a):
                return a[:, :].rearrange("p (t a) -> p t a", a=1).to_broadcast([P, NT, E1])

            def over_tiles(a):
                return a[:, :].rearrange("p (a e) -> p a e", a=1).to_broadcast([P, NT, E1])

            def first_of_max(dst, src):
                st.done(nc.vector.tensor_reduce(mx[:, :], src[:, :, :], AX.X, ALU.max))
                st.done(nc.vector.tensor_tensor(key[:, :, :], src[:, :, :], over_experts(mx), ALU.is_equal))
                st.done(nc.vector.tensor_tensor(key[:, :, :], key[:, :, :], over_tiles(rank), ALU.mult))
                st.done(nc.vector.tensor_reduce(kmx[:, :], key[:, :, :], AX.X, ALU.max))
                st.done(nc.vector.tensor_tensor(dst[:, :, :], key[:, :, :], over_experts(kmx), ALU.is_equal))

            def add(g, e):
                dve.wait_ge(s["y_mm"], g * NE + e + 1)
                if not (isinstance(g, int) and g == 0 and e == 0):
                    dve.wait_ge(s["y_added"], g * NE + e)
                yb = ps[:, 6 + e % 2, :]
                if e == 0:
                    x = X[:, bass.ds(g * 4, 4), :]
                    i = nc.vector.tensor_tensor(x, x, yb.rearrange("p (t d) -> p t d", t=4), ALU.add)
                else:
                    for t in range(4):
                        x = X[:, bass.ds(g * 4 + t, 1), :].rearrange("p a d -> p (a d)")
                        gate = G[:, bass.ds(g * 4 + t, 1), e - 1:e].rearrange("p a d -> p (a d)")
                        i = nc.vector.scalar_tensor_tensor(x, yb[:, t * P:(t + 1) * P], gate, x, ALU.mult, ALU.add)
                i.then_inc(s["y_added"], 1)

            def group(g):
                peeled = isinstance(g, int) and g == 0
                if not peeled:
                    hidden(g, 0)
                for e in range(NE):
                    if e + 1 < NE and not (peeled and e < 2):
                        hidden(g, e + 1)
                    if not (peeled and e == 0):
                        add(g, e)
            dve.wait_ge(d["loaded_small"], 16 * 3)
            router_weights(dve, nc, s, rw, rwp)
            for g in range(4):
                dve.wait_ge(s["xt"], g + 1)
                nc.vector.tensor_tensor(XnT[1][:, g * 512:(g + 1) * 512], ps[:, g, :],
                                        XnT[0][:, g * 512:(g + 1) * 512].bitcast(F32), ALU.subtract).then_inc(s["xt_low"], 1)
            dve.wait_ge(s["l_mm"], 1)
            nc.vector.tensor_copy(L[:, :, :].rearrange("p t e -> p (t e)"), ps[:, L_BANK, 0:NT * E1]).then_inc(s["l_out"], 1)
            dve.wait_ge(s["l_out"], 1)
            st.done(nc.vector.tensor_reduce(mx[:, :], L[:, :, :], AX.X, ALU.max))
            nc.vector.tensor_tensor(ex[:, :, :], L[:, :, :], over_experts(mx), ALU.subtract).then_inc(s["shifted"], 1)
            hidden(0, 0)
            dve.wait_ge(d["loaded_small"], 16 * 3)
            dve.wait_ge(s["exps"], 1)
            st.done(nc.vector.tensor_reduce(den[:, :], ex[:, :, :], AX.X, ALU.add))
            st.done(nc.vector.reciprocal(den[:, :], den[:, :]))
            st.done(nc.vector.tensor_tensor(ex[:, :, :], ex[:, :, :], over_experts(den), ALU.mult))
            hidden(0, 1)
            st.done(nc.vector.tensor_tensor(L[:, :, :], ex[:, :, :], over_tiles(biasB), ALU.add))
            add(0, 0)
            hidden(0, 2)
            first_of_max(k1, L)
            st.done(nc.vector.scalar_tensor_tensor(L[:, :, :], k1[:, :, :], -3e38, L[:, :, :], ALU.mult, ALU.add))
            first_of_max(k2, L)
            st.done(nc.vector.tensor_tensor(k1[:, :, :], k1[:, :, :], k2[:, :, :], ALU.add))
            st.done(nc.vector.tensor_tensor(G[:, :, :], k1[:, :, :], ex[:, :, :], ALU.mult))
            group(0)
            with dve.Fori(1, 4) as g:
                group(g)


def kernel(**inputs):
    import concourse.bacc as bacc
    from concourse.bass_utils import run_bass_kernel_spmd as run

    v = {k: np.asarray(a) for k, a in inputs.items()}
    perm = np.arange(D).reshape(PAIRS, 2, DK).transpose(1, 2, 0).reshape(-1)
    w = lambda a: np.ascontiguousarray(a)
    sel = np.zeros((2, DK, PAIRS, 2, PAIRS), np.float32)
    for half in range(2):
        for pair in range(PAIRS):
            sel[half, :, pair, half, pair] = 1
    arrays = {
        "x": w(v["x"].reshape(B * SQ, D)),
        "ctx": w(v["ctx_1024"].reshape(B * SK, D)),
        "ctxT": w(v["ctx_1024"].transpose(2, 0, 1)),
        "mask": w(v["mask_BxS2_bk1"]).view(np.int32).reshape(1, B * SK // 4),
        "ident": np.eye(P, dtype=np.float32),
        "sel": sel.reshape(P, H0),
        "wq0T": w(v["L0_xattn_Wq"][perm].T), "bq0": w(v["L0_xattn_bq"][perm].reshape(D, 1)),
        "wk0T": w(v["L0_xattn_Wk"][perm].T), "bk0": w(v["L0_xattn_bk"][perm].reshape(D, 1)),
        "wv0T": w(v["L0_xattn_Wv"].T), "bv0": w(v["L0_xattn_bv"].reshape(1, D)),
        "wo0T": w(v["L0_xattn_Wo"].T), "bo0": w(v["L0_xattn_bo"].reshape(1, D)),
        "tw1T": w(v["L0_xattn_w1"].T), "tb1": w(v["L0_xattn_b1"].reshape(64, 1)),
        "tw2T": w(v["L0_xattn_w2"].T), "tb2": w(v["L0_xattn_b2"].reshape(64, 1)),
        "rms_w": w(v["L0_ffn_rms_w"].reshape(D, 1)), "gate_wT": w(v["L0_ffn_gate_w"].T),
        "rank": np.tile(np.arange(E0, 0, -1, dtype=np.float32), (P, 1)),
        "eb1": w(v["L0_ffn_b1"].reshape(E0 * FC, P).T), "eb2": w(v["L0_ffn_b2"]),
        "eW1": w(v["L0_ffn_W1"]), "eW2": w(v["L0_ffn_W2"]),
        "maskc": w(v["mask_BxS2_bk1"].reshape(B * KT, P).T).view(np.int32),
        "wq1": w(v["L1_xattn_Wq"]), "wkv1": w(v["L1_xattn_Wkv"]), "wo1": w(v["L1_xattn_Wo"]),
        "lnx_g": w(v["L1_xattn_ln_x_g"].reshape(D, 1)), "lnx_b": w(v["L1_xattn_ln_x_b"].reshape(D, 1)),
        "lnl_g": w(v["L1_xattn_ln_l_g"].reshape(D, 1)), "lnl_b": w(v["L1_xattn_ln_l_b"].reshape(D, 1)),
        "lno_g": w(v["L1_xattn_ln_o_g"].reshape(1, D)), "lno_b": w(v["L1_xattn_ln_o_b"].reshape(1, D)),
        "router_w": w(v["L1_ffn_router_w"]), "expert_bias": w(v["L1_ffn_expert_bias"].reshape(1, E1)),
        "w1": w(v["L1_ffn_w1"]), "w2": w(v["L1_ffn_w2"]), "w3": w(v["L1_ffn_w3"]),
        "sw1": w(v["L1_ffn_sw1"]), "sw2": w(v["L1_ffn_sw2"]), "sw3": w(v["L1_ffn_sw3"]),
        "tw3": w(np.broadcast_to(v["L0_xattn_w3"].reshape(64, 1), (64, P))), "tb3": w(v["L0_xattn_b3"].reshape(1, 1)),
    }
    nc = bacc.Bacc("TRN2", target_bir_lowering=False, num_devices=1)
    dram = {n: nc.dram_tensor("in_" + n, a.shape, mybir.dt.from_np(a.dtype), kind="ExternalInput").ap()
            for n, a in arrays.items()}
    out = nc.dram_tensor("out", [B * SQ, D], F32, kind="ExternalOutput").ap()
    build(nc, dram, out)
    r = run(nc, [{"in_" + n: a for n, a in arrays.items()}], core_ids=[0])
    return r.results[0]["out"].reshape(B, SQ, D)
```
